# Optimizing a Trainium2 kernel written in Bass

```python
import numpy as np
import jax
import jax.numpy as jnp

def _softmax(x, axis=-1):
    return jax.nn.softmax(x, axis=axis)

def _gelu(x):
    return jax.nn.gelu(x, approximate=True)

def _silu(x):
    return jax.nn.silu(x)

def _sigmoid(x):
    return jax.nn.sigmoid(x)

def _layernorm(x, axis=-1, eps=1e-05):
    m = jnp.mean(x, axis=axis, keepdims=True)
    v = jnp.var(x, axis=axis, keepdims=True)
    return (x - m) / jnp.sqrt(v + eps)

def _scatter_add(tgt, idx, src, axis=0):
    return tgt.at[idx].add(src)

def _segment_sum(src, seg, n):
    return jax.ops.segment_sum(src, seg, n)
kernel_name = 'mk_early_fusion_d1_tok_img1024_r4_28f49a'

def setup_inputs(seed: int=0):
    np.random.seed(seed)
    _w = jnp.asarray

    def _rec_inputs():
        import jax
        import jax.numpy as jnp
        _rk = jax.random.key(seed)
        x = -7.10856e-05 + 0.999911 * jax.random.normal(jax.random.fold_in(_rk, 1), (8, 1024, 256, 4), jnp.float32)
        txt = 0.000285084 + 0.500834 * jax.random.normal(jax.random.fold_in(_rk, 2), (8, 32, 256), jnp.float32)
        return (x, txt)
    x, txt = _rec_inputs()

    def _L0_tok_setup():
        import jax, jax.numpy as jnp
        import numpy as np
        B, T, D, DV = (4, 1024, 256, 4)
        K = 4
        C = D * DV
        key = jax.random.key(seed)
        k1, k2, k3 = jax.random.split(key, 3)
        x = jax.random.normal(k1, (B, T, D, DV), dtype=jnp.float32)
        conv_w = jax.random.normal(k2, (C, K), dtype=jnp.float32) * (1.0 / np.sqrt(K))
        conv_b = jax.random.normal(k3, (C,), dtype=jnp.float32) * 0.02
        read = jnp.full((DV,), 1.0 / DV, dtype=jnp.float32)
        return {'x': x, 'conv_w': conv_w, 'conv_b': conv_b, 'read': read}
    _L0_tok_all = _L0_tok_setup()
    _L0_tok_in = {k: v for k, v in _L0_tok_all.items() if k in ('conv_w', 'conv_b', 'read')}
    del _L0_tok_all

    def _L0_attn_setup():
        import jax, jax.numpy as jnp
        import numpy as np
        FEATS = 256
        HEAD = 16
        HEAD_DIM = FEATS // HEAD
        EPS = 1e-12

        def _l2norm(t):
            n = jnp.sqrt(jnp.sum(t * t, axis=-1, keepdims=True))
            return t / jnp.maximum(n, EPS)
        key = jax.random.key(seed)
        ks = jax.random.split(key, 10)
        s = 0.02
        inp = {'x': jax.random.normal(ks[0], (4, 512, FEATS), dtype=jnp.float32), 'Wq': jax.random.normal(ks[1], (FEATS, FEATS), dtype=jnp.float32) * s, 'bq': jnp.zeros((FEATS,), dtype=jnp.float32), 'Wk': jax.random.normal(ks[2], (FEATS, FEATS), dtype=jnp.float32) * s, 'bk': jnp.zeros((FEATS,), dtype=jnp.float32), 'Wv': jax.random.normal(ks[3], (FEATS, FEATS), dtype=jnp.float32) * s, 'bv': jnp.zeros((FEATS,), dtype=jnp.float32), 'Wo': jax.random.normal(ks[4], (FEATS, FEATS), dtype=jnp.float32) * s, 'bo': jnp.zeros((FEATS,), dtype=jnp.float32), 'm': jnp.full((HEAD,), 0.5, dtype=jnp.float32)}
        return inp
    _L0_attn_all = _L0_attn_setup()
    _L0_attn_in = {k: v for k, v in _L0_attn_all.items() if k in ('Wq', 'bq', 'Wk', 'bk', 'Wv', 'bv', 'Wo', 'bo', 'm')}
    del _L0_attn_all

    def _L0_ffn_setup():
        import jax, jax.numpy as jnp
        import numpy as np
        E = 8
        K = 2
        CAP_RATIO = 1.05
        key = jax.random.key(seed)
        ks = jax.random.split(key, 4)
        B, S, D, H = (2, 512, 256, 1024)
        x = jax.random.normal(ks[0], (B, S, D), jnp.float32)
        Wg = jax.random.normal(ks[1], (E, D), jnp.float32) * 0.02
        W1 = jax.random.normal(ks[2], (E, D, H), jnp.float32) * 0.02
        b1 = jnp.zeros((E, H), jnp.float32)
        W2 = jax.random.normal(ks[3], (E, H, D), jnp.float32) * 0.02
        b2 = jnp.zeros((E, D), jnp.float32)
        return {'x': x, 'Wg': Wg, 'W1': W1, 'b1': b1, 'W2': W2, 'b2': b2}
    _L0_ffn_all = _L0_ffn_setup()
    _L0_ffn_in = {k: v for k, v in _L0_ffn_all.items() if k in ('Wg', 'W1', 'b1', 'W2', 'b2')}
    del _L0_ffn_all
    return {'x': x, 'txt': txt, 'L0_tok_conv_w': _L0_tok_in['conv_w'], 'L0_tok_conv_b': _L0_tok_in['conv_b'], 'L0_tok_read': _L0_tok_in['read'], 'L0_attn_Wq': _L0_attn_in['Wq'], 'L0_attn_bq': _L0_attn_in['bq'], 'L0_attn_Wk': _L0_attn_in['Wk'], 'L0_attn_bk': _L0_attn_in['bk'], 'L0_attn_Wv': _L0_attn_in['Wv'], 'L0_attn_bv': _L0_attn_in['bv'], 'L0_attn_Wo': _L0_attn_in['Wo'], 'L0_attn_bo': _L0_attn_in['bo'], 'L0_attn_m': _L0_attn_in['m'], 'L0_ffn_Wg': _L0_ffn_in['Wg'], 'L0_ffn_W1': _L0_ffn_in['W1'], 'L0_ffn_b1': _L0_ffn_in['b1'], 'L0_ffn_W2': _L0_ffn_in['W2'], 'L0_ffn_b2': _L0_ffn_in['b2']}

def reference(x, txt, L0_tok_conv_w, L0_tok_conv_b, L0_tok_read, L0_attn_Wq, L0_attn_bq, L0_attn_Wk, L0_attn_bk, L0_attn_Wv, L0_attn_bv, L0_attn_Wo, L0_attn_bo, L0_attn_m, L0_ffn_Wg, L0_ffn_W1, L0_ffn_b1, L0_ffn_W2, L0_ffn_b2):
    import jax
    import jax.numpy as jnp

    def _L0_tok_ref(x, conv_w, conv_b, read):
        import jax, jax.numpy as jnp
        import numpy as np
        B, T, D, DV = (4, 1024, 256, 4)
        K = 4
        C = D * DV
        Bb, Tt, d, dv = x.shape
        c = d * dv
        x_flat = x.reshape(Bb, Tt, c)
        k = conv_w.shape[1]
        x_pad = jnp.pad(x_flat, ((0, 0), (k - 1, 0), (0, 0)))
        acc = conv_b
        for j in range(k):
            acc = acc + x_pad[:, j:j + Tt, :] * conv_w[:, j]
        x_conv = acc.reshape(Bb, Tt, d, dv)
        return jnp.einsum('btdv,v->btd', x_conv, read)

    def _L0_attn_ref(x, Wq, bq, Wk, bk, Wv, bv, Wo, bo, m):
        import jax, jax.numpy as jnp
        import numpy as np
        FEATS = 256
        HEAD = 16
        HEAD_DIM = FEATS // HEAD
        EPS = 1e-12

        def _l2norm(t):
            n = jnp.sqrt(jnp.sum(t * t, axis=-1, keepdims=True))
            return t / jnp.maximum(n, EPS)
        b, n, f = x.shape

        def proj(W, bias):
            y = x @ W + bias
            return y.reshape(b, n, HEAD, HEAD_DIM).transpose(0, 2, 1, 3)
        q = _l2norm(proj(Wq, bq))
        k = _l2norm(proj(Wk, bk))
        v = proj(Wv, bv)
        sim = jnp.einsum('bhid,bhjd->bhij', q, k)
        sigma_m = jax.nn.sigmoid(m).reshape(1, HEAD, 1, 1)
        scaling = jnp.asarray(n, dtype=x.dtype) ** sigma_m
        attn = sim / scaling
        out = jnp.einsum('bhij,bhjd->bhid', attn, v)
        out = out.transpose(0, 2, 1, 3).reshape(b, n, f)
        return out @ Wo + bo

    def _L0_ffn_ref(x, Wg, W1, b1, W2, b2):
        import jax, jax.numpy as jnp
        import numpy as np
        E = 8
        K = 2
        CAP_RATIO = 1.05
        B, S, D = x.shape
        T = B * S
        xf = x.reshape(T, D)
        gates = jax.nn.softmax(xf @ Wg.T, axis=-1)
        topw, topi = jax.lax.top_k(gates, K)
        C = int(round(K * T * CAP_RATIO / E))
        e_ord = topi.T.reshape(-1)
        tok_ord = jnp.tile(jnp.arange(T), K)
        oh = jax.nn.one_hot(e_ord, E, dtype=jnp.int32)
        cnt = jnp.take_along_axis(jnp.cumsum(oh, 0) - oh, e_ord[:, None], 1)[:, 0]
        within = cnt < C
        pos = jnp.where(within, cnt, C)
        x_disp = xf[tok_ord]
        buf = jnp.zeros((E, C + 1, D), xf.dtype).at[e_ord, pos].add(x_disp)[:, :C]
        h = jax.nn.gelu(jnp.einsum('ecd,edh->ech', buf, W1) + b1[:, None, :], approximate=False)
        y = jnp.einsum('ech,ehd->ecd', h, W2) + b2[:, None, :]
        y_ord = y[e_ord, jnp.minimum(pos, C - 1)] * within[:, None].astype(y.dtype)
        y_tk = y_ord.reshape(K, T, D).transpose(1, 0, 2)
        cw = topw * within.reshape(K, T).T.astype(topw.dtype)
        out = jnp.einsum('tk,tkd->td', cw, y_tk)
        return out.reshape(B, S, D)
    h = _L0_tok_ref(x, L0_tok_conv_w, L0_tok_conv_b, L0_tok_read)
    h = jnp.concatenate([h, txt], axis=1)
    h = h + _L0_attn_ref(_layernorm(h, axis=-1), L0_attn_Wq, L0_attn_bq, L0_attn_Wk, L0_attn_bk, L0_attn_Wv, L0_attn_bv, L0_attn_Wo, L0_attn_bo, L0_attn_m)
    h = h + _L0_ffn_ref(_layernorm(h, axis=-1), L0_ffn_Wg, L0_ffn_W1, L0_ffn_b1, L0_ffn_W2, L0_ffn_b2)
    return h

_drawn_inputs = setup_inputs


def setup_inputs(seed=0):
    import zlib

    import numpy as np

    out = dict(_drawn_inputs(seed))
    spreads = {'L0_tok_read': (0.25, 0.2),
     'L0_attn_bq': (0.0, 0.333),
     'L0_attn_bk': (0.0, 0.1),
     'L0_attn_bv': (0.0, 0.1),
     'L0_attn_bo': (0.0, 0.1),
     'L0_attn_m': (0.5, 0.6),
     'L0_ffn_b1': (0.0, 0.449),
     'L0_ffn_b2': (0.0, 0.1)}
    factors = {}
    for name, (base, spread) in spreads.items():
        noise = np.random.default_rng([zlib.crc32(name.encode()), seed]).standard_normal(out[name].shape)
        drawn = base * np.exp(spread * noise) if base else spread * noise
        out[name] = jnp.asarray(drawn.astype(out[name].dtype))
    for name, factor in factors.items():
        out[name] = (out[name] * factor).astype(out[name].dtype)
    return out
```

```python
from contextlib import ExitStack

import concourse.bass as bass
from concourse import mybir

F32 = mybir.dt.float32
F32R = mybir.dt.float32r
BF16 = mybir.dt.bfloat16
I32 = mybir.dt.int32
U32 = mybir.dt.uint32
ALU = mybir.AluOpType
ACT = mybir.ActivationFunctionType
X = mybir.AxisListType.X

P = 128
B, TI, D, DV = 8, 1024, 256, 4
TX = 32
S = TI + TX
TOK = B * S
CH = D * DV
KC = 4
CBS = CH // P
FB = D // P
HEADS, HD = 16, 16
E, H = 8, 1024
CAP = int(round(2 * TOK * 1.05 / E))
NT = TI // P
CT = 4
CW = CT * P
UNITS = NT // 2 + 1

SR = 111
ST = 20
SL = SR * ST
CC = 4
NCH = ST // CC
N2 = CC * SR
MB = H // P
W_AT = ((0, FB, H), (FB * H, MB, D))
FAR = 1 << 20
LN_EPS = 1e-5


def in_register(eng, register, value):
    if isinstance(value, int):
        return value
    eng.reg_mov(register, value)
    return register


def stage_one(nc, ctx, dram, keep):
    x, txt, conv_w, conv_b, read, Wq, bq, Wk, bk, Wv, bv, Wo, bo, m, Wg, out = (
        dram[n] for n in ("x", "txt", "conv_w", "conv_b", "read", "Wq", "bq", "Wk", "bk", "Wv", "bv",
                          "Wo", "bo", "m", "Wg", "out"))
    rows, tab_first, tab_second = dram["rows"], dram["tab_first"], dram["tab_second"]
    ident, taken, x_in = keep["ident"], keep["taken"], keep["x_in"]
    W1, W2 = dram["W1"], dram["W2"]

    def sb(name, shape, dt=F32):
        return ctx.enter_context(nc.sbuf_tensor(name, shape, dt))

    def sem(name):
        return ctx.enter_context(nc.semaphore(name))

    ones_bf = sb("ones_bf", [P, P], BF16)
    before_bf = sb("before_bf", [P, P], BF16)
    head_of = sb("head_of", [HEADS, D])
    value_of = sb("value_of", [DV, P])
    feat_of = sb("feat_of", [P, 32])
    block_mask = sb("block_mask", [P, P])
    rank = sb("rank", [P, NT + 1, E])
    valid = sb("valid", [P, 2 * E * (NT + 1)])
    no_reset = sb("no_reset", [P, 2 * E, NT + 2])
    bad_row = sb("bad_row", [P, 2, NT + 1])
    token_id = sb("token_id", [P, NT + 1])
    empty_slots = sb("empty_slots", [P, E * ST, 2])
    wqk = sb("wqk", [P, FB, 2 * D])
    wv = sb("wv", [P, FB, D])
    wo = sb("wo", [P, FB, D])
    bqk_rows = sb("bqk_rows", [P, 2 * D])
    bo_rows = sb("bo_rows", [P, D])
    bv_rows = sb("bv_rows", [P, D])
    wg_in = sb("wg_in", [E, D])
    wgT = sb("wgT", [P, FB, 32])
    conv_in = sb("conv_in", [P, CBS, KC])
    conv_b_in = sb("conv_b_in", [CBS, P])
    read_in = sb("read_in", [DV, 1])
    m_in = sb("m_in", [HEADS, 1])
    read_col = sb("read_col", [P, 1])
    conv_col = sb("conv_col", [P, CBS, KC])
    conv_mat = sb("conv_mat", [P, CBS, KC, 32])
    conv_b_col = sb("conv_b_col", [P, CBS])
    h_bias = sb("h_bias", [P, FB])
    m_col = sb("m_col", [P, FB])
    head_scale = sb("head_scale", [P, FB])
    xT = [sb(f"xT{c}", [P, CBS, KC - 1 + CW]) for c in range(2)]
    hT = [sb(f"hT{c}", [P, FB, CW]) for c in range(2)]
    h = sb("h", [P, NT + 1, D])
    h_out = sb("h_out", [P, NT + 1, D])
    xln = sb("xln", [P, NT + 1, D])
    xlnT = sb("xlnT", [P, FB, (NT + 1) * P])
    qk = sb("qk", [P, 3, 2 * D])
    qk_sq = sb("qk_sq", [P, 2, 2 * D])
    qk_ss = sb("qk_ss", [P, 3, 2 * HEADS])
    qk_len = sb("qk_len", [P, 3, 2 * HEADS])
    qk_inv = sb("qk_inv", [P, 3, 2 * HEADS])
    q_n = sb("q_n", [P, NT + 1, D])
    k_n = sb("k_n", [P, NT + 1, D])
    k_sum = sb("k_sum", [P, D])
    qT = sb("qT", [P, FB, (NT + 1) * P])
    A = sb("A", [P, FB, D])
    kvT = sb("kvT", [P, FB, P])
    M = sb("M", [P, FB, D])
    xf = sb("xf", [P, NT + 1, D])
    xfT = sb("xfT", [P, FB, (NT + 1) * P])
    eps = sb("eps", [P, 1])
    stats = sb("stats", [P, 2, NT + 1, 6])
    mean_var = sb("mean_var", [P, 2, NT + 1, 2])
    std = sb("std", [P, 2, NT + 1])
    rstd = sb("rstd", [P, 2, NT + 1])
    lT = sb("lT", [P, 2 * P + TX])
    lg = sb("lg", [P, NT + 1, E])
    top = sb("top", [P, NT + 1])
    ex = sb("ex", [P, NT + 1, E])
    den = sb("den", [P, NT + 1])
    gate = sb("gate", [P, NT + 1, E])
    best = sb("best", [P, 2, NT + 1])
    same = sb("same", [P, NT + 1, E])
    chosen_rank = sb("chosen_rank", [P, 2, NT + 1])
    hot = sb("hot", [P, 2, E, NT + 1])
    hot_bf = sb("hot_bf", [P, 2 * E * (NT + 1)], BF16)
    runs = sb("runs", [P, 2 * E, NT + 2])
    ahead = sb("ahead", [P, 2 * E, NT + 2])
    place = sb("place", [P, 2 * E, NT + 1])
    count = sb("count", [P, 2, NT + 1])
    slot = sb("slot", [P, 2, NT + 1])
    slot_i = sb("slot_i", [P, 2, NT + 1], I32)
    entry = sb("entry", [P, 2, NT + 1, 2])

    ps = [ctx.enter_context(nc.psum_tensor(f"ps{i}", [P, 512], F32)) for i in range(8)]
    ps_x = ps[0:2]
    ps_t = [ps[2], ps[5]]
    ps_c = ps[3]
    ps_a = ps[4]
    ps_w = ps[6:8]

    const_ready = sem("const_ready")
    const_step = sem("const_step")
    params_in = sem("params_in")
    setup_mm = sem("setup_mm")
    setup_v = sem("setup_v")
    setup_a = sem("setup_a")
    x_loaded = [sem(f"x_loaded{c}") for c in range(2)]
    txt_loaded = sem("txt_loaded")
    x_turned = sem("x_turned")
    xT_act = sem("xT_act")
    xT_dve = sem("xT_dve")
    halo_ready = sem("halo_ready")
    conv_done = sem("conv_done")
    hT_ready = sem("hT_ready")
    h_turned = sem("h_turned")
    h_ready = sem("h_ready")
    xln_ready = sem("xln_ready")
    xln_turned = sem("xln_turned")
    xlnT_ready = sem("xlnT_ready")
    qk_done = sem("qk_done")
    qk_taken = sem("qk_taken")
    qk_squared = sem("qk_squared")
    qk_summed = sem("qk_summed")
    qk_rooted = sem("qk_rooted")
    h_measured = sem("h_measured")
    h_std = sem("h_std")
    out_measured = sem("out_measured")
    out_std = sem("out_std")
    qk_normed = sem("qk_normed")
    k_summed = sem("k_summed")
    q_turned = sem("q_turned")
    qT_ready = sem("qT_ready")
    A_done = sem("A_done")
    A_ready = sem("A_ready")
    kv_done = sem("kv_done")
    kv_ready = sem("kv_ready")
    M_done = sem("M_done")
    M_ready = sem("M_ready")
    base_ready = sem("base_ready")
    out_done = sem("out_done")
    out_taken = sem("out_taken")
    xf_ready = sem("xf_ready")
    xf_turned = sem("xf_turned")
    xfT_ready = sem("xfT_ready")
    gates_done = sem("gates_done")
    gates_copied = sem("gates_copied")
    logits_done = sem("logits_done")
    logits_taken = sem("logits_taken")
    shifted = sem("shifted")
    exp_done = sem("exp_done")
    hot_ready = sem("hot_ready")
    counts_done = sem("counts_done")
    counts_taken = sem("counts_taken")
    slots_ready = sem("slots_ready")
    scattered = sem("scattered")
    out_stored = sem("out_stored")
    xf_stored = sem("xf_stored")
    v_step = sem("v_step")
    N_PARAM = 13

    def t_bank(dst, u):
        if dst is xfT:
            return ps_t[(u + 1) % 2]
        if dst is qT:
            return ps_t[{0: 0, 1: 1, 2: 1, 3: 0, 4: 1}[u]]
        return ps_t[u % 2]

    def qk_bank(t):
        return t % 2 if t < CT else (t + 1) % 2

    block = ctx.enter_context(nc.Block())

    def loop(eng, body):
        body(0, True, False, 0)
        with eng.Fori(0, B - 1) as i:
            body(i + 1, True, True, i)
        body(B, False, True, B - 1)

    @block.sync
    def _(sp):
        normed_value, copied_value = sp.alloc_register("normed_value"), sp.alloc_register("copied_value")
        for dst, src in (
            (wqk[:, :, 0:D], Wq.rearrange("(b p) n -> p b n", p=P)),
            (wqk[:, :, D:2 * D], Wk.rearrange("(b p) n -> p b n", p=P)),
            (wv[:], Wv.rearrange("(b p) n -> p b n", p=P)),
            (wo[:], Wo.rearrange("(b p) n -> p b n", p=P)),
            (bqk_rows[:, 0:D], bq.rearrange("(a n) -> a n", a=1).to_broadcast([P, D])),
            (bqk_rows[:, D:2 * D], bk.rearrange("(a n) -> a n", a=1).to_broadcast([P, D])),
            (bo_rows[:], bo.rearrange("(a n) -> a n", a=1).to_broadcast([P, D])),
            (bv_rows[:], bv.rearrange("(a n) -> a n", a=1).to_broadcast([P, D])),
            (wg_in[:], Wg),
            (conv_in[:], conv_w.rearrange("(b p) k -> p b k", p=P)),
            (conv_b_in[:], conv_b.rearrange("(b p) -> b p", p=P)),
            (read_in[:], read.rearrange("(v a) -> v a", a=1)),
            (m_in[:], m.rearrange("(v a) -> v a", a=1)),
        ):
            sp.dma_start(dst, src).then_inc(params_in, 16)
        sp.wait_ge(params_in, 16 * N_PARAM)

        def load_x(b, c, waits):
            if waits:
                sp.wait_ge(x_turned, 16 * (b - 1) + 8 * (c + 1))
            sp.dma_start(x_in[:, CT * c:CT * (c + 1), :],
                         x4[bass.ds(b * 2 + c, 1), :, :, :].rearrange("a p i n -> p (a i) n")
                         ).then_inc(x_loaded[c], 16)

        def load_txt(b, waits):
            if waits:
                normed = in_register(sp, normed_value, UNITS * b)
                copied = in_register(sp, copied_value, 3 * b)
                sp.wait_ge(params_in, 16 * N_PARAM)
                sp.wait_ge(xln_ready, normed)
                sp.wait_ge(base_ready, copied)
            sp.dma_start(h[0:TX, NT, :], txt[bass.ds(b, 1), :, :].rearrange("a t n -> (a t) n")
                         ).then_inc(txt_loaded, 16)

        x4 = x.rearrange("b (c i p) d v -> (b c) p i (d v)", c=2, i=CT, p=P)
        o2 = out.rearrange("b s n -> (b s) n")

        def store(b, dst, src, ready, stored):
            for c in range(2):
                sp.wait_ge(ready, UNITS * b + 2 * (c + 1))
                sp.dma_start(dst[bass.ds(b * S + c * CW, CW), :].rearrange("(i p) n -> p i n", p=P),
                             src[:, CT * c:CT * (c + 1), :]).then_inc(stored, 16)
            sp.wait_ge(ready, UNITS * b + UNITS)
            sp.dma_start(dst[bass.ds(b * S + TI, TX), :], src[0:TX, NT, :]).then_inc(stored, 16)

        for c in range(2):
            load_x(0, c, False)
        load_txt(0, False)
        for c in range(2):
            load_x(1, c, True)
        load_txt(1, True)
        with sp.Fori(0, B - 2) as i:
            for c in range(2):
                load_x(i + 2, c, True)
            store(i, o2, h_out, xf_ready, out_stored)
            store(i, rows, xf, xf_ready, xf_stored)
            load_txt(i + 2, True)
        for b in (B - 2, B - 1):
            store(b, o2, h_out, xf_ready, out_stored)
            store(b, rows, xf, xf_ready, xf_stored)
            if b == B - 2:
                sp.wait_ge(x_turned, 16 * B)
                for (at, n, w), src in zip(W_AT, (W1, W2)):
                    sp.dma_start(x_in[:].rearrange("p i n -> p (i n)")[:, at:at + n * w].rearrange("p (b n) -> p b n", b=n),
                                 src[0:1, :, :].rearrange("a (b p) n -> p (a b) n", p=P)
                                 ).then_inc(keep["w1_loaded" if src is W1 else "w2_loaded"], 16)
        sp.wait_ge(out_stored, 16 * 3 * B)
        sp.wait_ge(xf_stored, 16 * 3 * B + 16)

    @block.gpsimd
    def _(pool):
        pool_value = pool.alloc_register("pool_value")
        n = [0]

        def step(ins):
            n[0] += 1
            ins.then_inc(const_step, 1)
            pool.wait_ge(const_step, n[0])

        def keep_where(t, pattern, base, mult, op, fill=0.0):
            step(pool.affine_select(out=t, in_=t, compare_op=op, fill=fill, base=base, pattern=pattern,
                                    channel_multiplier=mult))

        for t, v in ((ident, 0.0), (ones_bf, 1.0), (before_bf, 1.0), (head_of, 1.0), (value_of, 1.0),
                     (feat_of, 1.0), (valid, 1.0), (no_reset, 1.0), (bad_row, 0.0), (empty_slots, 0.0),
                     (lg, 0.0), (hot, 0.0), (runs, 0.0), (xT[0], 0.0), (taken, 0.0), (k_sum, 0.0),
                     (eps, LN_EPS), (mean_var, 1.0)):
            step(pool.memset(t[:], v))
        keep_where(ident[:], [[-1, P]], 0, 1, ALU.not_equal, 1.0)
        keep_where(before_bf[:], [[1, P]], -1, -1, ALU.is_ge)
        keep_where(head_of[:], [[1, D]], 0, -HD, ALU.is_ge)
        keep_where(head_of[:], [[-1, D]], HD - 1, HD, ALU.is_ge)
        v3 = value_of[:].rearrange("v (a b) -> v a b", b=DV)
        keep_where(v3, [[0, P // DV], [-1, DV]], 0, 1, ALU.is_equal)
        keep_where(feat_of[:], [[-DV, 32]], 0, 1, ALU.is_ge)
        keep_where(feat_of[:], [[DV, 32]], DV - 1, -1, ALU.is_ge)
        step(pool.memset(valid[:].rearrange("p (k i) -> p k i", i=NT + 1)[TX:2 * TX, :, NT], 0.0))
        step(pool.memset(valid[:].rearrange("p (k i) -> p k i", i=NT + 1)[2 * TX:P, :, NT], 0.0))
        step(pool.memset(no_reset[:, :, 0:1], 0.0))
        step(pool.memset(bad_row[:, 1, :], float(CAP - 1)))
        step(pool.memset(bad_row[TX:2 * TX, :, NT:NT + 1], float(FAR)))
        step(pool.memset(bad_row[2 * TX:P, :, NT:NT + 1], float(FAR)))
        step(pool.memset(empty_slots[:, :, 0:1], float(FAR)))
        for e in range(E):
            step(pool.memset(rank[:, :, e:e + 1], float(E - e)))
        pool.memset(xf[:], 0.0).then_inc(xf_stored, 16)
        pool.iota(token_id[:], [[P, NT + 1]], base=0, channel_multiplier=1,
                  allow_small_or_imprecise_dtypes=True).then_inc(const_ready, 1)
        for tab in (tab_first, tab_second):
            pool.dma_start(tab.rearrange("(p s) w -> p (s w)", p=SR),
                           empty_slots[0:SR, :, :].rearrange("p s w -> p (s w)")).then_inc(scattered, 16)

        def residual(b, waits):
            pool.wait_ge(h_ready, 4 * b + 4)
            pool.wait_ge(txt_loaded, 16 * b + 16)
            if waits:
                pool.wait_ge(xf_ready, UNITS * b)
                pool.wait_ge(out_stored, 16 * 3 * b)
            for t0, t1 in ((0, CT), (CT, NT)):
                bc = bo_rows[:].rearrange("p (a n) -> p a n", a=1).to_broadcast([P, t1 - t0, D])
                pool.tensor_tensor(h_out[:, t0:t1, :], h[:, t0:t1, :], bc, ALU.add).then_inc(base_ready, 1)
            pool.tensor_tensor(h_out[0:TX, NT, :], h[0:TX, NT, :], bo_rows[0:TX, :], ALU.add
                               ).then_inc(base_ready, 1)

        def scatter(b):
            ready = in_register(pool, pool_value, b + 1)
            pool.wait_ge(const_ready, 1)
            pool.wait_ge(slots_ready, ready)
            for t in range(NT + 1):
                for k, tab in enumerate((tab_first, tab_second)):
                    pool.indirect_dma_start(
                        tab, bass.IndirectOffsetOnAxis(slot_i[:, k, t:t + 1].bitcast(U32), 0),
                        entry[:, k, t, :], None, bounds_check=E * SL - 1, oob_is_err=False,
                    ).then_inc(scattered, 16)

        def sum_k(b, tiles):
            for i in tiles:
                r = P if i < NT else TX
                normed = (NT + 1) * b + i + 1
                if i == 0:
                    normed = in_register(pool, pool_value, normed)
                    pool.wait_ge(const_ready, 1)
                pool.wait_ge(qk_normed, normed)
                if i == 0:
                    pool.tensor_copy(k_sum[:], k_n[:, 0, :]).then_inc(k_summed, 1)
                else:
                    pool.wait_ge(k_summed, (NT + 1) * b + i)
                    pool.tensor_tensor(k_sum[0:r, :], k_sum[0:r, :], k_n[0:r, i, :], ALU.add
                                       ).then_inc(k_summed, 1)

        def body(b, lag):
            sum_k(b - 1, range(CT, NT + 1))
            if lag:
                scatter(b - 2)
            residual(b, True)
            pool.wait_ge(kv_done, b)
            sum_k(b, range(CT))

        pool.wait_ge(params_in, 16 * N_PARAM)
        residual(0, False)
        sum_k(0, range(CT))
        pool.wait_ge(scattered, 32)
        body(1, False)
        with pool.Fori(0, B - 2) as i:
            body(i + 2, True)
        sum_k(B - 1, range(CT, NT + 1))
        scatter(B - 2)
        scatter(B - 1)
        pool.wait_ge(scattered, 16 * 2 * (NT + 1) * B + 32)

    @block.scalar
    def _(act):
        act.wait_ge(setup_v, 3)
        act.activation(m_col[:], m_col[:], ACT.Exp, scale=-1.0).then_inc(setup_a, 1)
        act.wait_ge(setup_v, 5)
        act.activation(head_scale[:], head_scale[:], ACT.Exp, scale=-LOG_S).then_inc(setup_a, 1)

        def body(b, front, back, i):
            def root(n, c, measured, done, bb):
                tiles = slice(0, CT) if c == 0 else slice(CT, NT + 1)
                act.wait_ge(measured, 2 * bb + c + 1)
                act.activation(std[:, n, tiles], mean_var[:, n, tiles, 1], ACT.Sqrt, bias=eps[:, 0:1]).then_inc(done, 1)

            def blocks(c):
                for g in range(8 * c, 8 * c + 8, 2):
                    if g == 10:
                        root(0, 0, h_measured, h_std, b)
                    act.wait_ge(x_turned, 16 * b + g + 1)
                    if g % 8 == 0 and back:
                        act.wait_ge(conv_done, 4 * (b - 1) + 2 * (c + 1))
                    act.copy(xT[c][:, g % 8, KC - 1:], ps_x[g % 2][:, 0:CW]).then_inc(xT_act, 1)
                    if g % 8 == 4:
                        conv_out(c, 0)
                conv_out(c, 1)

            def conv_out(c, f):
                act.wait_ge(conv_done, 4 * b + 2 * c + f + 1)
                if f == 0 and back:
                    act.wait_ge(h_turned, 4 * (b - 1) + 2 * (c + 1))
                act.activation(hT[c][:, f, :], ps_c[:, 0:CW], ACT.Identity, bias=h_bias[:, f:f + 1]
                               ).then_inc(hT_ready, 1)

            def from_turned(dst, u, turned, ready, bb, per=UNITS):
                act.wait_ge(turned, per * bb + u + 1)
                if u < UNITS - 1:
                    act.copy(dst[:, :, 2 * u * P:(2 * u + 2) * P],
                             t_bank(dst, u)[:, 0:4 * P].rearrange("p (f t) -> p f t", f=FB)).then_inc(ready, 1)
                else:
                    act.copy(dst[:, :, NT * P:NT * P + TX],
                             t_bank(dst, u)[:, 0:2 * TX].rearrange("p (f t) -> p f t", f=FB)).then_inc(ready, 1)

            if front:
                blocks(0)
            if back:
                for u in (2, 3, 4):
                    from_turned(qT, u, q_turned, qT_ready, b - 1)
                act.wait_ge(A_done, 2 * b)
                act.copy(A[:], ps_a[:].rearrange("p (f n) -> p f n", f=FB)).then_inc(A_ready, 1)
            if front:
                for u in (0, 1):
                    h_rows(act, b, u, back)
                blocks(1)
            if back:
                act.wait_ge(M_done, b)
                act.copy(M[:], ps_w[1][:].rearrange("p (f n) -> p f n", f=FB)).then_inc(M_ready, 1)
            if front:
                for u in (0, 1):
                    if u == 0 and back:
                        act.wait_ge(qk_done, (NT + 1) * b)
                    from_turned(xlnT, u, xln_turned, xlnT_ready, b)
                for u in (2, 3):
                    h_rows(act, b, u, back)
                squares(b, range(0, CT))
                root(0, 1, h_measured, h_std, b)
            if back:
                root(1, 0, out_measured, out_std, b - 1)
            if front:
                for u in (2, 3, 4):
                    from_turned(xlnT, u, xln_turned, xlnT_ready, b)
            if back:
                root(1, 1, out_measured, out_std, b - 1)
            if front:
                squares(b, range(CT, 6))
            if back:
                for u in range(UNITS):
                    from_turned(xfT, u, xf_turned, xfT_ready, b - 1)
                act.wait_ge(gates_done, b)
                act.copy(lT[:, 0:2 * P], ps_c[:, 0:2 * P])
                act.copy(lT[0:TX, 2 * P:], ps_c[0:TX, 2 * P:2 * P + TX]).then_inc(gates_copied, 1)
                act.wait_ge(shifted, b)
                act.activation(ex[:], lg[:], ACT.Exp).then_inc(exp_done, 1)
            if front:
                squares(b, range(6, NT + 1))
                for u in (0, 1):
                    from_turned(qT, u, q_turned, qT_ready, b)

        def h_rows(act, b, u, back):
            act.wait_ge(h_turned, 4 * b + u + 1)
            if u == 0 and back:
                act.wait_ge(base_ready, 3 * b)
            act.copy(h[:, 2 * u:2 * u + 2, :], ps_t[u % 2][:].rearrange("p (t n) -> p t n", t=2)).then_inc(h_ready, 1)

        def square(b, t):
            r = P if t < NT else TX
            act.wait_ge(qk_taken, (NT + 1) * b + t + 1)
            act.activation(qk_sq[0:r, t % 2, :], qk[0:r, t % 3, :], ACT.Square).then_inc(qk_squared, 1)

        def lengths(b, t):
            r = P if t < NT else TX
            act.wait_ge(qk_summed, (NT + 1) * b + t + 1)
            act.activation(qk_len[0:r, t % 3, :], qk_ss[0:r, t % 3, :], ACT.Sqrt).then_inc(qk_rooted, 1)

        def squares(b, tiles):
            for t in tiles:
                square(b, t)
                if t - 1 in tiles:
                    lengths(b, t - 1)
            lengths(b, tiles[-1])

        loop(act, body)

    @block.vector
    def _(dve):
        dve_value = dve.alloc_register("dve_value")
        dve.wait_ge(const_ready, 1)
        dve.wait_ge(params_in, 16 * N_PARAM)
        dve.wait_ge(setup_mm, 3)
        dve.tensor_copy(read_col[:], ps[0][:, 0:1]).then_inc(setup_v, 1)
        dve.tensor_copy(conv_b_col[:], ps[0][:, 8:8 + CBS]).then_inc(setup_v, 1)
        dve.tensor_copy(m_col[:], ps[0][:, 16:16 + FB]).then_inc(setup_v, 1)
        dve.wait_ge(setup_a, 1)
        dve.tensor_scalar(m_col[:], m_col[:], 1.0, None, ALU.add).then_inc(setup_v, 1)
        dve.wait_ge(setup_v, 4)
        dve.reciprocal(head_scale[:], m_col[:]).then_inc(setup_v, 1)
        dve.tensor_copy(block_mask[:], ps[0][:, 128:256]).then_inc(setup_v, 1)
        dve.memset(wgT[:], 0.0).then_inc(setup_v, 1)
        dve.tensor_scalar(conv_b_col[:], conv_b_col[:], read_col[:, 0:1], None, ALU.mult).then_inc(setup_v, 1)
        dve.tensor_scalar(conv_col[:], conv_in[:], read_col[:, 0:1], None, ALU.mult).then_inc(setup_v, 1)
        dve.wait_ge(setup_v, 9)
        dve.tensor_copy(wgT[:, :, 0:E], ps[0][:, 32:32 + FB * E].rearrange("p (f e) -> p f e", f=FB)
                        ).then_inc(setup_v, 1)
        dve.tensor_tensor(
            conv_mat[:].rearrange("p b k d -> p (b k) d"),
            feat_of[:].rearrange("p (a d) -> p a d", a=1).to_broadcast([P, CBS * KC, 32]),
            conv_col[:].rearrange("p b (k a) -> p (b k) a", a=1).to_broadcast([P, CBS * KC, 32]),
            ALU.mult).then_inc(setup_v, 1)
        dve.wait_ge(setup_mm, 4)
        dve.tensor_copy(h_bias[:], ps[1][:, 0:FB]).then_inc(setup_v, 1)
        dve.memset(place[:], 0.0).then_inc(counts_taken, 1)
        dve.wait_ge(setup_a, 2)

        def body(b, front, back, it):
            steps = [0]

            def step(ins):
                steps[0] += 1
                ins.then_inc(v_step, 1)
                if not back:
                    return steps[0]
                return V_FRONT + V_BOTH * it + steps[0]

            def then(v):
                dve.wait_ge(v_step, v)

            def blocks(c, blocks_of):
                for g in blocks_of:
                    dve.wait_ge(x_turned, 16 * b + g + 1)
                    if g % 8 == 1 and back:
                        dve.wait_ge(conv_done, 4 * (b - 1) + 2 * (c + 1))
                    dve.tensor_copy(xT[c][:, g % 8, KC - 1:], ps_x[g % 2][:, 0:CW]).then_inc(xT_dve, 1)

            def tiles_of(c):
                return range(0, CT) if c == 0 else range(CT, NT + 1)

            def measure(n, c, src, done):
                for t in tiles_of(c):
                    r = P if t < NT else TX
                    v = step(dve.bn_stats(stats[0:r, n, t, :], src[0:r, t, :]))
                v = in_register(dve, dve_value, v)
                dve.wait_ge(const_ready, 1)
                then(v)
                for t in tiles_of(c):
                    r = P if t < NT else TX
                    ins = dve.bn_aggr(mean_var[0:r, n, t, :], stats[0:r, n, t, :])
                ins.then_inc(done, 1)

            def center(n, c, bb, src, dst, std_done, ready):
                dve.wait_ge(std_done, 2 * bb + c + 1)
                tiles = tiles_of(c)
                cols = slice(tiles[0], tiles[-1] + 1)
                v = step(dve.reciprocal(rstd[:, n, cols], std[:, n, cols]))
                then(v)
                for t in tiles:
                    r = P if t < NT else TX
                    ins = dve.tensor_scalar(dst[0:r, t, :], src[0:r, t, :], mean_var[0:r, n, t, 0:1],
                                            rstd[0:r, n, t:t + 1], ALU.subtract, ALU.mult)
                    if t % 2 == 1 or t == NT:
                        ins.then_inc(ready, 1)

            def measure_h(c):
                for u in ((0, 1) if c == 0 else (2, 3)):
                    dve.wait_ge(h_ready, 4 * b + u + 1)
                if c == 1:
                    dve.wait_ge(txt_loaded, 16 * b + 16)
                measure(0, c, h, h_measured)

            def center_h(c):
                if back:
                    dve.wait_ge(A_done, 2 * (b - 1) + c + 1)
                center(0, c, b, h, xln, h_std, xln_ready)

            def take_qk(t):
                r = P if t < NT else TX
                dve.wait_ge(qk_done, (NT + 1) * b + t + 1)
                if t >= 3 or back:
                    dve.wait_ge(qk_normed, (NT + 1) * b + t - 2)
                bank = ps_w[qk_bank(t)]
                dve.tensor_tensor(qk[0:r, t % 3, :], bank[0:r, :], bqk_rows[0:r, :], ALU.add).then_inc(qk_taken, 1)

            def sum_squares(t):
                r = P if t < NT else TX
                dve.wait_ge(qk_squared, (NT + 1) * b + t + 1)
                dve.tensor_reduce(qk_ss[0:r, t % 3, :], qk_sq[0:r, t % 2, :].rearrange("p (h d) -> p h d", d=HD),
                                  X, ALU.add).then_inc(qk_summed, 1)

            def norm_qk(t):
                r = P if t < NT else TX
                dve.wait_ge(qk_rooted, (NT + 1) * b + t + 1)
                v = step(dve.tensor_scalar(qk_inv[0:r, t % 3, :], qk_len[0:r, t % 3, :], 1e-12, None, ALU.max))
                then(v)
                v = step(dve.reciprocal(qk_inv[0:r, t % 3, :], qk_inv[0:r, t % 3, :]))
                then(v)
                if back and t in (0, CT):
                    dve.wait_ge(A_done, 2 * (b - 1) + (1 if t == 0 else 2))
                for lo, dst in ((0, q_n), (1, k_n)):
                    inv = qk_inv[0:r, t % 3, HEADS * lo:HEADS * lo + HEADS].rearrange("p (h a) -> p h a", a=1)
                    if lo == 1 and back:
                        dve.wait_ge(k_summed, (NT + 1) * (b - 1) + t + 1)
                    ins = dve.tensor_tensor(dst[0:r, t, :].rearrange("p (h d) -> p h d", d=HD),
                                            qk[0:r, t % 3, D * lo:D * lo + D].rearrange("p (h d) -> p h d", d=HD),
                                            inv.to_broadcast([r, HEADS, HD]), ALU.mult)
                ins.then_inc(qk_normed, 1)

            def qk_tiles(tiles):
                for t in tiles:
                    take_qk(t)
                    if t - 1 in tiles:
                        sum_squares(t - 1)
                    if t - 2 in tiles:
                        norm_qk(t - 2)
                sum_squares(tiles[-1])
                norm_qk(tiles[-2])
                norm_qk(tiles[-1])

            def out_rows(c):
                bb = b - 1
                dve.wait_ge(base_ready, 3 * bb + 3)
                for u in ((0, 1) if c == 0 else (2, 3, 4)):
                    tiles = slice(2 * u, 2 * u + 2) if u < UNITS - 1 else slice(NT, NT + 1)
                    r, w = (P, 2 * D) if u < UNITS - 1 else (TX, D)
                    dve.wait_ge(out_done, UNITS * bb + u + 1)
                    dst = h_out[0:r, tiles, :].rearrange("p t n -> p (t n)")
                    dve.tensor_tensor(dst, ps_w[u % 2][0:r, 0:w], dst, ALU.add).then_inc(out_taken, 1)
                dve.wait_ge(out_taken, UNITS * bb + (2 if c == 0 else UNITS))
                measure(1, c, h_out, out_measured)

            def center_out(c):
                if c == 0:
                    dve.wait_ge(xf_stored, 16 * 3 * (b - 1) + 16)
                center(1, c, b - 1, h_out, xf, out_std, xf_ready)

            def kv_out():
                dve.wait_ge(kv_done, b)
                for f in range(FB):
                    ins = dve.scalar_tensor_tensor(out=kvT[:, f, :], in0=ps_w[0][:, f * P:(f + 1) * P],
                                                   scalar=head_scale[:, f:f + 1], in1=block_mask[:],
                                                   op0=ALU.mult, op1=ALU.mult)
                ins.then_inc(kv_ready, 1)

            def choose():
                W = NT + 1
                def wide(t):
                    return t.rearrange("p (i a) -> p i a", a=1).to_broadcast([P, W, E])
                dve.wait_ge(logits_done, b)
                dve.tensor_copy(
                    lg[:, 0:NT, :].rearrange("p (u q) e -> p u q e", q=2),
                    ps_c[:, 0:2 * P].rearrange("p (q u z) -> p u q z", q=2, z=32)[:, :, :, 0:E])
                v = step(dve.tensor_copy(lg[0:TX, NT, :], ps_c[0:TX, 2 * P:2 * P + E]))
                then(v)
                v = step(dve.tensor_reduce(top[:], lg[:], X, ALU.max))
                then(v)
                dve.tensor_tensor(lg[:], lg[:], wide(top[:]), ALU.subtract).then_inc(shifted, 1)
                dve.wait_ge(exp_done, b)
                v = step(dve.tensor_reduce(den[:], ex[:], X, ALU.add))
                then(v)
                v = step(dve.reciprocal(top[:], den[:]))
                then(v)
                v = step(dve.tensor_tensor(gate[:], ex[:], wide(top[:]), ALU.mult))
                for k in range(2):
                    then(v)
                    v = step(dve.tensor_reduce(best[:, k, :], gate[:], X, ALU.max))
                    then(v)
                    v = step(dve.tensor_tensor(same[:], gate[:], wide(best[:, k, :]), ALU.is_equal))
                    then(v)
                    v = step(dve.tensor_tensor(same[:], same[:], rank[:], ALU.mult))
                    then(v)
                    v = step(dve.tensor_reduce(chosen_rank[:, k, :], same[:], X, ALU.max))
                    then(v)
                    v = step(dve.tensor_tensor(hot[:, k, :, :].rearrange("p e i -> p i e"), same[:],
                                               wide(chosen_rank[:, k, :]), ALU.is_equal))
                    if k == 0:
                        then(v)
                        v = step(dve.scalar_tensor_tensor(out=gate[:], in0=hot[:, 0, :, :].rearrange("p e i -> p i e"),
                                                          scalar=-4.0, in1=gate[:], op0=ALU.mult, op1=ALU.add))
                then(v)
                dve.tensor_tensor(hot_bf[:], hot[:].rearrange("p k e i -> p (k e i)"), valid[:], ALU.mult
                                  ).then_inc(hot_ready, 1)

            def number():
                W, n = NT + 1, 2 * E * (NT + 1)
                dve.wait_ge(counts_done, b)
                v = step(dve.tensor_copy(runs[:, :, 1:], ps_c[:, n:2 * n].rearrange("p (k i) -> p k i", i=W)))
                then(v)
                v = step(dve.tensor_tensor_scan(ahead[:].rearrange("p k i -> p (k i)"),
                                                no_reset[:].rearrange("p k i -> p (k i)"),
                                                runs[:].rearrange("p k i -> p (k i)"), 0.0, ALU.mult, ALU.add))
                then(v)
                v = dve.tensor_tensor(place[:], ps_c[:, 0:n].rearrange("p (k i) -> p k i", i=W),
                                      ahead[:, :, 0:W], ALU.add)
                v.then_inc(counts_taken, 1)
                step(dve.tensor_copy(runs[:, :, 0:1], ahead[:, :, W:W + 1]))
                dve.wait_ge(counts_taken, b + 1)
                v = step(dve.tensor_tensor(place[:].rearrange("p k i -> p (k i)"), place[:].rearrange("p k i -> p (k i)"),
                                           hot_bf[:], ALU.mult))
                then(v)
                v = step(dve.tensor_reduce(count[:], place[:].rearrange("p (k e) i -> p k i e", k=2), X, ALU.add))
                then(v)
                v = step(dve.tensor_scalar(slot[:], count[:], float(CAP), float(FAR), ALU.is_ge, ALU.mult))
                then(v)
                v = step(dve.tensor_tensor(slot[:], slot[:], bad_row[:], ALU.add))
                v = step(dve.tensor_scalar(chosen_rank[:], chosen_rank[:], -float(SL), float(E * SL), ALU.mult, ALU.add))
                then(v)
                v = step(dve.tensor_tensor(slot[:], slot[:], chosen_rank[:], ALU.add))
                then(v)
                dve.wait_ge(scattered, 16 * 2 * W * (b - 1) + 32)
                v = step(dve.tensor_tensor(slot_i[:, 0, :], slot[:, 0, :], count[:, 0, :], ALU.add))
                v = step(dve.tensor_tensor(slot_i[:, 1, :], slot[:, 1, :], count[:, 1, :], ALU.subtract))
                for k in range(2):
                    step(dve.tensor_copy(entry[:, k, :, 0], token_id[:]))
                v = step(dve.tensor_copy(entry[:, :, :, 1], best[:]))
                then(v)
                dve.tensor_scalar(token_id[:], token_id[:], float(S), None, ALU.add).then_inc(slots_ready, 1)

            if front:
                blocks(0, range(1, 8, 2))
            if back:
                kv_out()
            if front:
                measure_h(0)
                dve.wait_ge(xT_act, 8 * b + 4)
                dve.wait_ge(xT_dve, 8 * b + 4)
                if back:
                    dve.wait_ge(conv_done, 4 * b)
                dve.tensor_copy(xT[1][:, :, 0:KC - 1], xT[0][:, :, CW:CW + KC - 1]).then_inc(halo_ready, 1)
                blocks(1, (9, 11))
                center_h(0)
                blocks(1, (13, 15))
                measure_h(1)
                qk_tiles(range(0, CT))
                center_h(1)
            if back:
                out_rows(0)
                center_out(0)
                out_rows(1)
                center_out(1)
            if front:
                qk_tiles(range(CT, 6))
            if back:
                choose()
            if front:
                qk_tiles(range(6, NT + 1))
            if back:
                number()
            want = V_BOTH if front and back else V_FRONT if front else V_BACK
            assert steps[0] == want, (front, back, steps[0])

        loop(dve, body)
        dve.wait_ge(slots_ready, B)
        dve.tensor_copy(taken[:], runs[:, 0:E, 0])

    @block.tensor
    def _(pe):
        pe_value, normed_value = pe.alloc_register("pe_value"), pe.alloc_register("pe_normed_value")
        pe.wait_ge(const_ready, 1)
        pe.wait_ge(params_in, 16 * N_PARAM)
        pe.matmul(ps[0][:, 0:1], value_of[:], read_in[:], start=True, stop=True)
        pe.transpose(ps[0][:, 8:8 + CBS], conv_b_in[:], ident[0:CBS, 0:CBS]).then_inc(setup_mm, 1)
        for f in range(FB):
            pe.matmul(ps[0][:, 16 + f:17 + f], head_of[:, f * P:(f + 1) * P], m_in[:], start=True, stop=True)
        pe.matmul(ps[0][:, 128:256], head_of[:, 0:P], head_of[:, 0:P], start=True, stop=True).then_inc(setup_mm, 1)
        for f in range(FB):
            ins = pe.transpose(ps[0][:, 32 + f * E:32 + (f + 1) * E], wg_in[:, f * P:(f + 1) * P], ident[0:E, 0:E])
        ins.then_inc(setup_mm, 1)
        pe.wait_ge(setup_v, 8)
        for cb in range(CBS):
            q = cb % 4
            ins = pe.matmul(ps[1][32 * q:32 * q + 32, cb // 4:cb // 4 + 1], feat_of[:], conv_b_col[:, cb:cb + 1],
                            start=True, stop=True, skip_group_check=True)
        ins.then_inc(setup_mm, 1)
        pe.wait_ge(setup_v, 12)
        pe.wait_ge(setup_a, 2)

        def body(b, front, back, it):
            W = NT + 1

            def conv(c):
                def turn(g):
                    n, odd = divmod(g - 2, 2)
                    if g >= 2:
                        pe.wait_ge(xT_dve if odd else xT_act, 8 * b + n + 1)
                    elif back:
                        pe.wait_ge(xT_dve if odd else xT_act, 8 * b)
                    for i in range(CT):
                        ins = pe.transpose(ps_x[g % 2][:, i * P:(i + 1) * P],
                                           x_in[:, CT * c + i, (g % 8) * P:(g % 8 + 1) * P], ident[:])
                    ins.then_inc(x_turned, 1)

                def taps(f):
                    pe.wait_ge(xT_act, 8 * b + 4 * c + 2 * (f + 1))
                    pe.wait_ge(xT_dve, 8 * b + 4 * c + 2 * (f + 1))
                    if f == 1 or c == 1:
                        pe.wait_ge(hT_ready, 4 * b + 2 * c + f)
                    elif back:
                        pe.wait_ge(counts_taken, b)
                        pe.wait_ge(hT_ready, 4 * b)
                    if c == 1 and f == 0:
                        pe.wait_ge(halo_ready, b + 1)
                    for k in range(KC):
                        for q in range(4):
                            cb = 4 * f + q
                            ins = pe.matmul(ps_c[32 * q:32 * q + 32, 0:CW], conv_mat[:, cb, k, :],
                                            xT[c][:, cb, k:k + CW], start=(k == 0), stop=(k == KC - 1),
                                            skip_group_check=True)
                    ins.then_inc(conv_done, 1)

                pe.wait_ge(x_loaded[c], 16 * b + 16)
                for g in range(8 * c, 8 * c + 6):
                    turn(g)
                taps(0)
                for g in range(8 * c + 6, 8 * c + 8):
                    turn(g)
                taps(1)

            def turn_pair(src, dst, u, turned, feature_rows=False):
                bank = t_bank(dst, u)
                if u < UNITS - 1:
                    for f in range(FB):
                        for t in range(2):
                            ins = pe.transpose(bank[:, (2 * f + t) * P:(2 * f + t + 1) * P],
                                               src[:, 2 * u + t, f * P:(f + 1) * P], ident[:])
                else:
                    for f in range(FB):
                        ins = pe.transpose(bank[:, f * TX:(f + 1) * TX], src[0:TX, NT, f * P:(f + 1) * P],
                                           ident[0:TX, 0:TX])
                ins.then_inc(turned, 1)

            def turn_q(bb, u, free):
                for s, v in free:
                    pe.wait_ge(s, v)
                normed = W * bb + (2 * u + 2 if u < UNITS - 1 else W)
                if u == UNITS - 1:
                    normed = in_register(pe, pe_value, normed)
                    pe.wait_ge(const_ready, 1)
                pe.wait_ge(qk_normed, normed)
                turn_pair(q_n, qT, u, q_turned)

            def add_A(bb, tiles, first, last):
                for t in tiles:
                    r = P if t < NT else TX
                    for f in range(FB):
                        ins = pe.matmul(ps_a[:, f * D:(f + 1) * D], xln[0:r, t, f * P:(f + 1) * P], k_n[0:r, t, :],
                                        start=(first and t == 0 and f == 0), stop=(last and t == NT),
                                        skip_group_check=True)
                ins.then_inc(A_done, 1)

            def turn_h(u):
                pe.wait_ge(hT_ready, 4 * b + 2 * (u // 2) + 2)
                if back and u < 2:
                    pe.wait_ge(qT_ready, UNITS * (b - 1) + 4 + u)
                if u >= 2:
                    pe.wait_ge(xlnT_ready, UNITS * b + u - 1)
                c, bank = u // 2, ps_t[u % 2]
                for t in range(2):
                    for f in range(FB):
                        col = (2 * (u % 2) + t) * P
                        ins = pe.transpose(bank[:, t * D + f * P:t * D + (f + 1) * P], hT[c][:, f, col:col + P], ident[:])
                ins.then_inc(h_turned, 1)

            def turn_xln(u):
                normed = UNITS * b + u + 1
                if u == UNITS - 1:
                    normed = in_register(pe, normed_value, normed)
                    copied = in_register(pe, pe_value, UNITS * b + 3)
                    pe.wait_ge(const_ready, 1)
                pe.wait_ge(xln_ready, normed)
                if u < 4:
                    pe.wait_ge(h_ready, 4 * b + u + 1)
                else:
                    pe.wait_ge(xlnT_ready, copied)
                turn_pair(xln, xlnT, u, xln_turned)

            def qk_tile(t):
                r = P if t < NT else TX
                pe.wait_ge(xlnT_ready, UNITS * b + t // 2 + 1)
                if t == 0:
                    if back:
                        pe.wait_ge(kv_ready, b)
                elif t == 1:
                    if back:
                        pe.wait_ge(M_ready, b)
                elif t < CT:
                    pe.wait_ge(qk_taken, W * b + t - 1)
                elif t == 4 or t == 5:
                    if back:
                        pe.wait_ge(out_taken, UNITS * b - 5 + t)
                    else:
                        pe.wait_ge(qk_taken, W * b + (4 if t == 4 else 3))
                else:
                    pe.wait_ge(qk_taken, W * b + t - 1)
                for f in range(FB):
                    ins = pe.matmul(ps_w[qk_bank(t)][0:r, :], xlnT[:, f, t * P:t * P + r], wqk[:, f, :],
                                    start=(f == 0), stop=(f == FB - 1))
                ins.then_inc(qk_done, 1)

            def kv():
                pe.wait_ge(A_ready, b)
                pe.wait_ge(k_summed, W * b)
                pe.wait_ge(qk_taken, W * b - 1)
                for v in range(FB):
                    cols = slice(v * P, (v + 1) * P)
                    for f in range(FB):
                        pe.matmul(ps_w[0][:, cols], wv[:, f, cols], A[:, f, cols], start=(f == 0), stop=False)
                    ins = pe.matmul(ps_w[0][:, cols], bv_rows[:, cols], k_sum[:, cols], start=False, stop=True)
                ins.then_inc(kv_done, 1)

            def fold():
                pe.wait_ge(kv_ready, b)
                pe.wait_ge(qk_taken, W * b)
                for f in range(FB):
                    ins = pe.matmul(ps_w[1][:, f * D:(f + 1) * D], kvT[:, f, :], wo[:, f, :], start=True, stop=True)
                ins.then_inc(M_done, 1)

            def attend(u):
                bb = b - 1
                if u == 0:
                    pe.wait_ge(M_ready, b)
                pe.wait_ge(qT_ready, UNITS * bb + u + 1)
                if u < 2:
                    if front:
                        pe.wait_ge(qk_taken, W * b + 3 + u)
                else:
                    pe.wait_ge(out_taken, UNITS * bb + u - 1)
                for t in ((2 * u, 2 * u + 1) if u < UNITS - 1 else (NT,)):
                    r = P if t < NT else TX
                    for f in range(FB):
                        ins = pe.matmul(ps_w[u % 2][0:r, (t % 2) * D:(t % 2 + 1) * D], qT[:, f, t * P:t * P + r],
                                        M[:, f, :], start=(f == 0), stop=(f == FB - 1))
                ins.then_inc(out_done, 1)

            def turn_xf(u):
                bb = b - 1
                normed, copied = UNITS * bb + u + 1, UNITS * bb + u - 1
                if u == UNITS - 1:
                    normed = in_register(pe, normed_value, normed)
                    copied = in_register(pe, pe_value, copied)
                    pe.wait_ge(const_ready, 1)
                pe.wait_ge(xf_ready, normed)
                if u < 2:
                    if front:
                        pe.wait_ge(xlnT_ready, UNITS * b + 4 + u)
                else:
                    pe.wait_ge(xfT_ready, copied)
                turn_pair(xf, xfT, u, xf_turned)

            def gates():
                bb = b - 1
                pe.wait_ge(xfT_ready, UNITS * bb + UNITS)
                for f in range(FB):
                    for u in range(UNITS - 1):
                        pe.matmul(ps_c[32 * u:32 * u + 32, 0:2 * P], wgT[:, f, :], xfT[:, f, 2 * u * P:(2 * u + 2) * P],
                                  start=(f == 0), stop=(f == FB - 1), skip_group_check=True)
                for f in range(FB):
                    ins = pe.matmul(ps_c[0:32, 2 * P:2 * P + TX], wgT[:, f, :], xfT[:, f, NT * P:NT * P + TX],
                                    start=(f == 0), stop=(f == FB - 1), skip_group_check=True)
                ins.then_inc(gates_done, 1)

            def turn_gates():
                pe.wait_ge(gates_copied, b)
                for q in range(2):
                    pe.transpose(ps_c[:, q * P:(q + 1) * P], lT[:, q * P:(q + 1) * P], ident[:])
                pe.transpose(ps_c[0:TX, 2 * P:2 * P + TX], lT[0:TX, 2 * P:], ident[0:TX, 0:TX]).then_inc(logits_done, 1)

            def counts():
                n = 2 * E * W
                pe.wait_ge(hot_ready, b)
                pe.matmul(ps_c[:, 0:n], before_bf[:], hot_bf[:], start=True, stop=True)
                pe.matmul(ps_c[:, n:2 * n], ones_bf[:], hot_bf[:], start=True, stop=True).then_inc(counts_done, 1)

            if front:
                conv(0)
            if back:
                turn_q(b - 1, 2, [(qT_ready, UNITS * (b - 1) + 2)])
                turn_q(b - 1, 3, [])
                turn_q(b - 1, 4, [(qT_ready, UNITS * (b - 1) + 3)])
                add_A(b - 1, range(CT, NT + 1), False, True)
            if front:
                turn_h(0)
                turn_h(1)
            if back:
                kv()
            if front:
                conv(1)
            if back:
                fold()
            if front:
                turn_xln(0)
                turn_xln(1)
                turn_h(2)
                turn_h(3)
                for t in range(CT):
                    qk_tile(t)
            if back:
                attend(0)
                attend(1)
            if front:
                turn_xln(2)
                turn_xln(3)
                turn_xln(4)
            if back:
                attend(2)
                attend(3)
                attend(4)
            if front:
                qk_tile(4)
                qk_tile(5)
            if back:
                for u in range(UNITS):
                    turn_xf(u)
                gates()
            if front:
                qk_tile(6)
            if back:
                turn_gates()
            if front:
                qk_tile(7)
                qk_tile(8)
                if back:
                    turn_q(b, 0, [(xfT_ready, UNITS * b - 1)])
                    turn_q(b, 1, [(xfT_ready, UNITS * b)])
                    pe.wait_ge(A_ready, b)
                else:
                    turn_q(b, 0, [(xlnT_ready, UNITS * b + UNITS)])
                    turn_q(b, 1, [(xlnT_ready, UNITS * b + 4)])
                add_A(b, range(CT), True, False)
            if back:
                counts()

        loop(pe, body)


LOG_S = 6.962243464266207
V_FRONT, V_BOTH, V_BACK = 29, 70, 41


def stage_two(nc, ctx, dram, keep):
    W1, b1, W2, b2, out = (dram[n] for n in ("W1", "b1", "W2", "b2", "out"))
    rows, tab_first, tab_second = dram["rows"], dram["tab_first"], dram["tab_second"]
    ident, taken = keep["ident"], keep["taken"]

    def sb(name, shape, dt=F32):
        return ctx.enter_context(nc.sbuf_tensor(name, shape, dt))

    def sem(name):
        return ctx.enter_context(nc.semaphore(name))

    first = sb("first", [SR, E, ST, 2])
    second = sb("second", [SR, E, ST, 2])
    slot_no = sb("slot_no", [SR, ST])
    is_first = sb("is_first", [SR, E, ST], I32)
    near = sb("near", [SR, E * ST])
    plan = sb("plan", [SR, E * NCH, 3, CC], I32)
    take = sb("take", [SR, CC], I32)
    give = sb("give", [SR, 2, CC], I32)
    w1_in, w2_in = (keep["x_in"][:].rearrange("p i n -> p (i n)")[:, at:at + n * w].rearrange("p (b n) -> p b n", b=n)
                    for at, n, w in W_AT)
    w1_hi, w1_lo = (sb(f"w1_{n}", [P, FB, H], F32R) for n in ("hi", "lo"))
    w2_hi, w2_lo = (sb(f"w2_{n}", [P, MB, D], F32R) for n in ("hi", "lo"))
    b1_col = sb("b1_col", [P, MB])
    b2_col = sb("b2_col", [P, FB])
    xg = sb("xg", [SR, CC, D])
    x_hi, x_lo = (sb(f"x_{n}", [P, FB, N2], F32R) for n in ("hi", "lo"))
    g = sb("g", [P, 4, N2])
    g_hi, g_lo = (sb(f"g_{n}", [P, MB, N2], F32R) for n in ("hi", "lo"))
    yT = sb("yT", [P, FB, N2])
    y = sb("y", [SR, CC, D])

    ps = [ctx.enter_context(nc.psum_tensor(f"qs{i}", [P, 512], F32)) for i in range(8)]
    ps_h, ps_y, ps_x, ps_r = ps[0:3], ps[3:5], ps[5:7], ps[7]

    tables_in = sem("tables_in")
    t_step = sem("t_step")
    slots_no = sem("slots_no")
    plan_ready = sem("plan_ready")
    take_loaded = sem("take_loaded")
    give_loaded = sem("give_loaded")
    w1_loaded, w2_loaded = keep["w1_loaded"], keep["w2_loaded"]
    b1_loaded = sem("b1_loaded")
    b2_loaded = sem("b2_loaded")
    w1_high = sem("w1_high")
    w2_high = sem("w2_high")
    w1_split = sem("w1_split")
    w2_split = sem("w2_split")
    gathered = sem("gathered")
    x_turned = sem("x_turned2")
    x_halves = sem("x_halves")
    x_split = sem("x_split")
    h_done = sem("h_done")
    gelu_done = sem("gelu_done")
    g_high = sem("g_high")
    g_split = sem("g_split")
    y_done = sem("y_done")
    yT_ready = sem("yT_ready")
    y_turned = sem("y_turned")
    y_ready = sem("y_ready")
    added = sem("added")
    NG = E * NCH

    block = ctx.enter_context(nc.Block())

    @block.sync
    def _(sp):
        def load_w1(e):
            sp.wait_ge(w1_split, MB * e)
            sp.dma_start(w1_in, W1[bass.ds(e, 1), :, :].rearrange("a (b p) n -> p (a b) n", p=P)
                         ).then_inc(w1_loaded, 16)

        def load_w2(e):
            sp.wait_ge(w2_split, MB * e)
            sp.dma_start(w2_in, W2[bass.ds(e, 1), :, :].rearrange("a (b p) n -> p (a b) n", p=P)
                         ).then_inc(w2_loaded, 16)

        def load_b1(e):
            sp.dma_start(b1_col[:], b1[bass.ds(e, 1), :].rearrange("a (m p) -> p (a m)", p=P),
                         allow_slow_non_contiguous=True).then_inc(b1_loaded, 16)

        def load_b2(e):
            sp.dma_start(b2_col[:], b2[bass.ds(e, 1), :].rearrange("a (m p) -> p (a m)", p=P),
                         allow_slow_non_contiguous=True).then_inc(b2_loaded, 16)

        def load_take(c):
            sp.dma_start(take[:], plan[:, bass.ds(c, 1), 0, :].rearrange("p a i -> p (a i)")
                         ).then_inc(take_loaded, 16)

        def load_give(c, first):
            if not first:
                sp.wait_ge(added, 64 * c)
            sp.dma_start(give[:], plan[:, bass.ds(c, 1), 1:3, :].rearrange("p a k i -> p (a k) i")
                         ).then_inc(give_loaded, 16)

        def expert(e, first=False, last=False):
            if not last:
                load_w1(e + 1)
            for j in range(NCH):
                c = NCH * e + j
                if not (last and j == NCH - 1):
                    sp.wait_ge(gathered, 64 * (c + 1))
                    load_take(c + 1)
                if j == 0:
                    if not first:
                        sp.wait_ge(yT_ready, c)
                    load_b2(e)
                load_give(c, first and j == 0)
                if j == 1 and not last:
                    load_w2(e + 1)
            if not last:
                sp.wait_ge(gelu_done, MB * NCH * (e + 1))
                load_b1(e + 1)

        for tab, dst in ((tab_first, first), (tab_second, second)):
            sp.dma_start(dst[:].rearrange("p e i w -> p e (i w)"),
                         tab.rearrange("(e p i) w -> p e (i w)", e=E, p=SR)).then_inc(tables_in, 16)
        load_b1(0)
        sp.wait_ge(plan_ready, 1)
        load_take(0)
        expert(0, first=True)
        with sp.Fori(1, E - 1) as e:
            expert(e)
        expert(E - 1, last=True)

    @block.gpsimd
    def _(pool):
        loaded_value, weighed_value, before_value = (
            pool.alloc_register(f"{n}_value") for n in ("loaded", "weighed", "before"))
        pool.iota(slot_no[:], [[1, ST]], base=0, channel_multiplier=ST,
                  allow_small_or_imprecise_dtypes=True).then_inc(slots_no, 1)

        def gather(c):
            loaded = in_register(pool, loaded_value, 16 * (c + 1))
            pool.wait_ge(slots_no, 1)
            pool.wait_ge(take_loaded, loaded)
            for i in range(CC):
                pool.indirect_dma_start(xg[:, i, :], None, rows,
                                        bass.IndirectOffsetOnAxis(take[:, i:i + 1].bitcast(U32), 0)
                                        ).then_inc(gathered, 16)

        def add(c):
            loaded = in_register(pool, loaded_value, 16 * (c + 1))
            weighed = in_register(pool, weighed_value, 2 * (c + 1))
            before = in_register(pool, before_value, 64 * c)
            pool.wait_ge(slots_no, 1)
            pool.wait_ge(give_loaded, loaded)
            pool.wait_ge(y_ready, weighed)
            if not (isinstance(c, int) and c == 0):
                pool.wait_ge(added, before)
            for i in range(CC):
                pool.indirect_dma_start(dram["out_rows"], bass.IndirectOffsetOnAxis(give[:, 0, i:i + 1].bitcast(U32), 0),
                                        y[:, i, :], None, bounds_check=TOK - 1, oob_is_err=False,
                                        compute_op=ALU.add).then_inc(added, 16)

        gather(0)

        def gather_next(c):
            pool.wait_ge(x_turned, 2 * (c + 1))
            gather(c + 1)

        gather_next(0)
        gather_next(1)
        add(0)
        with pool.Fori(2, NG - 1) as c:
            gather_next(c)
            add(c - 1)
        add(NG - 2)
        add(NG - 1)
        pool.wait_ge(added, 64 * NG)

    @block.scalar
    def _(act):
        def body(c, first):
            for m in range(MB):
                act.wait_ge(h_done, MB * c + m + 1)
                if not (first and m < 4):
                    act.wait_ge(g_split, MB * c + m - 3)
                act.activation(g[:, m % 4, :], ps_h[m % 3][:, 0:N2], ACT.Gelu, bias=b1_col[:, m:m + 1]
                               ).then_inc(gelu_done, 1)
            act.wait_ge(y_done, c + 1)
            if not first:
                act.wait_ge(y_turned, 2 * c)
            for f in range(FB):
                ins = act.activation(yT[:, f, :], ps_y[f][:, 0:N2], ACT.Identity, bias=b2_col[:, f:f + 1])
            ins.then_inc(yT_ready, 1)

        body(0, True)
        with act.Fori(1, NG) as c:
            body(c, False)

    @block.vector
    def _(dve):
        dve.wait_ge(slots_no, 1)
        dve.tensor_tensor(is_first[:],
                          slot_no[:].rearrange("p (a i) -> p a i", a=1).to_broadcast([SR, E, ST]),
                          taken[0:SR, :].rearrange("p (e a) -> p e a", a=1).to_broadcast([SR, E, ST]),
                          ALU.is_lt).then_inc(t_step, 1)
        dve.wait_ge(t_step, 1)
        dve.wait_ge(tables_in, 32)
        for w in range(2):
            dve.copy_predicated(second[:, :, :, w], is_first[:], first[:, :, :, w]).then_inc(t_step, 1)
        dve.wait_ge(t_step, 3)
        dve.tensor_scalar(near[:], second[:, :, :, 0].rearrange("p e i -> p (e i)"), float(TOK - 1), None, ALU.min
                          ).then_inc(t_step, 1)
        chunks = second[:].rearrange("p e (c q) w -> p (e c) q w", q=CC)
        dve.tensor_copy(plan[:, :, 1, :], chunks[:, :, :, 0]).then_inc(t_step, 1)
        dve.tensor_copy(plan[:, :, 2, :].bitcast(F32), chunks[:, :, :, 1]).then_inc(t_step, 1)
        dve.wait_ge(t_step, 6)
        dve.tensor_copy(plan[:, :, 0, :], near[:].rearrange("p (c q) -> p c q", q=CC)).then_inc(plan_ready, 1)

        def split_w1(e, m):
            cols = slice(m * P, (m + 1) * P)
            if m == 0:
                dve.wait_ge(w1_loaded, 16 * (e + 1))
            dve.tensor_copy(w1_hi[:, :, cols], w1_in[:, :, cols]).then_inc(w1_high, 1)
            dve.wait_ge(w1_high, MB * e + m + 1)
            dve.tensor_tensor(w1_lo[:, :, cols], w1_in[:, :, cols], w1_hi[:, :, cols].bitcast(F32), ALU.subtract
                              ).then_inc(w1_split, 1)

        def split_w2(e, m):
            if m == 0:
                dve.wait_ge(w2_loaded, 16 * (e + 1))
            dve.tensor_copy(w2_hi[:, m, :], w2_in[:, m, :]).then_inc(w2_high, 1)
            dve.wait_ge(w2_high, MB * e + m + 1)
            dve.tensor_tensor(w2_lo[:, m, :], w2_in[:, m, :], w2_hi[:, m, :].bitcast(F32), ALU.subtract
                              ).then_inc(w2_split, 1)

        def split_x(c):
            for f in range(FB):
                dve.wait_ge(x_turned, 2 * c + f + 1)
                dve.tensor_copy(x_hi[:, f, :], ps_x[f][:, 0:N2]).then_inc(x_halves, 1)
            dve.wait_ge(x_halves, 2 * c + 2)
            for f in range(FB):
                ins = dve.tensor_tensor(x_lo[:, f, :], ps_x[f][:, 0:N2], x_hi[:, f, :].bitcast(F32), ALU.subtract)
            ins.then_inc(x_split, 1)

        def weigh(c, half):
            dve.wait_ge(y_turned, 2 * c + half + 1)
            if half == 0:
                dve.wait_ge(give_loaded, 16 * (c + 1))
                if not (isinstance(c, int) and c == 0):
                    dve.wait_ge(added, 64 * c)
            for i in (0, 1):
                t = 2 * half + i
                ins = dve.tensor_scalar(y[:, t, :], ps_r[0:SR, i * D:(i + 1) * D], give[:, 1, t:t + 1].bitcast(F32),
                                        None, ALU.mult)
            ins.then_inc(y_ready, 1)

        def chunk(c, e, start=False, end=False, first=False, last=False):
            if not first:
                dve.wait_ge(y_done, c)
            for m in range(MB):
                if start:
                    split_w2(e, m)
                dve.wait_ge(gelu_done, MB * c + m + 1)
                dve.tensor_copy(g_hi[:, m, :], g[:, m % 4, :]).then_inc(g_high, 1)
                dve.wait_ge(g_high, MB * c + m + 1)
                dve.tensor_tensor(g_lo[:, m, :], g[:, m % 4, :], g_hi[:, m, :].bitcast(F32), ALU.subtract
                                  ).then_inc(g_split, 1)
                if m in (2, 5) and not first:
                    weigh(c - 1, m // 3)
                if end and not last:
                    dve.wait_ge(h_done, MB * c + m + 1)
                    split_w1(e + 1, m)
                if m == 5 and start:
                    dve.wait_ge(b2_loaded, 16 * (e + 1))
            if last:
                return
            dve.wait_ge(h_done, MB * (c + 1))
            if end:
                dve.wait_ge(b1_loaded, 16 * (e + 2))
            split_x(c + 1)

        def expert(e, first=False, last=False):
            chunk(NCH * e, e, start=True, first=first)
            if first:
                for j in range(1, NCH - 1):
                    chunk(NCH * e + j, e)
            else:
                with dve.Fori(1, NCH - 1) as j:
                    chunk(NCH * e + j, e)
            chunk(NCH * e + NCH - 1, e, end=True, last=last)

        for m in range(MB):
            split_w1(0, m)
        dve.wait_ge(b1_loaded, 16)
        split_x(0)
        expert(0, first=True)
        with dve.Fori(1, E - 1) as e:
            expert(e)
        expert(E - 1, last=True)
        weigh(NG - 1, 0)
        weigh(NG - 1, 1)

    @block.tensor
    def _(pe):
        def turn_x(c):
            pe.wait_ge(gathered, 64 * (c + 1))
            for f in range(FB):
                for i in range(CC):
                    ins = pe.transpose(ps_x[f][:, i * SR:(i + 1) * SR], xg[:, i, f * P:(f + 1) * P],
                                       ident[0:SR, 0:SR])
                ins.then_inc(x_turned, 1)

        def turn_y(c, half, first):
            if half == 0:
                pe.wait_ge(yT_ready, c + 1)
            if not (first and half == 0):
                pe.wait_ge(y_ready, 2 * c + half)
            for i in (0, 1):
                t = 2 * half + i
                for f in range(FB):
                    ins = pe.transpose(ps_r[0:SR, i * D + f * P:i * D + (f + 1) * P],
                                       yT[:, f, t * SR:(t + 1) * SR], ident[:])
            ins.then_inc(y_turned, 1)

        def product(dst, w_hi, w_lo, v_hi, v_lo, start, stop):
            pe.matmul(dst, w_hi, v_hi, start=start, stop=False)
            pe.matmul(dst, w_hi, v_lo, start=False, stop=False)
            return pe.matmul(dst, w_lo, v_hi, start=False, stop=stop)

        def body(c, first, last):
            pe.wait_ge(x_split, c + 1)
            for m in range(MB):
                if m >= 3:
                    pe.wait_ge(gelu_done, MB * c + m - 2)
                elif not first and m < 2:
                    pe.wait_ge(gelu_done, MB * c - 1 + m)
                cols = slice(m * P, (m + 1) * P)
                for f in range(FB):
                    ins = product(ps_h[m % 3][:, 0:N2], w1_hi[:, f, cols], w1_lo[:, f, cols],
                                  x_hi[:, f, :], x_lo[:, f, :], f == 0, f == FB - 1)
                ins.then_inc(h_done, 1)
                if not first and m in (2, 5):
                    turn_y(c - 1, m // 3, False)
            for k in range(MB):
                pe.wait_ge(g_split, MB * c + k + 1)
                for f in range(FB):
                    cols = slice(f * P, (f + 1) * P)
                    ins = product(ps_y[f][:, 0:N2], w2_hi[:, k, cols], w2_lo[:, k, cols],
                                  g_hi[:, k, :], g_lo[:, k, :], k == 0, k == MB - 1)
                if k == MB // 2 - 1 and not last:
                    turn_x(c + 1)
            ins.then_inc(y_done, 1)

        turn_x(0)
        body(0, True, False)
        with pe.Fori(1, NG - 1) as c:
            body(c, False, False)
        body(NG - 1, False, True)
        for half in (0, 1):
            turn_y(NG - 1, half, False)


def tokens_attention_experts(nc, dram):
    with ExitStack() as ctx:
        rows = nc.dram_tensor("rows", [TOK, D], F32).ap()
        tab_first = nc.dram_tensor("tab_first", [E * SL, 2], F32).ap()
        tab_second = nc.dram_tensor("tab_second", [E * SL, 2], F32).ap()
        dram = dict(dram, rows=rows, tab_first=tab_first, tab_second=tab_second,
                    out_rows=dram["out"].rearrange("b s n -> (b s) n"))
        keep = {"ident": ctx.enter_context(nc.sbuf_tensor("ident", [P, P], F32)),
                "taken": ctx.enter_context(nc.sbuf_tensor("taken", [P, E], F32)),
                "x_in": ctx.enter_context(nc.sbuf_tensor("x_in", [P, NT, CH], F32)),
                "w1_loaded": ctx.enter_context(nc.semaphore("w1_loaded")),
                "w2_loaded": ctx.enter_context(nc.semaphore("w2_loaded"))}
        with ExitStack() as one:
            stage_one(nc, one, dram, keep)
        with ExitStack() as two:
            stage_two(nc, two, dram, keep)


_INS = {'x': 'x', 'txt': 'txt', 'L0_tok_conv_w': 'conv_w', 'L0_tok_conv_b': 'conv_b', 'L0_tok_read': 'read',
        'L0_attn_Wq': 'Wq', 'L0_attn_bq': 'bq', 'L0_attn_Wk': 'Wk', 'L0_attn_bk': 'bk', 'L0_attn_Wv': 'Wv',
        'L0_attn_bv': 'bv', 'L0_attn_Wo': 'Wo', 'L0_attn_bo': 'bo', 'L0_attn_m': 'm', 'L0_ffn_Wg': 'Wg',
        'L0_ffn_W1': 'W1', 'L0_ffn_b1': 'b1', 'L0_ffn_W2': 'W2', 'L0_ffn_b2': 'b2'}


def kernel(**inputs):
    import numpy as _np
    import concourse.bacc as _bacc
    from concourse import mybir as _mybir
    from concourse.bass_utils import run_bass_kernel_spmd as _run

    nc = _bacc.Bacc("TRN2", target_bir_lowering=False, num_devices=1)
    arrays, dram = {}, {}
    for name, short in _INS.items():
        a = _np.ascontiguousarray(inputs[name])
        arrays[f"in_{name}_dram"] = a
        dram[short] = nc.dram_tensor(f"in_{name}_dram", a.shape, _mybir.dt.from_np(a.dtype), kind="ExternalInput").ap()
    dram["out"] = nc.dram_tensor("out_0_dram", (B, S, D), F32, kind="ExternalOutput").ap()
    tokens_attention_experts(nc, dram)
    r = _run(nc, [arrays], core_ids=[0])
    return r.results[0]["out_0_dram"]
```

```python
from contextlib import ExitStack

import concourse.bass as bass
from concourse import mybir

F32 = mybir.dt.float32
F32R = mybir.dt.float32r
BF16 = mybir.dt.bfloat16
I32 = mybir.dt.int32
U32 = mybir.dt.uint32
ALU = mybir.AluOpType
ACT = mybir.ActivationFunctionType
X = mybir.AxisListType.X

P = 128
B, TI, D, DV = 8, 1024, 256, 4
TX = 32
S = TI + TX
TOK = B * S
CH = D * DV
KC = 4
CBS = CH // P
FB = D // P
HEADS, HD = 16, 16
E, H = 8, 1024
CAP = int(round(2 * TOK * 1.05 / E))
NT = TI // P
CT = 4
CW = CT * P
UNITS = NT // 2 + 1

SR = 111
ST = 20
SL = SR * ST
CC = 4
NCH = ST // CC
N2 = CC * SR
MB = H // P
W_AT = ((0, FB, H), (FB * H, MB, D))
FAR = 1 << 20
EMPTYING = 2 + CC
LN_EPS = 1e-5


def in_register(eng, register, value):
    if isinstance(value, int):
        return value
    eng.reg_mov(register, value)
    return register


def stage_one(nc, ctx, dram, keep):
    x, txt, conv_w, conv_b, read, Wq, bq, Wk, bk, Wv, bv, Wo, bo, m, Wg, sums = (
        dram[n] for n in ("x", "txt", "conv_w", "conv_b", "read", "Wq", "bq", "Wk", "bk", "Wv", "bv",
                          "Wo", "bo", "m", "Wg", "sums"))
    rows, tab_first, tab_second = dram["rows"], dram["tab_first"], dram["tab_second"]
    ident, taken, x_in = keep["ident"], keep["taken"], keep["x_in"]
    W1, W2 = dram["W1"], dram["W2"]

    def sb(name, shape, dt=F32):
        return ctx.enter_context(nc.sbuf_tensor(name, shape, dt))

    def sem(name):
        return ctx.enter_context(nc.semaphore(name))

    ones_bf = sb("ones_bf", [P, P], BF16)
    before_bf = sb("before_bf", [P, P], BF16)
    head_of = sb("head_of", [HEADS, D])
    value_of = sb("value_of", [DV, P])
    feat_of = sb("feat_of", [P, 32])
    block_mask = sb("block_mask", [P, P])
    rank = sb("rank", [P, NT + 1, E])
    valid = sb("valid", [P, 2 * E * (NT + 1)])
    no_reset = sb("no_reset", [P, 2 * E, NT + 2])
    bad_row = sb("bad_row", [P, 2, NT + 1])
    token_id = sb("token_id", [P, NT + 1])
    empty_slots = sb("empty_slots", [P, E * ST, 2])
    zeros = sb("zeros", [P, D])
    wqk = sb("wqk", [P, FB, 2 * D])
    wv = sb("wv", [P, FB, D])
    wo = sb("wo", [P, FB, D])
    bqk_rows = sb("bqk_rows", [P, 2 * D])
    bo_rows = sb("bo_rows", [P, D])
    bv_rows = sb("bv_rows", [P, D])
    wg_in = sb("wg_in", [E, D])
    wgT = sb("wgT", [P, FB, 32])
    conv_in = sb("conv_in", [P, CBS, KC])
    conv_b_in = sb("conv_b_in", [CBS, P])
    read_in = sb("read_in", [DV, 1])
    m_in = sb("m_in", [HEADS, 1])
    read_col = sb("read_col", [P, 1])
    conv_col = sb("conv_col", [P, CBS, KC])
    conv_mat = sb("conv_mat", [P, CBS, KC, 32])
    conv_b_col = sb("conv_b_col", [P, CBS])
    h_bias = sb("h_bias", [P, FB])
    m_col = sb("m_col", [P, FB])
    head_scale = sb("head_scale", [P, FB])
    xT = [sb(f"xT{c}", [P, CBS, KC - 1 + CW]) for c in range(2)]
    hT = [sb(f"hT{c}", [P, FB, CW]) for c in range(2)]
    h = sb("h", [P, NT + 1, D])
    h_out = sb("h_out", [P, NT + 1, D])
    xln = sb("xln", [P, NT + 1, D])
    xlnT = sb("xlnT", [P, FB, (NT + 1) * P])
    qk = sb("qk", [P, 3, 2 * D])
    qk_sq = sb("qk_sq", [P, 2, 2 * D])
    qk_ss = sb("qk_ss", [P, 3, 2 * HEADS])
    qk_len = sb("qk_len", [P, 3, 2 * HEADS])
    qk_inv = sb("qk_inv", [P, 3, 2 * HEADS])
    q_n = sb("q_n", [P, NT + 1, D])
    k_n = sb("k_n", [P, NT + 1, D])
    k_sum = sb("k_sum", [P, D])
    qT = sb("qT", [P, FB, (NT + 1) * P])
    A = sb("A", [P, FB, D])
    kvT = sb("kvT", [P, FB, P])
    M = sb("M", [P, FB, D])
    xf = sb("xf", [P, NT + 1, D])
    xfT = sb("xfT", [P, FB, (NT + 1) * P])
    eps = sb("eps", [P, 1])
    stats = sb("stats", [P, 2, NT + 1, 6])
    mean_var = sb("mean_var", [P, 2, NT + 1, 2])
    std = sb("std", [P, 2, NT + 1])
    rstd = sb("rstd", [P, 2, NT + 1])
    shift = sb("shift", [P, 2, NT + 1])
    lT = sb("lT", [P, 2 * P + TX])
    lg = sb("lg", [P, NT + 1, E])
    top = sb("top", [P, NT + 1])
    ex = sb("ex", [P, NT + 1, E])
    den = sb("den", [P, NT + 1])
    gate = sb("gate", [P, NT + 1, E])
    best = sb("best", [P, 2, NT + 1])
    same = sb("same", [P, NT + 1, E])
    chosen_rank = sb("chosen_rank", [P, 2, NT + 1])
    hot = sb("hot", [P, 2, E, NT + 1])
    hot_bf = sb("hot_bf", [P, 2 * E * (NT + 1)], BF16)
    runs = sb("runs", [P, 2 * E, NT + 2])
    ahead = sb("ahead", [P, 2 * E, NT + 2])
    place = sb("place", [P, 2 * E, NT + 1])
    count = sb("count", [P, 2, NT + 1])
    slot = sb("slot", [P, 2, NT + 1])
    slot_i = sb("slot_i", [P, 2, NT + 1], I32)
    entry = sb("entry", [P, 2, NT + 1, 2])

    ps = [ctx.enter_context(nc.psum_tensor(f"ps{i}", [P, 512], F32)) for i in range(8)]
    ps_x = ps[0:2]
    ps_t = [ps[2], ps[5]]
    ps_c = ps[3]
    ps_conv = [[ps[3], ps[7]], [ps[3], ps[6]]]
    ps_a = ps[4]
    ps_w = ps[6:8]

    const_ready = sem("const_ready")
    const_step = sem("const_step")
    params_in = sem("params_in")
    setup_mm = sem("setup_mm")
    setup_v = sem("setup_v")
    setup_a = sem("setup_a")
    x_loaded = [sem(f"x_loaded{c}") for c in range(2)]
    txt_loaded = sem("txt_loaded")
    x_turned = sem("x_turned")
    xT_ready = sem("xT_ready")
    halo_ready = sem("halo_ready")
    conv_done = sem("conv_done")
    hT_ready = sem("hT_ready")
    h_turned = sem("h_turned")
    h_ready = sem("h_ready")
    xln_ready = sem("xln_ready")
    xln_turned = sem("xln_turned")
    xlnT_ready = sem("xlnT_ready")
    qk_done = sem("qk_done")
    qk_taken = sem("qk_taken")
    qk_squared = sem("qk_squared")
    qk_summed = sem("qk_summed")
    qk_rooted = sem("qk_rooted")
    h_measured = sem("h_measured")
    h_std = sem("h_std")
    out_measured = sem("out_measured")
    out_std = sem("out_std")
    h_scale = sem("h_scale")
    out_scale = sem("out_scale")
    qk_normed = sem("qk_normed")
    k_summed = sem("k_summed")
    q_turned = sem("q_turned")
    qT_ready = sem("qT_ready")
    A_done = sem("A_done")
    A_ready = sem("A_ready")
    kv_done = sem("kv_done")
    kv_ready = sem("kv_ready")
    M_done = sem("M_done")
    M_ready = sem("M_ready")
    base_ready = sem("base_ready")
    out_done = sem("out_done")
    out_taken = sem("out_taken")
    xf_ready = sem("xf_ready")
    xf_turned = sem("xf_turned")
    xfT_ready = sem("xfT_ready")
    gates_done = sem("gates_done")
    gates_copied = sem("gates_copied")
    logits_done = sem("logits_done")
    logits_taken = sem("logits_taken")
    shifted = sem("shifted")
    exp_done = sem("exp_done")
    hot_ready = sem("hot_ready")
    counts_done = sem("counts_done")
    counts_taken = sem("counts_taken")
    slots_ready = sem("slots_ready")
    scattered = sem("scattered")
    out_stored = sem("out_stored")
    xf_stored = sem("xf_stored")
    v_step = sem("v_step")
    N_PARAM = 13

    def t_bank(dst, u):
        if dst is xfT:
            return ps_t[(u + 1) % 2]
        if dst is qT:
            return ps_t[{0: 0, 1: 1, 2: 1, 3: 0, 4: 1}[u]]
        return ps_t[u % 2]

    def qk_bank(t):
        return t % 2 if t < CT else (t + 1) % 2

    block = ctx.enter_context(nc.Block())

    def loop(eng, body):
        body(0, True, False, 0)
        with eng.Fori(0, B - 1) as i:
            body(i + 1, True, True, i)
        body(B, False, True, B - 1)

    @block.sync
    def _(sp):
        normed_value, copied_value = sp.alloc_register("normed_value"), sp.alloc_register("copied_value")
        x4 = x.rearrange("b (c i p) d v -> (b c) p i (d v)", c=2, i=CT, p=P)

        def load_x(b, c, waits):
            if waits:
                sp.wait_ge(x_turned, 16 * (b - 1) + 8 * (c + 1))
            sp.dma_start(x_in[:, CT * c:CT * (c + 1), :],
                         x4[bass.ds(b * 2 + c, 1), :, :, :].rearrange("a p i n -> p (a i) n")
                         ).then_inc(x_loaded[c], 16)

        load_x(0, 0, False)
        for dst, src in (
            (wqk[:, :, 0:D], Wq.rearrange("(b p) n -> p b n", p=P)),
            (wqk[:, :, D:2 * D], Wk.rearrange("(b p) n -> p b n", p=P)),
            (wv[:], Wv.rearrange("(b p) n -> p b n", p=P)),
            (wo[:], Wo.rearrange("(b p) n -> p b n", p=P)),
            (bqk_rows[:, 0:D], bq.rearrange("(a n) -> a n", a=1).to_broadcast([P, D])),
            (bqk_rows[:, D:2 * D], bk.rearrange("(a n) -> a n", a=1).to_broadcast([P, D])),
            (bo_rows[:], bo.rearrange("(a n) -> a n", a=1).to_broadcast([P, D])),
            (bv_rows[:], bv.rearrange("(a n) -> a n", a=1).to_broadcast([P, D])),
            (wg_in[:], Wg),
            (conv_in[:], conv_w.rearrange("(b p) k -> p b k", p=P)),
            (conv_b_in[:], conv_b.rearrange("(b p) -> b p", p=P)),
            (read_in[:], read.rearrange("(v a) -> v a", a=1)),
            (m_in[:], m.rearrange("(v a) -> v a", a=1)),
        ):
            sp.dma_start(dst, src).then_inc(params_in, 16)
        sp.wait_ge(params_in, 16 * N_PARAM)

        def load_txt(b, waits):
            if waits:
                normed = in_register(sp, normed_value, UNITS * b)
                copied = in_register(sp, copied_value, 3 * b)
                sp.wait_ge(params_in, 16 * N_PARAM)
                sp.wait_ge(xln_ready, normed)
                sp.wait_ge(base_ready, copied)
            sp.dma_start(h[0:TX, NT, :], txt[bass.ds(b, 1), :, :].rearrange("a t n -> (a t) n")
                         ).then_inc(txt_loaded, 16)


        def store(b, dst, src, ready, stored):
            for c in range(2):
                sp.wait_ge(ready, UNITS * b + 2 * (c + 1))
                sp.dma_start(dst[bass.ds(b * S + c * CW, CW), :].rearrange("(i p) n -> p i n", p=P),
                             src[:, CT * c:CT * (c + 1), :]).then_inc(stored, 16)
            sp.wait_ge(ready, UNITS * b + UNITS)
            sp.dma_start(dst[bass.ds(b * S + TI, TX), :], src[0:TX, NT, :]).then_inc(stored, 16)

        load_x(0, 1, False)
        load_txt(0, False)
        for c in range(2):
            load_x(1, c, True)
        load_txt(1, True)
        with sp.Fori(0, B - 2) as i:
            for c in range(2):
                load_x(i + 2, c, True)
            store(i, sums, h_out, xf_ready, out_stored)
            store(i, rows, xf, xf_ready, xf_stored)
            load_txt(i + 2, True)
        for b in (B - 2, B - 1):
            store(b, sums, h_out, xf_ready, out_stored)
            store(b, rows, xf, xf_ready, xf_stored)
            if b == B - 2:
                sp.wait_ge(x_turned, 16 * B)
                for (at, n, w), src in zip(W_AT, (W1, W2)):
                    sp.dma_start(x_in[:].rearrange("p i n -> p (i n)")[:, at:at + n * w].rearrange("p (b n) -> p b n", b=n),
                                 src[0:1, :, :].rearrange("a (b p) n -> p (a b) n", p=P)
                                 ).then_inc(keep["w1_loaded" if src is W1 else "w2_loaded"], 16)
        sp.wait_ge(out_stored, 16 * 3 * B)
        sp.wait_ge(xf_stored, 16 * 3 * B + 16)

    @block.gpsimd
    def _(pool):
        pool_value = pool.alloc_register("pool_value")
        n = [0]

        def step(ins, wait=True):
            n[0] += 1
            ins.then_inc(const_step, 1)
            if wait:
                pool.wait_ge(const_step, n[0])

        def keep_where(t, pattern, base, mult, op, fill=0.0):
            step(pool.affine_select(out=t, in_=t, compare_op=op, fill=fill, base=base, pattern=pattern,
                                    channel_multiplier=mult))

        for t, v in ((ident, 0.0), (ones_bf, 1.0), (before_bf, 1.0), (feat_of, 1.0), (valid, 1.0), (no_reset, 1.0), (bad_row, 0.0), (empty_slots, 0.0),
                     (lg, 0.0), (hot, 0.0), (runs, 0.0), (taken, 0.0), (k_sum, 0.0),
                     (eps, LN_EPS), (mean_var, 1.0), (zeros, 0.0)):
            step(pool.memset(t[:], v), wait=False)
        for e in range(E):
            step(pool.memset(rank[:, :, e:e + 1], float(E - e)), wait=False)
        step(pool.memset(xT[0][:, :, 0:KC - 1], 0.0))
        for t, v in ((head_of, 1.0), (value_of, 1.0)):
            step(pool.memset(t[:], v))
        keep_where(ident[:], [[-1, P]], 0, 1, ALU.not_equal, 1.0)
        keep_where(before_bf[:], [[1, P]], -1, -1, ALU.is_ge)
        keep_where(head_of[:], [[1, D]], 0, -HD, ALU.is_ge)
        keep_where(head_of[:], [[-1, D]], HD - 1, HD, ALU.is_ge)
        v3 = value_of[:].rearrange("v (a b) -> v a b", b=DV)
        keep_where(v3, [[0, P // DV], [-1, DV]], 0, 1, ALU.is_equal)
        keep_where(feat_of[:], [[-DV, 32]], 0, 1, ALU.is_ge)
        keep_where(feat_of[:], [[DV, 32]], DV - 1, -1, ALU.is_ge)
        step(pool.memset(valid[:].rearrange("p (k i) -> p k i", i=NT + 1)[TX:2 * TX, :, NT], 0.0))
        step(pool.memset(valid[:].rearrange("p (k i) -> p k i", i=NT + 1)[2 * TX:P, :, NT], 0.0))
        step(pool.memset(no_reset[:, :, 0:1], 0.0))
        step(pool.memset(bad_row[:, 1, :], float(CAP - 1)))
        step(pool.memset(bad_row[TX:2 * TX, :, NT:NT + 1], float(FAR)))
        step(pool.memset(bad_row[2 * TX:P, :, NT:NT + 1], float(FAR)))
        step(pool.memset(empty_slots[:, :, 0:1], float(FAR)))
        pool.memset(xf[:, 0, 0:1], 0.0).then_inc(xf_stored, 16)
        pool.iota(token_id[:], [[P, NT + 1]], base=0, channel_multiplier=1,
                  allow_small_or_imprecise_dtypes=True).then_inc(const_ready, 1)
        for tab in (tab_first, tab_second):
            pool.dma_start(tab.rearrange("(p s) w -> p (s w)", p=SR),
                           empty_slots[0:SR, :, :].rearrange("p s w -> p (s w)")).then_inc(scattered, 16)

        for i in range(CC):
            pool.dma_start(sums[TOK + i * SR:TOK + (i + 1) * SR, :], zeros[0:SR, :]).then_inc(scattered, 16)

        def residual(b, waits):
            pool.wait_ge(h_ready, 4 * b + 4)
            pool.wait_ge(txt_loaded, 16 * b + 16)
            if waits:
                pool.wait_ge(xf_ready, UNITS * b)
                pool.wait_ge(out_stored, 16 * 3 * b)
            for t0, t1 in ((0, CT), (CT, NT)):
                bc = bo_rows[:].rearrange("p (a n) -> p a n", a=1).to_broadcast([P, t1 - t0, D])
                pool.tensor_tensor(h_out[:, t0:t1, :], h[:, t0:t1, :], bc, ALU.add).then_inc(base_ready, 1)
            pool.tensor_tensor(h_out[0:TX, NT, :], h[0:TX, NT, :], bo_rows[0:TX, :], ALU.add
                               ).then_inc(base_ready, 1)

        def scatter(b):
            ready = in_register(pool, pool_value, b + 1)
            pool.wait_ge(const_ready, 1)
            pool.wait_ge(slots_ready, ready)
            for t in range(NT + 1):
                for k, tab in enumerate((tab_first, tab_second)):
                    pool.indirect_dma_start(
                        tab, bass.IndirectOffsetOnAxis(slot_i[:, k, t:t + 1].bitcast(U32), 0),
                        entry[:, k, t, :], None, bounds_check=E * SL - 1, oob_is_err=False,
                    ).then_inc(scattered, 16)

        def sum_k(b, tiles):
            for i in tiles:
                r = P if i < NT else TX
                normed = (NT + 1) * b + i + 1
                if i == 0:
                    normed = in_register(pool, pool_value, normed)
                    pool.wait_ge(const_ready, 1)
                pool.wait_ge(qk_normed, normed)
                if i == 0:
                    pool.tensor_copy(k_sum[:], k_n[:, 0, :]).then_inc(k_summed, 1)
                else:
                    pool.wait_ge(k_summed, (NT + 1) * b + i)
                    pool.tensor_tensor(k_sum[0:r, :], k_sum[0:r, :], k_n[0:r, i, :], ALU.add
                                       ).then_inc(k_summed, 1)

        def body(b, lag):
            sum_k(b - 1, range(CT, NT + 1))
            if lag:
                scatter(b - 2)
            residual(b, True)
            pool.wait_ge(kv_done, b)
            sum_k(b, range(CT))

        pool.wait_ge(params_in, 16 * N_PARAM)
        residual(0, False)
        sum_k(0, range(CT))
        pool.wait_ge(scattered, 16 * EMPTYING)
        body(1, False)
        with pool.Fori(0, B - 2) as i:
            body(i + 2, True)
        sum_k(B - 1, range(CT, NT + 1))
        scatter(B - 2)
        scatter(B - 1)
        pool.wait_ge(scattered, 16 * (2 * (NT + 1) * B + EMPTYING))

    @block.scalar
    def _(act):
        act.wait_ge(setup_v, 3)
        act.activation(m_col[:], m_col[:], ACT.Exp, scale=-1.0).then_inc(setup_a, 1)
        act.wait_ge(setup_v, 5)
        act.activation(head_scale[:], head_scale[:], ACT.Exp, scale=-LOG_S).then_inc(setup_a, 1)

        def body(b, front, back, i):
            def root(n, c, measured, done, bb):
                tiles = slice(0, CT) if c == 0 else slice(CT, NT + 1)
                act.wait_ge(measured, 2 * bb + c + 1)
                act.activation(std[:, n, tiles], mean_var[:, n, tiles, 1], ACT.Sqrt, bias=eps[:, 0:1]).then_inc(done, 1)

            def center(n, c, src, dst, scaled, value, ready):
                act.wait_ge(scaled, value)
                for t in range(0, CT) if c == 0 else range(CT, NT + 1):
                    r = P if t < NT else TX
                    ins = act.activation(dst[0:r, t, :], src[0:r, t, :], ACT.Identity,
                                         bias=shift[0:r, n, t:t + 1], scale=rstd[0:r, n, t:t + 1])
                    if t % 2 == 1 or t == NT:
                        ins.then_inc(ready, 1)

            def x_blocks(*blocks):
                for g in blocks:
                    c = g // 8
                    act.wait_ge(x_turned, 16 * b + g + 1)
                    if g % 8 == 0 and back:
                        act.wait_ge(conv_done, 4 * (b - 1) + 2 * (c + 1))
                    act.copy(xT[c][:, g % 8, KC - 1:], ps_x[g % 2][:, 0:CW]).then_inc(xT_ready, 1)

            def conv_out(c, f):
                act.wait_ge(conv_done, 4 * b + 2 * c + f + 1)
                if f == 0 and back:
                    act.wait_ge(h_turned, 4 * (b - 1) + 2 * (c + 1))
                act.activation(hT[c][:, f, :], ps_conv[c][f][:, 0:CW], ACT.Identity, bias=h_bias[:, f:f + 1]
                               ).then_inc(hT_ready, 1)

            def from_turned(dst, u, turned, ready, bb, per=UNITS):
                act.wait_ge(turned, per * bb + u + 1)
                if u < UNITS - 1:
                    act.copy(dst[:, :, 2 * u * P:(2 * u + 2) * P],
                             t_bank(dst, u)[:, 0:4 * P].rearrange("p (f t) -> p f t", f=FB)).then_inc(ready, 1)
                else:
                    act.copy(dst[:, :, NT * P:NT * P + TX],
                             t_bank(dst, u)[:, 0:2 * TX].rearrange("p (f t) -> p f t", f=FB)).then_inc(ready, 1)

            if front:
                x_blocks(0, 1)
            if back:
                from_turned(qT, 2, q_turned, qT_ready, b - 1)
            if front:
                x_blocks(2, 3)
            if back:
                square(b - 1, 8)
                lengths(b - 1, 8)
                for u in (3, 4):
                    from_turned(qT, u, q_turned, qT_ready, b - 1)
                act.wait_ge(A_done, 2 * b)
                act.copy(A[:], ps_a[:].rearrange("p (f n) -> p f n", f=FB)).then_inc(A_ready, 1)
            if front:
                x_blocks(4, 5, 6, 7)
                conv_out(0, 0)
                x_blocks(8, 9, 10, 11)
                conv_out(0, 1)
                for u in (0, 1):
                    h_rows(act, b, u, back)
                x_blocks(12, 13)
                root(0, 0, h_measured, h_std, b)
                x_blocks(14, 15)
                conv_out(1, 0)
                conv_out(1, 1)
                for u in (0, 1):
                    from_turned(xlnT, u, xln_turned, xlnT_ready, b)
            if back:
                act.wait_ge(M_done, b)
                act.copy(M[:], ps_w[1][:].rearrange("p (f n) -> p f n", f=FB)).then_inc(M_ready, 1)
            if front:
                for u in (2, 3):
                    h_rows(act, b, u, back)
                root(0, 1, h_measured, h_std, b)
                square(b, 0)
                square(b, 1)
                lengths(b, 0)
                center(0, 1, h, xln, h_scale, b + 1, xln_ready)
                square(b, 2)
                lengths(b, 1)
                from_turned(xlnT, 2, xln_turned, xlnT_ready, b)
                square(b, 3)
                from_turned(xlnT, 3, xln_turned, xlnT_ready, b)
                lengths(b, 2)
                from_turned(xlnT, 4, xln_turned, xlnT_ready, b)
                lengths(b, 3)
            if back:
                root(1, 0, out_measured, out_std, b - 1)
                center(1, 0, h_out, xf, out_scale, 2 * (b - 1) + 1, xf_ready)
                root(1, 1, out_measured, out_std, b - 1)
                center(1, 1, h_out, xf, out_scale, 2 * (b - 1) + 2, xf_ready)
            if front:
                square(b, 4)
            if back:
                for u in (0, 1):
                    from_turned(xfT, u, xf_turned, xfT_ready, b - 1)
            if front:
                square(b, 5)
                lengths(b, 4)
            if back:
                for u in (2, 3):
                    from_turned(xfT, u, xf_turned, xfT_ready, b - 1)
            if front:
                square(b, 6)
            if back:
                from_turned(xfT, 4, xf_turned, xfT_ready, b - 1)
                act.wait_ge(gates_done, b)
                act.copy(lT[:, 0:2 * P], ps_c[:, 0:2 * P])
                act.copy(lT[0:TX, 2 * P:], ps_c[0:TX, 2 * P:2 * P + TX]).then_inc(gates_copied, 1)
            if front:
                lengths(b, 5)
                lengths(b, 6)
            if back:
                act.wait_ge(shifted, b)
                act.activation(ex[:], lg[:], ACT.Exp).then_inc(exp_done, 1)
            if front:
                square(b, 7)
                for u in (0, 1):
                    from_turned(qT, u, q_turned, qT_ready, b)
                lengths(b, 7)

        def h_rows(act, b, u, back):
            act.wait_ge(h_turned, 4 * b + u + 1)
            if u == 0 and back:
                act.wait_ge(base_ready, 3 * b)
            act.copy(h[:, 2 * u:2 * u + 2, :], ps_t[u % 2][:].rearrange("p (t n) -> p t n", t=2)).then_inc(h_ready, 1)

        def square(b, t):
            r = P if t < NT else TX
            act.wait_ge(qk_taken, (NT + 1) * b + t + 1)
            act.activation(qk_sq[0:r, t % 2, :], qk[0:r, t % 3, :], ACT.Square).then_inc(qk_squared, 1)

        def lengths(b, t):
            r = P if t < NT else TX
            act.wait_ge(qk_summed, (NT + 1) * b + t + 1)
            act.activation(qk_len[0:r, t % 3, :], qk_ss[0:r, t % 3, :], ACT.Sqrt).then_inc(qk_rooted, 1)

        loop(act, body)

    @block.vector
    def _(dve):
        dve_value = dve.alloc_register("dve_value")
        dve.wait_ge(const_ready, 1)
        dve.wait_ge(params_in, 16 * N_PARAM)
        dve.wait_ge(setup_mm, 3)
        dve.tensor_copy(read_col[:], ps[0][:, 0:1]).then_inc(setup_v, 1)
        dve.tensor_copy(conv_b_col[:], ps[0][:, 8:8 + CBS]).then_inc(setup_v, 1)
        dve.tensor_copy(m_col[:], ps[0][:, 16:16 + FB]).then_inc(setup_v, 1)
        dve.wait_ge(setup_a, 1)
        dve.tensor_scalar(m_col[:], m_col[:], 1.0, None, ALU.add).then_inc(setup_v, 1)
        dve.wait_ge(setup_v, 4)
        dve.reciprocal(head_scale[:], m_col[:]).then_inc(setup_v, 1)
        dve.tensor_copy(block_mask[:], ps[0][:, 128:256]).then_inc(setup_v, 1)
        dve.memset(wgT[:], 0.0).then_inc(setup_v, 1)
        dve.tensor_scalar(conv_b_col[:], conv_b_col[:], read_col[:, 0:1], None, ALU.mult).then_inc(setup_v, 1)
        dve.tensor_scalar(conv_col[:], conv_in[:], read_col[:, 0:1], None, ALU.mult).then_inc(setup_v, 1)
        dve.wait_ge(setup_v, 9)
        dve.tensor_copy(wgT[:, :, 0:E], ps[0][:, 32:32 + FB * E].rearrange("p (f e) -> p f e", f=FB)
                        ).then_inc(setup_v, 1)
        dve.tensor_tensor(
            conv_mat[:].rearrange("p b k d -> p (b k) d"),
            feat_of[:].rearrange("p (a d) -> p a d", a=1).to_broadcast([P, CBS * KC, 32]),
            conv_col[:].rearrange("p b (k a) -> p (b k) a", a=1).to_broadcast([P, CBS * KC, 32]),
            ALU.mult).then_inc(setup_v, 1)
        dve.wait_ge(setup_mm, 4)
        dve.tensor_copy(h_bias[:], ps[1][:, 0:FB]).then_inc(setup_v, 1)
        dve.memset(place[:], 0.0).then_inc(counts_taken, 1)
        dve.wait_ge(setup_a, 2)

        def body(b, front, back, it):
            steps = [0]

            def step(ins):
                steps[0] += 1
                ins.then_inc(v_step, 1)
                if not back:
                    return steps[0]
                return V_FRONT + V_BOTH * it + steps[0]

            def then(v):
                dve.wait_ge(v_step, v)

            def tiles_of(c):
                return range(0, CT) if c == 0 else range(CT, NT + 1)

            def measure(n, c, src, done):
                for t in tiles_of(c):
                    r = P if t < NT else TX
                    v = step(dve.bn_stats(stats[0:r, n, t, :], src[0:r, t, :]))
                v = in_register(dve, dve_value, v)
                dve.wait_ge(const_ready, 1)
                then(v)
                for t in tiles_of(c):
                    r = P if t < NT else TX
                    ins = dve.bn_aggr(mean_var[0:r, n, t, :], stats[0:r, n, t, :])
                ins.then_inc(done, 1)

            def center(n, c, bb, src, dst, std_done, ready):
                dve.wait_ge(std_done, 2 * bb + c + 1)
                tiles = tiles_of(c)
                cols = slice(tiles[0], tiles[-1] + 1)
                v = step(dve.reciprocal(rstd[:, n, cols], std[:, n, cols]))
                then(v)
                for t in tiles:
                    r = P if t < NT else TX
                    ins = dve.tensor_scalar(dst[0:r, t, :], src[0:r, t, :], mean_var[0:r, n, t, 0:1],
                                            rstd[0:r, n, t:t + 1], ALU.subtract, ALU.mult)
                    if t % 2 == 1 or t == NT:
                        ins.then_inc(ready, 1)

            def scale(n, c, bb, std_done, done):
                dve.wait_ge(std_done, 2 * bb + c + 1)
                cols = slice(tiles_of(c)[0], tiles_of(c)[-1] + 1)
                v = step(dve.reciprocal(rstd[:, n, cols], std[:, n, cols]))
                then(v)
                dve.scalar_tensor_tensor(out=shift[:, n, cols], in0=mean_var[:, n, cols, 0], scalar=-1.0,
                                         in1=rstd[:, n, cols], op0=ALU.mult, op1=ALU.mult).then_inc(done, 1)

            def measure_h(c):
                for u in ((0, 1) if c == 0 else (2, 3)):
                    dve.wait_ge(h_ready, 4 * b + u + 1)
                if c == 1:
                    dve.wait_ge(txt_loaded, 16 * b + 16)
                measure(0, c, h, h_measured)

            def center_h(c):
                if back:
                    dve.wait_ge(A_done, 2 * (b - 1) + c + 1)
                if c == 0:
                    center(0, c, b, h, xln, h_std, xln_ready)
                else:
                    scale(0, c, b, h_std, h_scale)

            def take_qk(t):
                r = P if t < NT else TX
                dve.wait_ge(qk_done, (NT + 1) * b + t + 1)
                if t >= 3 or back:
                    dve.wait_ge(qk_normed, (NT + 1) * b + t - 2)
                bank = ps_w[qk_bank(t)]
                dve.tensor_tensor(qk[0:r, t % 3, :], bank[0:r, :], bqk_rows[0:r, :], ALU.add).then_inc(qk_taken, 1)

            def sum_squares(t):
                r = P if t < NT else TX
                dve.wait_ge(qk_squared, (NT + 1) * b + t + 1)
                dve.tensor_reduce(qk_ss[0:r, t % 3, :], qk_sq[0:r, t % 2, :].rearrange("p (h d) -> p h d", d=HD),
                                  X, ALU.add).then_inc(qk_summed, 1)

            def norm_qk(t):
                r = P if t < NT else TX
                dve.wait_ge(qk_rooted, (NT + 1) * b + t + 1)
                v = step(dve.tensor_scalar(qk_inv[0:r, t % 3, :], qk_len[0:r, t % 3, :], 1e-12, None, ALU.max))
                then(v)
                v = step(dve.reciprocal(qk_inv[0:r, t % 3, :], qk_inv[0:r, t % 3, :]))
                then(v)
                if back and t in (0, CT):
                    dve.wait_ge(A_done, 2 * (b - 1) + (1 if t == 0 else 2))
                for lo, dst in ((0, q_n), (1, k_n)):
                    inv = qk_inv[0:r, t % 3, HEADS * lo:HEADS * lo + HEADS].rearrange("p (h a) -> p h a", a=1)
                    if lo == 1 and back:
                        dve.wait_ge(k_summed, (NT + 1) * (b - 1) + t + 1)
                    ins = dve.tensor_tensor(dst[0:r, t, :].rearrange("p (h d) -> p h d", d=HD),
                                            qk[0:r, t % 3, D * lo:D * lo + D].rearrange("p (h d) -> p h d", d=HD),
                                            inv.to_broadcast([r, HEADS, HD]), ALU.mult)
                ins.then_inc(qk_normed, 1)

            def out_rows(*pairs):
                bb = b - 1
                if pairs[0] == 0:
                    dve.wait_ge(base_ready, 3 * bb + 3)
                for u in pairs:
                    tiles = slice(2 * u, 2 * u + 2) if u < UNITS - 1 else slice(NT, NT + 1)
                    r, w = (P, 2 * D) if u < UNITS - 1 else (TX, D)
                    dve.wait_ge(out_done, UNITS * bb + u + 1)
                    dst = h_out[0:r, tiles, :].rearrange("p t n -> p (t n)")
                    dve.tensor_tensor(dst, ps_w[u % 2][0:r, 0:w], dst, ALU.add).then_inc(out_taken, 1)

            def measure_out(c):
                dve.wait_ge(out_taken, UNITS * (b - 1) + (2 if c == 0 else UNITS))
                measure(1, c, h_out, out_measured)

            def scale_out(c):
                if c == 0:
                    dve.wait_ge(xf_stored, 16 * 3 * (b - 1) + 16)
                scale(1, c, b - 1, out_std, out_scale)

            def kv_out():
                dve.wait_ge(kv_done, b)
                for f in range(FB):
                    ins = dve.scalar_tensor_tensor(out=kvT[:, f, :], in0=ps_w[0][:, f * P:(f + 1) * P],
                                                   scalar=head_scale[:, f:f + 1], in1=block_mask[:],
                                                   op0=ALU.mult, op1=ALU.mult)
                ins.then_inc(kv_ready, 1)

            W = NT + 1

            def wide(t):
                return t.rearrange("p (i a) -> p i a", a=1).to_broadcast([P, W, E])

            def take_logits():
                dve.wait_ge(logits_done, b)
                dve.tensor_copy(
                    lg[:, 0:NT, :].rearrange("p (u q) e -> p u q e", q=2),
                    ps_c[:, 0:2 * P].rearrange("p (q u z) -> p u q z", q=2, z=32)[:, :, :, 0:E])
                v = step(dve.tensor_copy(lg[0:TX, NT, :], ps_c[0:TX, 2 * P:2 * P + E]))
                then(v)
                v = step(dve.tensor_reduce(top[:], lg[:], X, ALU.max))
                then(v)
                dve.tensor_tensor(lg[:], lg[:], wide(top[:]), ALU.subtract).then_inc(shifted, 1)

            def weights():
                dve.wait_ge(exp_done, b)
                v = step(dve.tensor_reduce(den[:], ex[:], X, ALU.add))
                then(v)
                v = step(dve.reciprocal(top[:], den[:]))
                then(v)
                return step(dve.tensor_tensor(gate[:], ex[:], wide(top[:]), ALU.mult))

            def choose(k, v):
                then(v)
                v = step(dve.tensor_reduce(best[:, k, :], gate[:], X, ALU.max))
                then(v)
                v = step(dve.tensor_tensor(same[:], gate[:], wide(best[:, k, :]), ALU.is_equal))
                then(v)
                v = step(dve.tensor_tensor(same[:], same[:], rank[:], ALU.mult))
                then(v)
                v = step(dve.tensor_reduce(chosen_rank[:, k, :], same[:], X, ALU.max))
                then(v)
                v = step(dve.tensor_tensor(hot[:, k, :, :].rearrange("p e i -> p i e"), same[:],
                                           wide(chosen_rank[:, k, :]), ALU.is_equal))
                then(v)
                if k == 0:
                    return step(dve.scalar_tensor_tensor(out=gate[:], in0=hot[:, 0, :, :].rearrange("p e i -> p i e"),
                                                         scalar=-4.0, in1=gate[:], op0=ALU.mult, op1=ALU.add))
                dve.tensor_tensor(hot_bf[:], hot[:].rearrange("p k e i -> p (k e i)"), valid[:], ALU.mult
                                  ).then_inc(hot_ready, 1)

            def places():
                n = 2 * E * W
                dve.wait_ge(counts_done, b)
                v = step(dve.tensor_copy(runs[:, :, 1:], ps_c[:, n:2 * n].rearrange("p (k i) -> p k i", i=W)))
                then(v)
                v = step(dve.tensor_tensor_scan(ahead[:].rearrange("p k i -> p (k i)"),
                                                no_reset[:].rearrange("p k i -> p (k i)"),
                                                runs[:].rearrange("p k i -> p (k i)"), 0.0, ALU.mult, ALU.add))
                then(v)
                v = dve.tensor_tensor(place[:], ps_c[:, 0:n].rearrange("p (k i) -> p k i", i=W),
                                      ahead[:, :, 0:W], ALU.add)
                v.then_inc(counts_taken, 1)

            def slots():
                step(dve.tensor_copy(runs[:, :, 0:1], ahead[:, :, W:W + 1]))
                dve.wait_ge(counts_taken, b + 1)
                v = step(dve.tensor_tensor(place[:].rearrange("p k i -> p (k i)"), place[:].rearrange("p k i -> p (k i)"),
                                           hot_bf[:], ALU.mult))
                then(v)
                v = step(dve.tensor_reduce(count[:], place[:].rearrange("p (k e) i -> p k i e", k=2), X, ALU.add))
                then(v)
                v = step(dve.tensor_scalar(slot[:], count[:], float(CAP), float(FAR), ALU.is_ge, ALU.mult))
                then(v)
                v = step(dve.tensor_tensor(slot[:], slot[:], bad_row[:], ALU.add))
                v = step(dve.tensor_scalar(chosen_rank[:], chosen_rank[:], -float(SL), float(E * SL), ALU.mult, ALU.add))
                then(v)
                v = step(dve.tensor_tensor(slot[:], slot[:], chosen_rank[:], ALU.add))
                then(v)
                dve.wait_ge(scattered, 16 * (2 * W * (b - 1) + EMPTYING))
                v = step(dve.tensor_tensor(slot_i[:, 0, :], slot[:, 0, :], count[:, 0, :], ALU.add))
                v = step(dve.tensor_tensor(slot_i[:, 1, :], slot[:, 1, :], count[:, 1, :], ALU.subtract))
                for k in range(2):
                    step(dve.tensor_copy(entry[:, k, :, 0], token_id[:]))
                v = step(dve.tensor_copy(entry[:, :, :, 1], best[:]))
                then(v)
                dve.tensor_scalar(token_id[:], token_id[:], float(S), None, ALU.add).then_inc(slots_ready, 1)

            if front:
                dve.wait_ge(xT_ready, 16 * b + 8)
                if back:
                    dve.wait_ge(conv_done, 4 * b)
                dve.tensor_copy(xT[1][:, :, 0:KC - 1], xT[0][:, :, CW:CW + KC - 1]).then_inc(halo_ready, 1)
            if back:
                kv_out()
            if front:
                measure_h(0)
                center_h(0)
                measure_h(1)
                take_qk(0)
                take_qk(1)
                sum_squares(0)
                center_h(1)
                take_qk(2)
                sum_squares(1)
                norm_qk(0)
                take_qk(3)
                sum_squares(2)
                norm_qk(1)
            if back:
                out_rows(0)
            if front:
                sum_squares(3)
            if back:
                out_rows(1)
            if front:
                norm_qk(2)
            if back:
                measure_out(0)
                out_rows(2)
            if front:
                norm_qk(3)
            if back:
                scale_out(0)
                out_rows(3, 4)
                measure_out(1)
            if front:
                take_qk(4)
            if back:
                scale_out(1)
            if front:
                take_qk(5)
                sum_squares(4)
                take_qk(6)
                sum_squares(5)
                norm_qk(4)
                sum_squares(6)
            if back:
                take_logits()
            if front:
                take_qk(7)
                norm_qk(5)
            if back:
                v = weights()
                v = choose(0, v)
                choose(1, v)
            if front:
                sum_squares(7)
                norm_qk(6)
                norm_qk(7)
                take_qk(8)
            if back:
                places()
            if front:
                sum_squares(8)
                norm_qk(8)
            if back:
                slots()
            want = V_BOTH if front and back else V_FRONT if front else V_BACK
            assert steps[0] == want, (front, back, steps[0])

        loop(dve, body)
        dve.wait_ge(slots_ready, B)
        dve.tensor_copy(taken[:], runs[:, 0:E, 0])

    @block.tensor
    def _(pe):
        pe_value, normed_value = pe.alloc_register("pe_value"), pe.alloc_register("pe_normed_value")
        pe.wait_ge(const_ready, 1)
        pe.wait_ge(params_in, 16 * N_PARAM)
        pe.matmul(ps[0][:, 0:1], value_of[:], read_in[:], start=True, stop=True)
        pe.transpose(ps[0][:, 8:8 + CBS], conv_b_in[:], ident[0:CBS, 0:CBS]).then_inc(setup_mm, 1)
        for f in range(FB):
            pe.matmul(ps[0][:, 16 + f:17 + f], head_of[:, f * P:(f + 1) * P], m_in[:], start=True, stop=True)
        pe.matmul(ps[0][:, 128:256], head_of[:, 0:P], head_of[:, 0:P], start=True, stop=True).then_inc(setup_mm, 1)
        for f in range(FB):
            ins = pe.transpose(ps[0][:, 32 + f * E:32 + (f + 1) * E], wg_in[:, f * P:(f + 1) * P], ident[0:E, 0:E])
        ins.then_inc(setup_mm, 1)
        pe.wait_ge(setup_v, 8)
        for cb in range(CBS):
            q = cb % 4
            ins = pe.matmul(ps[1][32 * q:32 * q + 32, cb // 4:cb // 4 + 1], feat_of[:], conv_b_col[:, cb:cb + 1],
                            start=True, stop=True, skip_group_check=True)
        ins.then_inc(setup_mm, 1)
        pe.wait_ge(setup_v, 12)
        pe.wait_ge(setup_a, 2)

        def body(b, front, back, it):
            W = NT + 1

            def turn_x(g):
                c = g // 8
                if g % 8 == 0:
                    pe.wait_ge(x_loaded[c], 16 * b + 16)
                if g >= 2 or back:
                    pe.wait_ge(xT_ready, 16 * b + g - 1)
                for i in range(CT):
                    ins = pe.transpose(ps_x[g % 2][:, i * P:(i + 1) * P],
                                       x_in[:, CT * c + i, (g % 8) * P:(g % 8 + 1) * P], ident[:])
                ins.then_inc(x_turned, 1)

            def taps(c, f, between):
                pe.wait_ge(xT_ready, 16 * b + 8 * c + 4 * (f + 1))
                if (c, f) == (0, 0):
                    if back:
                        pe.wait_ge(counts_taken, b)
                elif (c, f) == (0, 1):
                    if back:
                        pe.wait_ge(qk_taken, W * b)
                elif (c, f) == (1, 0):
                    pe.wait_ge(hT_ready, 4 * b + 1)
                    pe.wait_ge(halo_ready, b + 1)
                elif back:
                    pe.wait_ge(kv_ready, b)
                for k in range(KC):
                    for q in range(4):
                        cb = 4 * f + q
                        ins = pe.matmul(ps_conv[c][f][32 * q:32 * q + 32, 0:CW], conv_mat[:, cb, k, :],
                                        xT[c][:, cb, k:k + CW], start=(k == 0), stop=(k == KC - 1),
                                        skip_group_check=True)
                    for g in between[k] if between else ():
                        turn_x(g)
                ins.then_inc(conv_done, 1)

            def turn_pair(src, dst, u, turned, feature_rows=False):
                bank = t_bank(dst, u)
                if u < UNITS - 1:
                    for f in range(FB):
                        for t in range(2):
                            ins = pe.transpose(bank[:, (2 * f + t) * P:(2 * f + t + 1) * P],
                                               src[:, 2 * u + t, f * P:(f + 1) * P], ident[:])
                else:
                    for f in range(FB):
                        ins = pe.transpose(bank[:, f * TX:(f + 1) * TX], src[0:TX, NT, f * P:(f + 1) * P],
                                           ident[0:TX, 0:TX])
                ins.then_inc(turned, 1)

            def turn_q(bb, u, free):
                for s, v in free:
                    pe.wait_ge(s, v)
                normed = W * bb + (2 * u + 2 if u < UNITS - 1 else W)
                if u == UNITS - 1:
                    normed = in_register(pe, pe_value, normed)
                    pe.wait_ge(const_ready, 1)
                pe.wait_ge(qk_normed, normed)
                turn_pair(q_n, qT, u, q_turned)

            def add_A(bb, tiles, first, last):
                for t in tiles:
                    r = P if t < NT else TX
                    for f in range(FB):
                        ins = pe.matmul(ps_a[:, f * D:(f + 1) * D], xln[0:r, t, f * P:(f + 1) * P], k_n[0:r, t, :],
                                        start=(first and t == 0 and f == 0), stop=bool(last) and t == NT,
                                        skip_group_check=True)
                if last is not None:
                    ins.then_inc(A_done, 1)

            def turn_h(u):
                pe.wait_ge(hT_ready, 4 * b + 2 * (u // 2) + 2)
                if back and u < 2:
                    pe.wait_ge(qT_ready, UNITS * (b - 1) + 4 + u)
                if u >= 2:
                    pe.wait_ge(xlnT_ready, UNITS * b + u - 1)
                c, bank = u // 2, ps_t[u % 2]
                for t in range(2):
                    for f in range(FB):
                        col = (2 * (u % 2) + t) * P
                        ins = pe.transpose(bank[:, t * D + f * P:t * D + (f + 1) * P], hT[c][:, f, col:col + P], ident[:])
                ins.then_inc(h_turned, 1)

            def turn_xln(u):
                normed = UNITS * b + u + 1
                if u == UNITS - 1:
                    normed = in_register(pe, normed_value, normed)
                    copied = in_register(pe, pe_value, UNITS * b + 3)
                    pe.wait_ge(const_ready, 1)
                pe.wait_ge(xln_ready, normed)
                if u < 4:
                    pe.wait_ge(h_ready, 4 * b + u + 1)
                else:
                    pe.wait_ge(xlnT_ready, copied)
                turn_pair(xln, xlnT, u, xln_turned)

            def qk_tile(t):
                r = P if t < NT else TX
                pe.wait_ge(xlnT_ready, UNITS * b + t // 2 + 1)
                if t == 0:
                    pe.wait_ge(hT_ready, 4 * b + 4)
                elif t == 1:
                    if back:
                        pe.wait_ge(M_ready, b)
                elif t < CT:
                    pe.wait_ge(qk_taken, W * b + t - 1)
                elif t == 4 or t == 5:
                    if back:
                        pe.wait_ge(out_taken, UNITS * b - 5 + t)
                    else:
                        pe.wait_ge(qk_taken, W * b + (4 if t == 4 else 3))
                else:
                    pe.wait_ge(qk_taken, W * b + t - 1)
                for f in range(FB):
                    ins = pe.matmul(ps_w[qk_bank(t)][0:r, :], xlnT[:, f, t * P:t * P + r], wqk[:, f, :],
                                    start=(f == 0), stop=(f == FB - 1))
                ins.then_inc(qk_done, 1)

            def kv():
                pe.wait_ge(A_ready, b)
                pe.wait_ge(k_summed, W * b)
                pe.wait_ge(qk_taken, W * b - 1)
                for v in range(FB):
                    cols = slice(v * P, (v + 1) * P)
                    for f in range(FB):
                        pe.matmul(ps_w[0][:, cols], wv[:, f, cols], A[:, f, cols], start=(f == 0), stop=False)
                    ins = pe.matmul(ps_w[0][:, cols], bv_rows[:, cols], k_sum[:, cols], start=False, stop=True)
                ins.then_inc(kv_done, 1)

            def fold():
                pe.wait_ge(kv_ready, b)
                if front:
                    pe.wait_ge(hT_ready, 4 * b + 2)
                else:
                    pe.wait_ge(qk_taken, W * b)
                for f in range(FB):
                    ins = pe.matmul(ps_w[1][:, f * D:(f + 1) * D], kvT[:, f, :], wo[:, f, :], start=True, stop=True)
                ins.then_inc(M_done, 1)

            def attend(u):
                bb = b - 1
                if u == 0:
                    pe.wait_ge(M_ready, b)
                pe.wait_ge(qT_ready, UNITS * bb + u + 1)
                if u < 2:
                    if front:
                        pe.wait_ge(qk_taken, W * b + 3 + u)
                else:
                    pe.wait_ge(out_taken, UNITS * bb + u - 1)
                for t in ((2 * u, 2 * u + 1) if u < UNITS - 1 else (NT,)):
                    r = P if t < NT else TX
                    for f in range(FB):
                        ins = pe.matmul(ps_w[u % 2][0:r, (t % 2) * D:(t % 2 + 1) * D], qT[:, f, t * P:t * P + r],
                                        M[:, f, :], start=(f == 0), stop=(f == FB - 1))
                ins.then_inc(out_done, 1)

            def turn_xf(u):
                bb = b - 1
                normed, copied = UNITS * bb + u + 1, UNITS * bb + u - 1
                if u == UNITS - 1:
                    normed = in_register(pe, normed_value, normed)
                    copied = in_register(pe, pe_value, copied)
                    pe.wait_ge(const_ready, 1)
                pe.wait_ge(xf_ready, normed)
                if u < 2:
                    if front:
                        pe.wait_ge(xlnT_ready, UNITS * b + 4 + u)
                else:
                    pe.wait_ge(xfT_ready, copied)
                turn_pair(xf, xfT, u, xf_turned)

            def gates():
                bb = b - 1
                pe.wait_ge(xfT_ready, UNITS * bb + UNITS)
                for f in range(FB):
                    for u in range(UNITS - 1):
                        pe.matmul(ps_c[32 * u:32 * u + 32, 0:2 * P], wgT[:, f, :], xfT[:, f, 2 * u * P:(2 * u + 2) * P],
                                  start=(f == 0), stop=(f == FB - 1), skip_group_check=True)
                for f in range(FB):
                    ins = pe.matmul(ps_c[0:32, 2 * P:2 * P + TX], wgT[:, f, :], xfT[:, f, NT * P:NT * P + TX],
                                    start=(f == 0), stop=(f == FB - 1), skip_group_check=True)
                ins.then_inc(gates_done, 1)

            def turn_gates():
                pe.wait_ge(gates_copied, b)
                for q in range(2):
                    pe.transpose(ps_c[:, q * P:(q + 1) * P], lT[:, q * P:(q + 1) * P], ident[:])
                pe.transpose(ps_c[0:TX, 2 * P:2 * P + TX], lT[0:TX, 2 * P:], ident[0:TX, 0:TX]).then_inc(logits_done, 1)

            def counts():
                n = 2 * E * W
                pe.wait_ge(hot_ready, b)
                pe.matmul(ps_c[:, 0:n], before_bf[:], hot_bf[:], start=True, stop=True)
                pe.matmul(ps_c[:, n:2 * n], ones_bf[:], hot_bf[:], start=True, stop=True).then_inc(counts_done, 1)

            if front:
                turn_x(0)
                turn_x(1)
            if back:
                turn_q(b - 1, 2, [(qT_ready, UNITS * (b - 1) + 2)])
            if front:
                turn_x(2)
                turn_x(3)
            if back:
                turn_q(b - 1, 3, [])
                add_A(b - 1, range(CT, NT), False, None)
                turn_q(b - 1, 4, [(qT_ready, UNITS * (b - 1) + 3)])
                add_A(b - 1, (NT,), False, True)
            if front:
                taps(0, 0, ((4, 5), (6,), (7,), ()))
                taps(0, 1, ((8, 9), (10,), (11,), ()))
            if back:
                kv()
            if front:
                turn_h(0)
                turn_h(1)
                taps(1, 0, ((12, 13), (14,), (15,), ()))
                taps(1, 1, ())
                turn_xln(0)
                turn_xln(1)
            if back:
                fold()
            if front:
                turn_h(2)
                turn_h(3)
                for t in range(CT):
                    qk_tile(t)
                turn_xln(2)
                turn_xln(3)
            if back:
                attend(0)
            if front:
                turn_xln(4)
            if back:
                for u in range(1, UNITS):
                    attend(u)
            if front:
                qk_tile(4)
            if back:
                turn_xf(0)
                turn_xf(1)
            if front:
                qk_tile(5)
            if back:
                turn_xf(2)
                turn_xf(3)
            if front:
                qk_tile(6)
            if back:
                turn_xf(4)
                gates()
            if front:
                qk_tile(7)
            if back:
                turn_gates()
            if front:
                if back:
                    turn_q(b, 0, [(xfT_ready, UNITS * b - 1)])
                    turn_q(b, 1, [(xfT_ready, UNITS * b)])
                    pe.wait_ge(A_ready, b)
                else:
                    turn_q(b, 0, [(xlnT_ready, UNITS * b + UNITS)])
                    turn_q(b, 1, [(xlnT_ready, UNITS * b + 4)])
                add_A(b, range(CT), True, False)
                qk_tile(8)
            if back:
                counts()

        loop(pe, body)


LOG_S = 6.962243464266207
V_FRONT, V_BOTH, V_BACK = 29, 70, 41


def stage_two(nc, ctx, dram, keep):
    W1, b1, W2, b2, sums = (dram[n] for n in ("W1", "b1", "W2", "b2", "sums"))
    rows, tab_first, tab_second = dram["rows"], dram["tab_first"], dram["tab_second"]
    ident, taken = keep["ident"], keep["taken"]

    def sb(name, shape, dt=F32):
        return ctx.enter_context(nc.sbuf_tensor(name, shape, dt))

    def sem(name):
        return ctx.enter_context(nc.semaphore(name))

    first = sb("first", [SR, E, ST, 2])
    second = sb("second", [SR, E, ST, 2])
    slot_no = sb("slot_no", [SR, ST])
    is_first = sb("is_first", [SR, E, ST], I32)
    near = sb("near", [SR, E * ST])
    spare = sb("spare", [SR, E * NCH, CC])
    plan = sb("plan", [SR, E * NCH, 3, CC], I32)
    take = sb("take", [SR, CC], I32)
    give = sb("give", [SR, 2, CC], I32)
    w1_in, w2_in = (keep["x_in"][:].rearrange("p i n -> p (i n)")[:, at:at + n * w].rearrange("p (b n) -> p b n", b=n)
                    for at, n, w in W_AT)
    w1_hi, w1_lo = (sb(f"w1_{n}", [P, FB, H], F32R) for n in ("hi", "lo"))
    w2_hi, w2_lo = (sb(f"w2_{n}", [P, MB, D], F32R) for n in ("hi", "lo"))
    b1_col, b1_next = sb("b1_col", [P, MB]), sb("b1_next", [P, MB])
    b2_col = sb("b2_col", [P, FB])
    xg = sb("xg", [SR, CC, D])
    x_hi, x_lo = (sb(f"x_{n}", [P, FB, N2], F32R) for n in ("hi", "lo"))
    g = sb("g", [P, 4, N2])
    g_hi, g_lo = (sb(f"g_{n}", [P, MB, N2], F32R) for n in ("hi", "lo"))
    yT = sb("yT", [P, FB, N2])
    y = sb("y", [SR, CC, D])
    y_last = sb("y_last", [SR, NCH, CC, D])

    ps = [ctx.enter_context(nc.psum_tensor(f"qs{i}", [P, 512], F32)) for i in range(8)]
    ps_h, ps_y, ps_x, ps_r = ps[0:3], ps[3:5], ps[5:7], ps[7]

    tables_in = sem("tables_in")
    t_step = sem("t_step")
    slots_no = sem("slots_no")
    plan_ready = sem("plan_ready")
    take_loaded = sem("take_loaded")
    give_loaded = sem("give_loaded")
    w1_loaded, w2_loaded = keep["w1_loaded"], keep["w2_loaded"]
    b1_loaded = sem("b1_loaded")
    b1_taken = sem("b1_taken")
    b2_loaded = sem("b2_loaded")
    w1_high = sem("w1_high")
    w2_high = sem("w2_high")
    w1_split = sem("w1_split")
    w2_split = sem("w2_split")
    gathered = sem("gathered")
    x_turned = sem("x_turned2")
    x_halves = sem("x_halves")
    x_split = sem("x_split")
    h_done = sem("h_done")
    gelu_done = sem("gelu_done")
    g_high = sem("g_high")
    g_split = sem("g_split")
    y_done = sem("y_done")
    yT_ready = sem("yT_ready")
    y_turned = sem("y_turned")
    y_ready = sem("y_ready")
    added = sem("added")
    based = [sem(f"based{j}") for j in range(NCH)]
    copied = sem("copied")
    placed = sem("placed")
    NG = E * NCH
    LAST = NG - NCH

    block = ctx.enter_context(nc.Block())

    @block.sync
    def _(sp):
        def load_w1(e):
            sp.wait_ge(w1_split, MB * e)
            sp.dma_start(w1_in, W1[bass.ds(e, 1), :, :].rearrange("a (b p) n -> p (a b) n", p=P)
                         ).then_inc(w1_loaded, 16)

        def load_w2(e):
            sp.wait_ge(w2_split, MB * e)
            sp.dma_start(w2_in, W2[bass.ds(e, 1), :, :].rearrange("a (b p) n -> p (a b) n", p=P)
                         ).then_inc(w2_loaded, 16)

        def load_b1(e):
            sp.dma_start(b1_next[:], b1[bass.ds(e, 1), :].rearrange("a (m p) -> p (a m)", p=P),
                         allow_slow_non_contiguous=True).then_inc(b1_loaded, 16)

        def load_b2(e):
            sp.dma_start(b2_col[:], b2[bass.ds(e, 1), :].rearrange("a (m p) -> p (a m)", p=P),
                         allow_slow_non_contiguous=True).then_inc(b2_loaded, 16)

        def load_take(c):
            sp.dma_start(take[:], plan[:, bass.ds(c, 1), 0, :].rearrange("p a i -> p (a i)")
                         ).then_inc(take_loaded, 16)

        def load_give(c, first):
            if not first:
                sp.wait_ge(added, 64 * c)
            sp.dma_start(give[:], plan[:, bass.ds(c, 1), 1:3, :].rearrange("p a k i -> p (a k) i")
                         ).then_inc(give_loaded, 16)

        def copy_sums(batches, done):
            for n, b in enumerate(batches):
                sp.wait_ge(h_done, done + 3 * n + 1)
                sp.dma_start(dram["out"][b, :, :], sums[b * S:(b + 1) * S, :]).then_inc(copied, 16)

        def expert(e, first=False, last=False):
            if not last:
                load_w1(e + 1)
                sp.wait_ge(b1_taken, e + 1)
                load_b1(e + 1)
            for j in range(NCH):
                c = NCH * e + j
                if not (last and j == NCH - 1):
                    sp.wait_ge(gathered, 64 * (c + 1))
                    load_take(c + 1)
                if j == 0:
                    if not first:
                        sp.wait_ge(yT_ready, c)
                    load_b2(e)
                if not last:
                    load_give(c, first and j == 0)
                elif j == 0:
                    sp.wait_ge(added, 64 * LAST)
                elif j == 2:
                    copy_sums((0, 1), MB * (LAST + 1))
                elif j == 3:
                    copy_sums((2, 3, 4), MB * (LAST + 2))
                    copy_sums((5, 6, 7), MB * (LAST + 3))
                if j == 1 and not last:
                    load_w2(e + 1)

        for tab, dst in ((tab_first, first), (tab_second, second)):
            sp.dma_start(dst[:].rearrange("p e i w -> p e (i w)"),
                         tab.rearrange("(e p i) w -> p e (i w)", e=E, p=SR)).then_inc(tables_in, 16)
        load_b1(0)
        sp.wait_ge(plan_ready, 1)
        load_take(0)
        expert(0, first=True)
        with sp.Fori(1, E - 1) as e:
            expert(e)
        expert(E - 1, last=True)
        sp.wait_ge(copied, 16 * B)

    @block.gpsimd
    def _(pool):
        loaded_value, weighed_value, before_value = (
            pool.alloc_register(f"{n}_value") for n in ("loaded", "weighed", "before"))
        pool.iota(slot_no[:], [[1, ST]], base=0, channel_multiplier=ST,
                  allow_small_or_imprecise_dtypes=True).then_inc(slots_no, 1)
        pool.iota(spare[:], [[0, E * NCH], [SR, CC]], base=TOK, channel_multiplier=1,
                  allow_small_or_imprecise_dtypes=True).then_inc(slots_no, 1)

        def gather(c):
            loaded = in_register(pool, loaded_value, 16 * (c + 1))
            pool.wait_ge(slots_no, 1)
            pool.wait_ge(take_loaded, loaded)
            for i in range(CC):
                pool.indirect_dma_start(xg[:, i, :], None, rows,
                                        bass.IndirectOffsetOnAxis(take[:, i:i + 1].bitcast(U32), 0)
                                        ).then_inc(gathered, 16)

        def add(c):
            loaded = in_register(pool, loaded_value, 16 * (c + 1))
            weighed = in_register(pool, weighed_value, 2 * (c + 1))
            before = in_register(pool, before_value, 64 * c)
            pool.wait_ge(slots_no, 1)
            pool.wait_ge(give_loaded, loaded)
            pool.wait_ge(y_ready, weighed)
            if not (isinstance(c, int) and c == 0):
                pool.wait_ge(added, before)
            for i in range(CC):
                pool.indirect_dma_start(sums, bass.IndirectOffsetOnAxis(give[:, 0, i:i + 1].bitcast(U32), 0),
                                        y[:, i, :], None, compute_op=ALU.add).then_inc(added, 16)

        def gather_sums(j):
            for i in range(CC):
                pool.indirect_dma_start(y_last[:, j, i, :], None, sums,
                                        bass.IndirectOffsetOnAxis(plan[:, LAST + j, 0, i:i + 1].bitcast(U32), 0)
                                        ).then_inc(based[j], 16)

        def place(j):
            pool.wait_ge(y_ready, 2 * (LAST + j + 1))
            for i in range(CC):
                pool.indirect_dma_start(dram["out_rows"],
                                        bass.IndirectOffsetOnAxis(plan[:, LAST + j, 1, i:i + 1].bitcast(U32), 0),
                                        y_last[:, j, i, :], None, bounds_check=TOK - 1, oob_is_err=False
                                        ).then_inc(placed, 16)

        def gather_next(c):
            pool.wait_ge(x_turned, 2 * (c + 1))
            gather(c + 1)

        gather(0)
        gather_next(0)
        gather_next(1)
        add(0)
        with pool.Fori(2, LAST + 1) as c:
            gather_next(c)
            add(c - 1)
        pool.wait_ge(added, 64 * LAST)
        gather_sums(0)
        for j in range(1, NCH):
            if j < NCH - 1:
                gather_next(LAST + j)
            gather_sums(j)
        pool.wait_ge(copied, 16 * B)
        for j in range(NCH):
            place(j)
        pool.wait_ge(placed, 64 * NCH)

    @block.scalar
    def _(act):
        def body(c, first):
            for m in range(MB):
                act.wait_ge(h_done, MB * c + m + 1)
                if not (first and m < 4):
                    act.wait_ge(g_split, MB * c + m - 3)
                act.activation(g[:, m % 4, :], ps_h[m % 3][:, 0:N2], ACT.Gelu, bias=b1_col[:, m:m + 1]
                               ).then_inc(gelu_done, 1)
            act.wait_ge(y_done, c + 1)
            if not first:
                act.wait_ge(y_turned, 2 * c)
            for f in range(FB):
                ins = act.activation(yT[:, f, :], ps_y[f][:, 0:N2], ACT.Identity, bias=b2_col[:, f:f + 1])
            ins.then_inc(yT_ready, 1)

        body(0, True)
        with act.Fori(1, NG) as c:
            body(c, False)

    @block.vector
    def _(dve):
        dve.wait_ge(slots_no, 2)
        dve.tensor_tensor(is_first[:],
                          slot_no[:].rearrange("p (a i) -> p a i", a=1).to_broadcast([SR, E, ST]),
                          taken[0:SR, :].rearrange("p (e a) -> p e a", a=1).to_broadcast([SR, E, ST]),
                          ALU.is_lt).then_inc(t_step, 1)
        dve.wait_ge(t_step, 1)
        dve.wait_ge(tables_in, 32)
        for w in range(2):
            dve.copy_predicated(second[:, :, :, w], is_first[:], first[:, :, :, w]).then_inc(t_step, 1)
        dve.wait_ge(t_step, 3)
        dve.tensor_scalar(near[:], second[:, :, :, 0].rearrange("p e i -> p (e i)"), float(TOK - 1), None, ALU.min
                          ).then_inc(t_step, 1)
        chunks = second[:].rearrange("p e (c q) w -> p (e c) q w", q=CC)
        dve.tensor_tensor(plan[:, :, 1, :], chunks[:, :, :, 0], spare[:], ALU.min).then_inc(t_step, 1)
        dve.tensor_copy(plan[:, :, 2, :].bitcast(F32), chunks[:, :, :, 1]).then_inc(t_step, 1)
        dve.wait_ge(t_step, 6)
        dve.tensor_copy(plan[:, :, 0, :], near[:].rearrange("p (c q) -> p c q", q=CC)).then_inc(plan_ready, 1)

        def split_w1(e, m):
            cols = slice(m * P, (m + 1) * P)
            if m == 0:
                dve.wait_ge(w1_loaded, 16 * (e + 1))
            dve.tensor_copy(w1_hi[:, :, cols], w1_in[:, :, cols]).then_inc(w1_high, 1)
            dve.wait_ge(w1_high, MB * e + m + 1)
            dve.tensor_tensor(w1_lo[:, :, cols], w1_in[:, :, cols], w1_hi[:, :, cols].bitcast(F32), ALU.subtract
                              ).then_inc(w1_split, 1)

        def split_w2(e, m):
            if m == 0:
                dve.wait_ge(w2_loaded, 16 * (e + 1))
            dve.tensor_copy(w2_hi[:, m, :], w2_in[:, m, :]).then_inc(w2_high, 1)
            dve.wait_ge(w2_high, MB * e + m + 1)
            dve.tensor_tensor(w2_lo[:, m, :], w2_in[:, m, :], w2_hi[:, m, :].bitcast(F32), ALU.subtract
                              ).then_inc(w2_split, 1)

        def take_b1(e):
            dve.wait_ge(b1_loaded, 16 * (e + 1))
            dve.tensor_copy(b1_col[:], b1_next[:]).then_inc(b1_taken, 1)

        def split_x(c):
            for f in range(FB):
                dve.wait_ge(x_turned, 2 * c + f + 1)
                dve.tensor_copy(x_hi[:, f, :], ps_x[f][:, 0:N2]).then_inc(x_halves, 1)
            dve.wait_ge(x_halves, 2 * c + 2)
            for f in range(FB):
                ins = dve.tensor_tensor(x_lo[:, f, :], ps_x[f][:, 0:N2], x_hi[:, f, :].bitcast(F32), ALU.subtract)
            ins.then_inc(x_split, 1)

        def weigh(c, half):
            last = isinstance(c, int) and c >= LAST
            dve.wait_ge(y_turned, 2 * c + half + 1)
            if last:
                dve.wait_ge(based[c - LAST], 64)
            elif half == 0:
                dve.wait_ge(give_loaded, 16 * (c + 1))
                if not (isinstance(c, int) and c == 0):
                    dve.wait_ge(added, 64 * c)
            for i in (0, 1):
                t = 2 * half + i
                rows_in = ps_r[0:SR, i * D:(i + 1) * D]
                if last:
                    dst = y_last[:, c - LAST, t, :]
                    ins = dve.scalar_tensor_tensor(out=dst, in0=rows_in, scalar=plan[:, c, 2, t:t + 1].bitcast(F32),
                                                   in1=dst, op0=ALU.mult, op1=ALU.add)
                else:
                    ins = dve.tensor_scalar(y[:, t, :], rows_in, give[:, 1, t:t + 1].bitcast(F32), None, ALU.mult)
            ins.then_inc(y_ready, 1)

        def chunk(c, e, start=False, end=False, first=False, last=False):
            if not first:
                dve.wait_ge(y_done, c)
            for m in range(MB):
                if start:
                    split_w2(e, m)
                dve.wait_ge(gelu_done, MB * c + m + 1)
                dve.tensor_copy(g_hi[:, m, :], g[:, m % 4, :]).then_inc(g_high, 1)
                dve.wait_ge(g_high, MB * c + m + 1)
                dve.tensor_tensor(g_lo[:, m, :], g[:, m % 4, :], g_hi[:, m, :].bitcast(F32), ALU.subtract
                                  ).then_inc(g_split, 1)
                if m in (2, 5) and not first:
                    weigh(c - 1, m // 3)
                if end and not last:
                    dve.wait_ge(h_done, MB * c + m + 1)
                    split_w1(e + 1, m)
                if m == 5 and start:
                    dve.wait_ge(b2_loaded, 16 * (e + 1))
            if last:
                return
            dve.wait_ge(h_done, MB * (c + 1))
            if end:
                take_b1(e + 1)
            split_x(c + 1)

        def expert(e, first=False, last=False):
            chunk(NCH * e, e, start=True, first=first)
            if first or last:
                for j in range(1, NCH - 1):
                    chunk(NCH * e + j, e)
            else:
                with dve.Fori(1, NCH - 1) as j:
                    chunk(NCH * e + j, e)
            chunk(NCH * e + NCH - 1, e, end=True, last=last)

        for m in range(MB):
            split_w1(0, m)
        take_b1(0)
        split_x(0)
        expert(0, first=True)
        with dve.Fori(1, E - 1) as e:
            expert(e)
        expert(E - 1, last=True)
        weigh(NG - 1, 0)
        weigh(NG - 1, 1)

    @block.tensor
    def _(pe):
        def turn_x(c):
            pe.wait_ge(gathered, 64 * (c + 1))
            for f in range(FB):
                for i in range(CC):
                    ins = pe.transpose(ps_x[f][:, i * SR:(i + 1) * SR], xg[:, i, f * P:(f + 1) * P],
                                       ident[0:SR, 0:SR])
                ins.then_inc(x_turned, 1)

        def turn_y(c, half, first):
            if half == 0:
                pe.wait_ge(yT_ready, c + 1)
            if not (first and half == 0):
                pe.wait_ge(y_ready, 2 * c + half)
            for i in (0, 1):
                t = 2 * half + i
                for f in range(FB):
                    ins = pe.transpose(ps_r[0:SR, i * D + f * P:i * D + (f + 1) * P],
                                       yT[:, f, t * SR:(t + 1) * SR], ident[:])
            ins.then_inc(y_turned, 1)

        def product(dst, w_hi, w_lo, v_hi, v_lo, start, stop):
            pe.matmul(dst, w_hi, v_hi, start=start, stop=False)
            pe.matmul(dst, w_hi, v_lo, start=False, stop=False)
            return pe.matmul(dst, w_lo, v_hi, start=False, stop=stop)

        def body(c, first, last):
            pe.wait_ge(x_split, c + 1)
            for m in range(MB):
                if m >= 3:
                    pe.wait_ge(gelu_done, MB * c + m - 2)
                elif not first and m < 2:
                    pe.wait_ge(gelu_done, MB * c - 1 + m)
                cols = slice(m * P, (m + 1) * P)
                for f in range(FB):
                    ins = product(ps_h[m % 3][:, 0:N2], w1_hi[:, f, cols], w1_lo[:, f, cols],
                                  x_hi[:, f, :], x_lo[:, f, :], f == 0, f == FB - 1)
                ins.then_inc(h_done, 1)
                if not first and m in (2, 5):
                    turn_y(c - 1, m // 3, False)
            for k in range(MB):
                pe.wait_ge(g_split, MB * c + k + 1)
                for f in range(FB):
                    cols = slice(f * P, (f + 1) * P)
                    ins = product(ps_y[f][:, 0:N2], w2_hi[:, k, cols], w2_lo[:, k, cols],
                                  g_hi[:, k, :], g_lo[:, k, :], k == 0, k == MB - 1)
                if k == MB // 2 - 1 and not last:
                    turn_x(c + 1)
            ins.then_inc(y_done, 1)

        turn_x(0)
        body(0, True, False)
        with pe.Fori(1, NG - 1) as c:
            body(c, False, False)
        body(NG - 1, False, True)
        for half in (0, 1):
            turn_y(NG - 1, half, False)


def tokens_attention_experts(nc, dram):
    with ExitStack() as ctx:
        rows = nc.dram_tensor("rows", [TOK, D], F32).ap()
        sums = nc.dram_tensor("sums", [TOK + N2, D], F32).ap()
        tab_first = nc.dram_tensor("tab_first", [E * SL, 2], F32).ap()
        tab_second = nc.dram_tensor("tab_second", [E * SL, 2], F32).ap()
        dram = dict(dram, rows=rows, sums=sums, tab_first=tab_first, tab_second=tab_second,
                    out_rows=dram["out"].rearrange("b s n -> (b s) n"))
        keep = {"ident": ctx.enter_context(nc.sbuf_tensor("ident", [P, P], F32)),
                "taken": ctx.enter_context(nc.sbuf_tensor("taken", [P, E], F32)),
                "x_in": ctx.enter_context(nc.sbuf_tensor("x_in", [P, NT, CH], F32)),
                "w1_loaded": ctx.enter_context(nc.semaphore("w1_loaded")),
                "w2_loaded": ctx.enter_context(nc.semaphore("w2_loaded"))}
        with ExitStack() as one:
            stage_one(nc, one, dram, keep)
        with ExitStack() as two:
            stage_two(nc, two, dram, keep)


_INS = {'x': 'x', 'txt': 'txt', 'L0_tok_conv_w': 'conv_w', 'L0_tok_conv_b': 'conv_b', 'L0_tok_read': 'read',
        'L0_attn_Wq': 'Wq', 'L0_attn_bq': 'bq', 'L0_attn_Wk': 'Wk', 'L0_attn_bk': 'bk', 'L0_attn_Wv': 'Wv',
        'L0_attn_bv': 'bv', 'L0_attn_Wo': 'Wo', 'L0_attn_bo': 'bo', 'L0_attn_m': 'm', 'L0_ffn_Wg': 'Wg',
        'L0_ffn_W1': 'W1', 'L0_ffn_b1': 'b1', 'L0_ffn_W2': 'W2', 'L0_ffn_b2': 'b2'}


def kernel(**inputs):
    import numpy as _np
    import concourse.bacc as _bacc
    from concourse import mybir as _mybir
    from concourse.bass_utils import run_bass_kernel_spmd as _run

    nc = _bacc.Bacc("TRN2", target_bir_lowering=False, num_devices=1)
    arrays, dram = {}, {}
    for name, short in _INS.items():
        a = _np.ascontiguousarray(inputs[name])
        arrays[f"in_{name}_dram"] = a
        dram[short] = nc.dram_tensor(f"in_{name}_dram", a.shape, _mybir.dt.from_np(a.dtype), kind="ExternalInput").ap()
    dram["out"] = nc.dram_tensor("out_0_dram", (B, S, D), F32, kind="ExternalOutput").ap()
    tokens_attention_experts(nc, dram)
    r = _run(nc, [arrays], core_ids=[0])
    return r.results[0]["out_0_dram"]
```

```python
from contextlib import ExitStack

import concourse.bass as bass
from concourse import mybir

F32 = mybir.dt.float32
F32R = mybir.dt.float32r
BF16 = mybir.dt.bfloat16
I32 = mybir.dt.int32
U32 = mybir.dt.uint32
ALU = mybir.AluOpType
ACT = mybir.ActivationFunctionType
X = mybir.AxisListType.X

P = 128
B, TI, D, DV = 8, 1024, 256, 4
TX = 32
S = TI + TX
TOK = B * S
CH = D * DV
KC = 4
CBS = CH // P
FB = D // P
HEADS, HD = 16, 16
E, H = 8, 1024
CAP = int(round(2 * TOK * 1.05 / E))
NT = TI // P
CT = 4
CW = CT * P
UNITS = NT // 2 + 1

SR = 111
ST = 20
SL = SR * ST
CC = 4
NCH = ST // CC
N2 = CC * SR
MB = H // P
W_AT = ((0, FB, H), (FB * H, MB, D))
FAR = 1 << 20
EMPTYING = 2 + CC
RING = 4
LN_EPS = 1e-5


def in_register(eng, register, value):
    if isinstance(value, int):
        return value
    eng.reg_mov(register, value)
    return register


def stage_one(nc, ctx, dram, keep):
    x, txt, conv_w, conv_b, read, Wq, bq, Wk, bk, Wv, bv, Wo, bo, m, Wg, sums = (
        dram[n] for n in ("x", "txt", "conv_w", "conv_b", "read", "Wq", "bq", "Wk", "bk", "Wv", "bv",
                          "Wo", "bo", "m", "Wg", "sums"))
    rows, tab_first, tab_second = dram["rows"], dram["tab_first"], dram["tab_second"]
    ident, taken, x_in = keep["ident"], keep["taken"], keep["x_in"]
    W1, W2 = dram["W1"], dram["W2"]

    def sb(name, shape, dt=F32):
        return ctx.enter_context(nc.sbuf_tensor(name, shape, dt))

    def sem(name):
        return ctx.enter_context(nc.semaphore(name))

    ones_bf = sb("ones_bf", [P, P], BF16)
    before_bf = sb("before_bf", [P, P], BF16)
    head_of = sb("head_of", [HEADS, D])
    value_of = sb("value_of", [DV, P])
    feat_of = sb("feat_of", [P, 32])
    block_mask = sb("block_mask", [P, P])
    rank = sb("rank", [P, NT + 1, E])
    valid = sb("valid", [P, 2 * E * (NT + 1)])
    no_reset = sb("no_reset", [P, 2 * E, NT + 2])
    bad_row = sb("bad_row", [P, 2, NT + 1])
    token_id = sb("token_id", [P, NT + 1])
    empty_slots = sb("empty_slots", [P, E * ST, 2])
    zeros = sb("zeros", [P, D])
    wqk = sb("wqk", [P, FB, 2 * D])
    wv = sb("wv", [P, FB, D])
    wo = sb("wo", [P, FB, D])
    bqk_rows = sb("bqk_rows", [P, 2 * D])
    bo_rows = sb("bo_rows", [P, D])
    bv_rows = sb("bv_rows", [P, D])
    wg_in = sb("wg_in", [E, D])
    wgT = sb("wgT", [P, FB, 32])
    conv_in = sb("conv_in", [P, CBS, KC])
    conv_b_in = sb("conv_b_in", [CBS, P])
    read_in = sb("read_in", [DV, 1])
    m_in = sb("m_in", [HEADS, 1])
    read_col = sb("read_col", [P, 1])
    conv_col = sb("conv_col", [P, CBS, KC])
    conv_mat = sb("conv_mat", [P, CBS, KC, 32])
    conv_b_col = sb("conv_b_col", [P, CBS])
    h_bias = sb("h_bias", [P, FB])
    m_col = sb("m_col", [P, FB])
    head_scale = sb("head_scale", [P, FB])
    xT = [sb(f"xT{c}", [P, CBS, KC - 1 + CW]) for c in range(2)]
    hT = [sb(f"hT{c}", [P, FB, CW]) for c in range(2)]
    h = sb("h", [P, NT + 1, D])
    h_out = sb("h_out", [P, NT + 1, D])
    xln = sb("xln", [P, NT + 1, D])
    xlnT = sb("xlnT", [P, FB, (NT + 1) * P])
    qk = sb("qk", [P, RING, 2 * D])
    qk_sq = sb("qk_sq", [P, 2, 2 * D])
    qk_ss = sb("qk_ss", [P, RING, 2 * HEADS])
    qk_len = sb("qk_len", [P, RING, 2 * HEADS])
    qk_inv = sb("qk_inv", [P, RING, 2 * HEADS])
    q_n = sb("q_n", [P, NT + 1, D])
    k_n = sb("k_n", [P, NT + 1, D])
    k_sum = sb("k_sum", [P, D])
    qT = sb("qT", [P, FB, (NT + 1) * P])
    A = sb("A", [P, FB, D])
    kvT = sb("kvT", [P, FB, P])
    M = sb("M", [P, FB, D])
    xf = sb("xf", [P, NT + 1, D])
    xfT = sb("xfT", [P, FB, (NT + 1) * P])
    eps = sb("eps", [P, 1])
    stats = sb("stats", [P, 2, NT + 1, 6])
    mean_var = sb("mean_var", [P, 2, NT + 1, 2])
    std = sb("std", [P, 2, NT + 1])
    rstd = sb("rstd", [P, 2, NT + 1])
    shift = sb("shift", [P, 2, NT + 1])
    lT = sb("lT", [P, 2 * P + TX])
    lg = sb("lg", [P, NT + 1, E])
    top = sb("top", [P, NT + 1])
    ex = sb("ex", [P, NT + 1, E])
    den = sb("den", [P, NT + 1])
    gate = sb("gate", [P, NT + 1, E])
    best = sb("best", [P, 2, NT + 1])
    same = sb("same", [P, NT + 1, E])
    chosen_rank = sb("chosen_rank", [P, 2, NT + 1])
    hot = sb("hot", [P, 2, E, NT + 1])
    hot_bf = sb("hot_bf", [P, 2 * E * (NT + 1)], BF16)
    runs = sb("runs", [P, 2 * E, NT + 2])
    ahead = sb("ahead", [P, 2 * E, NT + 2])
    place = sb("place", [P, 2 * E, NT + 1])
    count = sb("count", [P, 2, NT + 1])
    slot = sb("slot", [P, 2, NT + 1])
    slot_i = sb("slot_i", [P, 2, NT + 1], I32)
    entry = sb("entry", [P, 2, NT + 1, 2])

    ps = [ctx.enter_context(nc.psum_tensor(f"ps{i}", [P, 512], F32)) for i in range(8)]
    ps_x = ps[0:2]
    ps_t = [ps[2], ps[5]]
    ps_c = ps[3]
    ps_conv = [[ps[3], ps[7]], [ps[3], ps[7]]]
    ps_a = ps[4]
    ps_w = ps[6:8]
    ps_qk = [ps[6], ps[7], ps[0], ps[1]]

    shapes_ready = sem("shapes_ready")
    const_ready = sem("const_ready")
    const_step = sem("const_step")
    small_in = sem("small_in")
    params_in = sem("params_in")
    setup_mm = sem("setup_mm")
    setup_v = sem("setup_v")
    setup_a = sem("setup_a")
    x_loaded = [sem(f"x_loaded{c}") for c in range(2)]
    x_first = sem("x_first")
    txt_loaded = sem("txt_loaded")
    x_turned = sem("x_turned")
    xT_ready = sem("xT_ready")
    halo_ready = sem("halo_ready")
    conv_done = sem("conv_done")
    hT_ready = sem("hT_ready")
    h_turned = sem("h_turned")
    h_ready = sem("h_ready")
    xln_ready = sem("xln_ready")
    xln_turned = sem("xln_turned")
    xlnT_ready = sem("xlnT_ready")
    qk_done = sem("qk_done")
    qk_taken = sem("qk_taken")
    qk_squared = sem("qk_squared")
    qk_summed = sem("qk_summed")
    qk_rooted = sem("qk_rooted")
    h_measured = sem("h_measured")
    h_std = sem("h_std")
    out_measured = sem("out_measured")
    out_std = sem("out_std")
    h_scale = sem("h_scale")
    out_scale = sem("out_scale")
    qk_normed = sem("qk_normed")
    k_summed = sem("k_summed")
    q_turned = sem("q_turned")
    qT_ready = sem("qT_ready")
    A_done = sem("A_done")
    A_ready = sem("A_ready")
    kv_done = sem("kv_done")
    kv_ready = sem("kv_ready")
    M_done = sem("M_done")
    M_ready = sem("M_ready")
    base_ready = sem("base_ready")
    out_done = sem("out_done")
    out_taken = sem("out_taken")
    xf_ready = sem("xf_ready")
    xf_turned = sem("xf_turned")
    xfT_ready = sem("xfT_ready")
    gates_done = sem("gates_done")
    gates_copied = sem("gates_copied")
    logits_done = sem("logits_done")
    logits_taken = sem("logits_taken")
    shifted = sem("shifted")
    exp_done = sem("exp_done")
    hot_ready = sem("hot_ready")
    counts_done = sem("counts_done")
    counts_taken = sem("counts_taken")
    slots_ready = sem("slots_ready")
    scattered = sem("scattered")
    out_stored = sem("out_stored")
    xf_stored = sem("xf_stored")
    v_step = sem("v_step")
    N_SMALL, N_PARAM = 5, 8

    def t_bank(dst, u):
        if dst is xfT:
            return ps_t[u % 2]
        if dst is xlnT:
            return ps_t[(u + 1) % 2]
        return ps_t[(0, 1, 1, 0, 1)[u]]

    def h_bank(u):
        return ps_t[(0, 1, 1, 0)[u]]

    block = ctx.enter_context(nc.Block())

    def loop(eng, body):
        body(0, True, False, 0)
        with eng.Fori(0, B - 1) as i:
            body(i + 1, True, True, i)
        body(B, False, True, B - 1)

    @block.sync
    def _(sp):
        normed_value, copied_value = sp.alloc_register("normed_value"), sp.alloc_register("copied_value")
        x4 = x.rearrange("b (c i p) d v -> (b c) p i (d v)", c=2, i=CT, p=P)

        def load_x(b, c, waits):
            if waits:
                sp.wait_ge(x_turned, 16 * (b - 1) + 8 * (c + 1))
            sp.dma_start(x_in[:, CT * c:CT * (c + 1), :],
                         x4[bass.ds(b * 2 + c, 1), :, :, :].rearrange("a p i n -> p (a i) n")
                         ).then_inc(x_loaded[c], 16)

        for dst, src in (
            (wg_in[:], Wg),
            (conv_in[:], conv_w.rearrange("(b p) k -> p b k", p=P)),
            (conv_b_in[:], conv_b.rearrange("(b p) -> b p", p=P)),
            (read_in[:], read.rearrange("(v a) -> v a", a=1)),
            (m_in[:], m.rearrange("(v a) -> v a", a=1)),
        ):
            sp.dma_start(dst, src).then_inc(small_in, 16)
        x0 = x4[0:1, :, :, :].rearrange("a p i n -> p (a i) n")
        sp.dma_start(x_in[:, 0:CT, 0:CH // 2], x0[:, :, 0:CH // 2]).then_inc(x_first, 16)
        sp.dma_start(x_in[:, 0:CT, CH // 2:], x0[:, :, CH // 2:]).then_inc(x_loaded[0], 16)
        load_x(0, 1, False)
        for dst, src in (
            (wqk[:, :, 0:D], Wq.rearrange("(b p) n -> p b n", p=P)),
            (wqk[:, :, D:2 * D], Wk.rearrange("(b p) n -> p b n", p=P)),
            (wv[:], Wv.rearrange("(b p) n -> p b n", p=P)),
            (wo[:], Wo.rearrange("(b p) n -> p b n", p=P)),
            (bqk_rows[:, 0:D], bq.rearrange("(a n) -> a n", a=1).to_broadcast([P, D])),
            (bqk_rows[:, D:2 * D], bk.rearrange("(a n) -> a n", a=1).to_broadcast([P, D])),
            (bo_rows[:], bo.rearrange("(a n) -> a n", a=1).to_broadcast([P, D])),
            (bv_rows[:], bv.rearrange("(a n) -> a n", a=1).to_broadcast([P, D])),
        ):
            sp.dma_start(dst, src).then_inc(params_in, 16)
        sp.wait_ge(params_in, 16 * N_PARAM)

        def load_txt(b, waits):
            if waits:
                normed = in_register(sp, normed_value, UNITS * b)
                copied = in_register(sp, copied_value, 3 * b)
                sp.wait_ge(params_in, 16 * N_PARAM)
                sp.wait_ge(xln_ready, normed)
                sp.wait_ge(base_ready, copied)
            sp.dma_start(h[0:TX, NT, :], txt[bass.ds(b, 1), :, :].rearrange("a t n -> (a t) n")
                         ).then_inc(txt_loaded, 16)


        def store(b, dst, src, ready, stored):
            for c in range(2):
                sp.wait_ge(ready, UNITS * b + 2 * (c + 1))
                sp.dma_start(dst[bass.ds(b * S + c * CW, CW), :].rearrange("(i p) n -> p i n", p=P),
                             src[:, CT * c:CT * (c + 1), :]).then_inc(stored, 16)
            sp.wait_ge(ready, UNITS * b + UNITS)
            sp.dma_start(dst[bass.ds(b * S + TI, TX), :], src[0:TX, NT, :]).then_inc(stored, 16)

        load_txt(0, False)
        for c in range(2):
            load_x(1, c, True)
        load_txt(1, True)
        with sp.Fori(0, B - 2) as i:
            for c in range(2):
                load_x(i + 2, c, True)
            store(i, sums, h_out, xf_ready, out_stored)
            store(i, rows, xf, xf_ready, xf_stored)
            load_txt(i + 2, True)
        for b in (B - 2, B - 1):
            store(b, sums, h_out, xf_ready, out_stored)
            store(b, rows, xf, xf_ready, xf_stored)
            if b == B - 2:
                sp.wait_ge(x_turned, 16 * B)
                for (at, n, w), src in zip(W_AT, (W1, W2)):
                    sp.dma_start(x_in[:].rearrange("p i n -> p (i n)")[:, at:at + n * w].rearrange("p (b n) -> p b n", b=n),
                                 src[0:1, :, :].rearrange("a (b p) n -> p (a b) n", p=P)
                                 ).then_inc(keep["w1_loaded" if src is W1 else "w2_loaded"], 16)
        sp.wait_ge(out_stored, 16 * 3 * B)
        sp.wait_ge(xf_stored, 16 * 3 * B + 16)

    @block.gpsimd
    def _(pool):
        pool_value = pool.alloc_register("pool_value")
        n = [0]

        def step(ins, wait=True):
            n[0] += 1
            ins.then_inc(const_step, 1)
            if wait:
                pool.wait_ge(const_step, n[0])

        def keep_where(t, pattern, base, mult, op, fill=0.0):
            step(pool.affine_select(out=t, in_=t, compare_op=op, fill=fill, base=base, pattern=pattern,
                                    channel_multiplier=mult))

        for t, v in ((ident, 0.0), (feat_of, 1.0), (head_of, 1.0)):
            step(pool.memset(t[:], v), wait=False)
        step(pool.memset(value_of[:], 1.0))
        v3 = value_of[:].rearrange("v (a b) -> v a b", b=DV)
        keep_where(v3, [[0, P // DV], [-1, DV]], 0, 1, ALU.is_equal)
        keep_where(ident[:], [[-1, P]], 0, 1, ALU.not_equal, 1.0)
        keep_where(head_of[:], [[1, D]], 0, -HD, ALU.is_ge)
        keep_where(head_of[:], [[-1, D]], HD - 1, HD, ALU.is_ge)
        keep_where(feat_of[:], [[-DV, 32]], 0, 1, ALU.is_ge)
        keep_where(feat_of[:], [[DV, 32]], DV - 1, -1, ALU.is_ge)
        pool.memset(eps[:], LN_EPS).then_inc(shapes_ready, 1)
        for t, v in ((ones_bf, 1.0), (before_bf, 1.0), (valid, 1.0), (no_reset, 1.0), (bad_row, 0.0), (empty_slots, 0.0),
                     (lg, 0.0), (hot, 0.0), (runs, 0.0), (taken, 0.0), (k_sum, 0.0),
                     (mean_var, 1.0), (zeros, 0.0)):
            step(pool.memset(t[:], v), wait=False)
        for e in range(E):
            step(pool.memset(rank[:, :, e:e + 1], float(E - e)), wait=False)
        step(pool.memset(xT[0][:, :, 0:KC - 1], 0.0))
        keep_where(before_bf[:], [[1, P]], -1, -1, ALU.is_ge)
        step(pool.memset(valid[:].rearrange("p (k i) -> p k i", i=NT + 1)[TX:2 * TX, :, NT], 0.0))
        step(pool.memset(valid[:].rearrange("p (k i) -> p k i", i=NT + 1)[2 * TX:P, :, NT], 0.0))
        step(pool.memset(no_reset[:, :, 0:1], 0.0))
        step(pool.memset(bad_row[:, 1, :], float(CAP - 1)))
        step(pool.memset(bad_row[TX:2 * TX, :, NT:NT + 1], float(FAR)))
        step(pool.memset(bad_row[2 * TX:P, :, NT:NT + 1], float(FAR)))
        step(pool.memset(empty_slots[:, :, 0:1], float(FAR)))
        pool.memset(xf[:, 0, 0:1], 0.0).then_inc(xf_stored, 16)
        pool.iota(token_id[:], [[P, NT + 1]], base=0, channel_multiplier=1,
                  allow_small_or_imprecise_dtypes=True).then_inc(const_ready, 1)
        for tab in (tab_first, tab_second):
            pool.dma_start(tab.rearrange("(p s) w -> p (s w)", p=SR),
                           empty_slots[0:SR, :, :].rearrange("p s w -> p (s w)")).then_inc(scattered, 16)

        for i in range(CC):
            pool.dma_start(sums[TOK + i * SR:TOK + (i + 1) * SR, :], zeros[0:SR, :]).then_inc(scattered, 16)

        def residual(b, waits):
            pool.wait_ge(h_ready, 4 * b + 4)
            pool.wait_ge(txt_loaded, 16 * b + 16)
            if waits:
                pool.wait_ge(xf_ready, UNITS * b)
                pool.wait_ge(out_stored, 16 * 3 * b)
            for t0, t1 in ((0, CT), (CT, NT)):
                bc = bo_rows[:].rearrange("p (a n) -> p a n", a=1).to_broadcast([P, t1 - t0, D])
                pool.tensor_tensor(h_out[:, t0:t1, :], h[:, t0:t1, :], bc, ALU.add).then_inc(base_ready, 1)
            pool.tensor_tensor(h_out[0:TX, NT, :], h[0:TX, NT, :], bo_rows[0:TX, :], ALU.add
                               ).then_inc(base_ready, 1)

        def scatter(b):
            ready = in_register(pool, pool_value, b + 1)
            pool.wait_ge(const_ready, 1)
            pool.wait_ge(slots_ready, ready)
            for t in range(NT + 1):
                for k, tab in enumerate((tab_first, tab_second)):
                    pool.indirect_dma_start(
                        tab, bass.IndirectOffsetOnAxis(slot_i[:, k, t:t + 1].bitcast(U32), 0),
                        entry[:, k, t, :], None, bounds_check=E * SL - 1, oob_is_err=False,
                    ).then_inc(scattered, 16)

        def sum_k(b, tiles):
            for i in tiles:
                r = P if i < NT else TX
                normed = (NT + 1) * b + i + 1
                if i == 0:
                    normed = in_register(pool, pool_value, normed)
                    pool.wait_ge(const_ready, 1)
                pool.wait_ge(qk_normed, normed)
                if i == 0:
                    pool.tensor_copy(k_sum[:], k_n[:, 0, :]).then_inc(k_summed, 1)
                else:
                    pool.wait_ge(k_summed, (NT + 1) * b + i)
                    pool.tensor_tensor(k_sum[0:r, :], k_sum[0:r, :], k_n[0:r, i, :], ALU.add
                                       ).then_inc(k_summed, 1)

        def body(b, lag):
            sum_k(b - 1, range(CT, NT + 1))
            if lag:
                scatter(b - 2)
            residual(b, True)
            pool.wait_ge(kv_done, b)
            sum_k(b, range(CT))

        pool.wait_ge(params_in, 16 * N_PARAM)
        residual(0, False)
        sum_k(0, range(CT))
        pool.wait_ge(scattered, 16 * EMPTYING)
        body(1, False)
        with pool.Fori(0, B - 2) as i:
            body(i + 2, True)
        sum_k(B - 1, range(CT, NT + 1))
        scatter(B - 2)
        scatter(B - 1)
        pool.wait_ge(scattered, 16 * (2 * (NT + 1) * B + EMPTYING))

    @block.scalar
    def _(act):
        act.wait_ge(setup_v, 3)
        act.activation(m_col[:], m_col[:], ACT.Exp, scale=-1.0).then_inc(setup_a, 1)
        act.wait_ge(setup_v, 5)
        act.activation(head_scale[:], head_scale[:], ACT.Exp, scale=-LOG_S).then_inc(setup_a, 1)

        def body(b, front, back, i):
            def root(n, c, measured, done, bb):
                tiles = slice(0, CT) if c == 0 else slice(CT, NT + 1)
                act.wait_ge(measured, 2 * bb + c + 1)
                act.activation(std[:, n, tiles], mean_var[:, n, tiles, 1], ACT.Sqrt, bias=eps[:, 0:1]).then_inc(done, 1)

            def center(n, c, src, dst, scaled, value, ready):
                act.wait_ge(scaled, value)
                for t in range(0, CT) if c == 0 else range(CT, NT + 1):
                    r = P if t < NT else TX
                    ins = act.activation(dst[0:r, t, :], src[0:r, t, :], ACT.Identity,
                                         bias=shift[0:r, n, t:t + 1], scale=rstd[0:r, n, t:t + 1])
                    if t % 2 == 1 or t == NT:
                        ins.then_inc(ready, 1)

            def x_blocks(*blocks):
                for g in blocks:
                    c = g // 8
                    act.wait_ge(x_turned, 16 * b + g + 1)
                    if g % 8 == 0 and back:
                        act.wait_ge(conv_done, 4 * (b - 1) + 2 * (c + 1))
                    act.copy(xT[c][:, g % 8, KC - 1:], ps_x[g % 2][:, 0:CW]).then_inc(xT_ready, 1)

            def conv_out(c, f):
                act.wait_ge(conv_done, 4 * b + 2 * c + f + 1)
                if f == 0 and back:
                    act.wait_ge(h_turned, 4 * (b - 1) + 2 * (c + 1))
                act.activation(hT[c][:, f, :], ps_conv[c][f][:, 0:CW], ACT.Identity, bias=h_bias[:, f:f + 1]
                               ).then_inc(hT_ready, 1)

            def from_turned(dst, u, turned, ready, bb, per=UNITS):
                if dst is xlnT and u == 0 and back:
                    act.wait_ge(qk_done, (NT + 1) * b)
                act.wait_ge(turned, per * bb + u + 1)
                if u < UNITS - 1:
                    act.copy(dst[:, :, 2 * u * P:(2 * u + 2) * P],
                             t_bank(dst, u)[:, 0:4 * P].rearrange("p (f t) -> p f t", f=FB)).then_inc(ready, 1)
                else:
                    act.copy(dst[:, :, NT * P:NT * P + TX],
                             t_bank(dst, u)[:, 0:2 * TX].rearrange("p (f t) -> p f t", f=FB)).then_inc(ready, 1)

            if front:
                x_blocks(0, 1, 2, 3)
            if back:
                lengths(b - 1, 7)
                square(b - 1, 8)
            if front:
                x_blocks(4, 5)
            if back:
                lengths(b - 1, 8)
            if front:
                x_blocks(6, 7)
                conv_out(0, 0)
            if back:
                for u in (2, 3, 4):
                    from_turned(qT, u, q_turned, qT_ready, b - 1)
                act.wait_ge(A_done, 2 * b)
                act.copy(A[:], ps_a[:].rearrange("p (f n) -> p f n", f=FB)).then_inc(A_ready, 1)
            if front:
                x_blocks(8, 9, 10, 11)
                conv_out(0, 1)
                for u in (0, 1):
                    h_rows(act, b, u, back)
            if back:
                act.wait_ge(M_done, b)
                act.copy(M[:], ps_c[:].rearrange("p (f n) -> p f n", f=FB)).then_inc(M_ready, 1)
            if front:
                root(0, 0, h_measured, h_std, b)
            if back:
                root(1, 0, out_measured, out_std, b - 1)
                center(1, 0, h_out, xf, out_scale, 2 * (b - 1) + 1, xf_ready)
            if front:
                x_blocks(12, 13, 14, 15)
            if back:
                root(1, 1, out_measured, out_std, b - 1)
            if front:
                conv_out(1, 0)
            if back:
                for u in (0, 1):
                    from_turned(xfT, u, xf_turned, xfT_ready, b - 1)
                center(1, 1, h_out, xf, out_scale, 2 * (b - 1) + 2, xf_ready)
            if front:
                conv_out(1, 1)
            if back:
                for u in (2, 3, 4):
                    from_turned(xfT, u, xf_turned, xfT_ready, b - 1)
            if front:
                from_turned(xlnT, 0, xln_turned, xlnT_ready, b)
            if back:
                act.wait_ge(gates_done, b)
                act.copy(lT[:, 0:2 * P], ps_c[:, 0:2 * P])
                act.copy(lT[0:TX, 2 * P:], ps_c[0:TX, 2 * P:2 * P + TX]).then_inc(gates_copied, 1)
            if front:
                from_turned(xlnT, 1, xln_turned, xlnT_ready, b)
                for u in (2, 3):
                    h_rows(act, b, u, back)
            if back:
                act.wait_ge(shifted, b)
                act.activation(ex[:], lg[:], ACT.Exp).then_inc(exp_done, 1)
            if front:
                root(0, 1, h_measured, h_std, b)
                square(b, 0)
                center(0, 1, h, xln, h_scale, b + 1, xln_ready)
                square(b, 1)
                lengths(b, 0)
                from_turned(xlnT, 2, xln_turned, xlnT_ready, b)
                square(b, 2)
                lengths(b, 1)
                from_turned(xlnT, 3, xln_turned, xlnT_ready, b)
                square(b, 3)
                lengths(b, 2)
                from_turned(xlnT, 4, xln_turned, xlnT_ready, b)
                for t in range(4, 8):
                    square(b, t)
                    lengths(b, t - 1)
                for u in (0, 1):
                    from_turned(qT, u, q_turned, qT_ready, b)

        def h_rows(act, b, u, back):
            act.wait_ge(h_turned, 4 * b + u + 1)
            if u == 0 and back:
                act.wait_ge(base_ready, 3 * b)
            act.copy(h[:, 2 * u:2 * u + 2, :], h_bank(u)[:].rearrange("p (t n) -> p t n", t=2)).then_inc(h_ready, 1)

        def square(b, t):
            r = P if t < NT else TX
            act.wait_ge(qk_taken, (NT + 1) * b + t + 1)
            act.activation(qk_sq[0:r, t % 2, :], qk[0:r, t % RING, :], ACT.Square).then_inc(qk_squared, 1)

        def lengths(b, t):
            r = P if t < NT else TX
            act.wait_ge(qk_summed, (NT + 1) * b + t + 1)
            act.activation(qk_len[0:r, t % RING, :], qk_ss[0:r, t % RING, :], ACT.Sqrt).then_inc(qk_rooted, 1)

        loop(act, body)

    @block.vector
    def _(dve):
        dve_value = dve.alloc_register("dve_value")
        dve.wait_ge(shapes_ready, 1)
        dve.wait_ge(small_in, 16 * N_SMALL)
        dve.wait_ge(setup_mm, 3)
        dve.tensor_copy(read_col[:], ps[6][:, 0:1]).then_inc(setup_v, 1)
        dve.tensor_copy(conv_b_col[:], ps[6][:, 8:8 + CBS]).then_inc(setup_v, 1)
        dve.tensor_copy(m_col[:], ps[6][:, 16:16 + FB]).then_inc(setup_v, 1)
        dve.wait_ge(setup_a, 1)
        dve.tensor_scalar(m_col[:], m_col[:], 1.0, None, ALU.add).then_inc(setup_v, 1)
        dve.wait_ge(setup_v, 4)
        dve.reciprocal(head_scale[:], m_col[:]).then_inc(setup_v, 1)
        dve.tensor_copy(block_mask[:], ps[6][:, 128:256]).then_inc(setup_v, 1)
        dve.memset(wgT[:], 0.0).then_inc(setup_v, 1)
        dve.tensor_scalar(conv_b_col[:], conv_b_col[:], read_col[:, 0:1], None, ALU.mult).then_inc(setup_v, 1)
        dve.tensor_scalar(conv_col[:], conv_in[:], read_col[:, 0:1], None, ALU.mult).then_inc(setup_v, 1)
        dve.wait_ge(setup_v, 9)
        dve.tensor_copy(wgT[:, :, 0:E], ps[6][:, 32:32 + FB * E].rearrange("p (f e) -> p f e", f=FB)
                        ).then_inc(setup_v, 1)
        dve.tensor_tensor(
            conv_mat[:].rearrange("p b k d -> p (b k) d"),
            feat_of[:].rearrange("p (a d) -> p a d", a=1).to_broadcast([P, CBS * KC, 32]),
            conv_col[:].rearrange("p b (k a) -> p (b k) a", a=1).to_broadcast([P, CBS * KC, 32]),
            ALU.mult).then_inc(setup_v, 1)
        dve.wait_ge(setup_mm, 4)
        dve.tensor_copy(h_bias[:], ps[7][:, 0:FB]).then_inc(setup_v, 1)
        dve.wait_ge(const_ready, 1)
        dve.memset(place[:], 0.0).then_inc(counts_taken, 1)
        dve.wait_ge(setup_a, 2)

        def body(b, front, back, it):
            steps = [0]

            def step(ins):
                steps[0] += 1
                ins.then_inc(v_step, 1)
                if not back:
                    return steps[0]
                return V_FRONT + V_BOTH * it + steps[0]

            def then(v):
                dve.wait_ge(v_step, v)

            def tiles_of(c):
                return range(0, CT) if c == 0 else range(CT, NT + 1)

            def measure(n, c, src, done):
                for t in tiles_of(c):
                    r = P if t < NT else TX
                    v = step(dve.bn_stats(stats[0:r, n, t, :], src[0:r, t, :]))
                v = in_register(dve, dve_value, v)
                dve.wait_ge(const_ready, 1)
                then(v)
                for t in tiles_of(c):
                    r = P if t < NT else TX
                    ins = dve.bn_aggr(mean_var[0:r, n, t, :], stats[0:r, n, t, :])
                ins.then_inc(done, 1)

            def center(n, c, bb, src, dst, std_done, ready):
                dve.wait_ge(std_done, 2 * bb + c + 1)
                tiles = tiles_of(c)
                cols = slice(tiles[0], tiles[-1] + 1)
                v = step(dve.reciprocal(rstd[:, n, cols], std[:, n, cols]))
                then(v)
                for t in tiles:
                    r = P if t < NT else TX
                    ins = dve.tensor_scalar(dst[0:r, t, :], src[0:r, t, :], mean_var[0:r, n, t, 0:1],
                                            rstd[0:r, n, t:t + 1], ALU.subtract, ALU.mult)
                    if t % 2 == 1 or t == NT:
                        ins.then_inc(ready, 1)

            def scale(n, c, bb, std_done, done):
                dve.wait_ge(std_done, 2 * bb + c + 1)
                cols = slice(tiles_of(c)[0], tiles_of(c)[-1] + 1)
                v = step(dve.reciprocal(rstd[:, n, cols], std[:, n, cols]))
                then(v)
                dve.scalar_tensor_tensor(out=shift[:, n, cols], in0=mean_var[:, n, cols, 0], scalar=-1.0,
                                         in1=rstd[:, n, cols], op0=ALU.mult, op1=ALU.mult).then_inc(done, 1)

            def measure_h(c):
                for u in ((0, 1) if c == 0 else (2, 3)):
                    dve.wait_ge(h_ready, 4 * b + u + 1)
                if c == 1:
                    dve.wait_ge(txt_loaded, 16 * b + 16)
                measure(0, c, h, h_measured)

            def center_h(c):
                if back:
                    dve.wait_ge(A_done, 2 * (b - 1) + c + 1)
                if c == 0:
                    center(0, c, b, h, xln, h_std, xln_ready)
                else:
                    scale(0, c, b, h_std, h_scale)

            def take_qk(t):
                r = P if t < NT else TX
                if t == 0 and not back:
                    dve.wait_ge(params_in, 16 * N_PARAM)
                dve.wait_ge(qk_done, (NT + 1) * b + t + 1)
                if t >= RING or back:
                    dve.wait_ge(qk_normed, (NT + 1) * b + t - RING + 1)
                bank = ps_qk[t % 4]
                dve.tensor_tensor(qk[0:r, t % RING, :], bank[0:r, :], bqk_rows[0:r, :], ALU.add).then_inc(qk_taken, 1)

            def sum_squares(t):
                r = P if t < NT else TX
                dve.wait_ge(qk_squared, (NT + 1) * b + t + 1)
                dve.tensor_reduce(qk_ss[0:r, t % RING, :], qk_sq[0:r, t % 2, :].rearrange("p (h d) -> p h d", d=HD),
                                  X, ALU.add).then_inc(qk_summed, 1)

            norm_step, choice_step = {}, [None]

            def floor_qk(t):
                r = P if t < NT else TX
                dve.wait_ge(qk_rooted, (NT + 1) * b + t + 1)
                norm_step[t] = step(dve.tensor_scalar(qk_inv[0:r, t % RING, :], qk_len[0:r, t % RING, :],
                                                      1e-12, None, ALU.max))

            def invert_qk(t):
                r = P if t < NT else TX
                then(norm_step[t])
                norm_step[t] = step(dve.reciprocal(qk_inv[0:r, t % RING, :], qk_inv[0:r, t % RING, :]))

            def norm_qk(t):
                r = P if t < NT else TX
                then(norm_step[t])
                if back and t in (0, CT):
                    dve.wait_ge(A_done, 2 * (b - 1) + (1 if t == 0 else 2))
                for lo, dst in ((0, q_n), (1, k_n)):
                    inv = qk_inv[0:r, t % RING, HEADS * lo:HEADS * lo + HEADS].rearrange("p (h a) -> p h a", a=1)
                    if lo == 1 and back:
                        dve.wait_ge(k_summed, (NT + 1) * (b - 1) + t + 1)
                    ins = dve.tensor_tensor(dst[0:r, t, :].rearrange("p (h d) -> p h d", d=HD),
                                            qk[0:r, t % RING, D * lo:D * lo + D].rearrange("p (h d) -> p h d", d=HD),
                                            inv.to_broadcast([r, HEADS, HD]), ALU.mult)
                ins.then_inc(qk_normed, 1)

            def out_rows(*pairs):
                bb = b - 1
                if pairs[0] == 0:
                    dve.wait_ge(base_ready, 3 * bb + 3)
                for u in pairs:
                    tiles = slice(2 * u, 2 * u + 2) if u < UNITS - 1 else slice(NT, NT + 1)
                    r, w = (P, 2 * D) if u < UNITS - 1 else (TX, D)
                    dve.wait_ge(out_done, UNITS * bb + u + 1)
                    dst = h_out[0:r, tiles, :].rearrange("p t n -> p (t n)")
                    dve.tensor_tensor(dst, ps_w[u % 2][0:r, 0:w], dst, ALU.add).then_inc(out_taken, 1)

            def measure_out(c):
                dve.wait_ge(out_taken, UNITS * (b - 1) + (2 if c == 0 else UNITS))
                measure(1, c, h_out, out_measured)

            def scale_out(c):
                if c == 0:
                    dve.wait_ge(xf_stored, 16 * 3 * (b - 1) + 16)
                scale(1, c, b - 1, out_std, out_scale)

            def kv_out():
                dve.wait_ge(kv_done, b)
                for f in range(FB):
                    ins = dve.scalar_tensor_tensor(out=kvT[:, f, :], in0=ps_w[0][:, f * P:(f + 1) * P],
                                                   scalar=head_scale[:, f:f + 1], in1=block_mask[:],
                                                   op0=ALU.mult, op1=ALU.mult)
                ins.then_inc(kv_ready, 1)

            W = NT + 1

            def wide(t):
                return t.rearrange("p (i a) -> p i a", a=1).to_broadcast([P, W, E])

            def take_logits():
                dve.wait_ge(logits_done, b)
                dve.tensor_copy(
                    lg[:, 0:NT, :].rearrange("p (u q) e -> p u q e", q=2),
                    ps_c[:, 0:2 * P].rearrange("p (q u z) -> p u q z", q=2, z=32)[:, :, :, 0:E])
                v = step(dve.tensor_copy(lg[0:TX, NT, :], ps_c[0:TX, 2 * P:2 * P + E]))
                then(v)
                v = step(dve.tensor_reduce(top[:], lg[:], X, ALU.max))
                then(v)
                dve.tensor_tensor(lg[:], lg[:], wide(top[:]), ALU.subtract).then_inc(shifted, 1)

            def link(ins):
                choice_step[0] = step(ins)

            def weight_sum():
                dve.wait_ge(exp_done, b)
                link(dve.tensor_reduce(den[:], ex[:], X, ALU.add))

            def weight_inverse():
                then(choice_step[0])
                link(dve.reciprocal(top[:], den[:]))

            def weights():
                then(choice_step[0])
                link(dve.tensor_tensor(gate[:], ex[:], wide(top[:]), ALU.mult))

            def best_weight(k):
                then(choice_step[0])
                link(dve.tensor_reduce(best[:, k, :], gate[:], X, ALU.max))

            def is_best(k):
                then(choice_step[0])
                link(dve.tensor_tensor(same[:], gate[:], wide(best[:, k, :]), ALU.is_equal))

            def rank_best():
                then(choice_step[0])
                link(dve.tensor_tensor(same[:], same[:], rank[:], ALU.mult))

            def top_rank(k):
                then(choice_step[0])
                link(dve.tensor_reduce(chosen_rank[:, k, :], same[:], X, ALU.max))

            def mark(k):
                then(choice_step[0])
                link(dve.tensor_tensor(hot[:, k, :, :].rearrange("p e i -> p i e"), same[:],
                                       wide(chosen_rank[:, k, :]), ALU.is_equal))

            def drop_best():
                then(choice_step[0])
                link(dve.scalar_tensor_tensor(out=gate[:], in0=hot[:, 0, :, :].rearrange("p e i -> p i e"),
                                              scalar=-4.0, in1=gate[:], op0=ALU.mult, op1=ALU.add))

            def marks_out():
                then(choice_step[0])
                dve.tensor_tensor(hot_bf[:], hot[:].rearrange("p k e i -> p (k e i)"), valid[:], ALU.mult
                                  ).then_inc(hot_ready, 1)

            def take_counts():
                n = 2 * E * W
                dve.wait_ge(counts_done, b)
                link(dve.tensor_copy(runs[:, :, 1:], ps_c[:, n:2 * n].rearrange("p (k i) -> p k i", i=W)))

            def scan_counts():
                then(choice_step[0])
                link(dve.tensor_tensor_scan(ahead[:].rearrange("p k i -> p (k i)"),
                                            no_reset[:].rearrange("p k i -> p (k i)"),
                                            runs[:].rearrange("p k i -> p (k i)"), 0.0, ALU.mult, ALU.add))

            def places():
                n = 2 * E * W
                then(choice_step[0])
                dve.tensor_tensor(place[:], ps_c[:, 0:n].rearrange("p (k i) -> p k i", i=W),
                                  ahead[:, :, 0:W], ALU.add).then_inc(counts_taken, 1)

            def slots():
                step(dve.tensor_copy(runs[:, :, 0:1], ahead[:, :, W:W + 1]))
                dve.wait_ge(counts_taken, b + 1)
                v = step(dve.tensor_tensor(place[:].rearrange("p k i -> p (k i)"), place[:].rearrange("p k i -> p (k i)"),
                                           hot_bf[:], ALU.mult))
                then(v)
                v = step(dve.tensor_reduce(count[:], place[:].rearrange("p (k e) i -> p k i e", k=2), X, ALU.add))
                then(v)
                v = step(dve.tensor_scalar(slot[:], count[:], float(CAP), float(FAR), ALU.is_ge, ALU.mult))
                then(v)
                v = step(dve.tensor_tensor(slot[:], slot[:], bad_row[:], ALU.add))
                v = step(dve.tensor_scalar(chosen_rank[:], chosen_rank[:], -float(SL), float(E * SL), ALU.mult, ALU.add))
                then(v)
                v = step(dve.tensor_tensor(slot[:], slot[:], chosen_rank[:], ALU.add))
                then(v)
                dve.wait_ge(scattered, 16 * (2 * W * (b - 1) + EMPTYING))
                v = step(dve.tensor_tensor(slot_i[:, 0, :], slot[:, 0, :], count[:, 0, :], ALU.add))
                v = step(dve.tensor_tensor(slot_i[:, 1, :], slot[:, 1, :], count[:, 1, :], ALU.subtract))
                for k in range(2):
                    step(dve.tensor_copy(entry[:, k, :, 0], token_id[:]))
                v = step(dve.tensor_copy(entry[:, :, :, 1], best[:]))
                then(v)
                dve.tensor_scalar(token_id[:], token_id[:], float(S), None, ALU.add).then_inc(slots_ready, 1)

            if front:
                dve.wait_ge(xT_ready, 16 * b + 8)
                if back:
                    dve.wait_ge(conv_done, 4 * b)
                dve.tensor_copy(xT[1][:, :, 0:KC - 1], xT[0][:, :, CW:CW + KC - 1]).then_inc(halo_ready, 1)
            if back:
                kv_out()
            if front:
                measure_h(0)
            if back:
                out_rows(0)
            if front:
                center_h(0)
            if back:
                out_rows(1)
                measure_out(0)
                out_rows(2)
                scale_out(0)
                out_rows(3, 4)
                measure_out(1)
                scale_out(1)
                take_logits()
            if front:
                measure_h(1)
                take_qk(0)
                center_h(1)
                take_qk(1)
                sum_squares(0)
            if back:
                weight_sum()
            if front:
                take_qk(2)
            if back:
                weight_inverse()
            if front:
                sum_squares(1)
            if back:
                weights()
            if front:
                floor_qk(0)
            if back:
                best_weight(0)
            if front:
                invert_qk(0)
            if back:
                is_best(0)
            if front:
                norm_qk(0)
            if back:
                rank_best()
            if front:
                take_qk(3)
            if back:
                top_rank(0)
            if front:
                sum_squares(2)
            if back:
                mark(0)
            if front:
                floor_qk(1)
            if back:
                drop_best()
            if front:
                invert_qk(1)
            if back:
                best_weight(1)
            if front:
                norm_qk(1)
            if back:
                is_best(1)
            if front:
                take_qk(4)
            if back:
                rank_best()
            if front:
                sum_squares(3)
            if back:
                top_rank(1)
            if front:
                floor_qk(2)
            if back:
                mark(1)
            if front:
                invert_qk(2)
            if back:
                marks_out()
            if front:
                take_qk(5)
                norm_qk(2)
                sum_squares(4)
                floor_qk(3)
                take_qk(6)
                invert_qk(3)
                sum_squares(5)
                norm_qk(3)
                floor_qk(4)
                take_qk(7)
                invert_qk(4)
                sum_squares(6)
                norm_qk(4)
                floor_qk(5)
            if back:
                take_counts()
            if front:
                invert_qk(5)
            if back:
                scan_counts()
            if front:
                norm_qk(5)
            if back:
                places()
            if front:
                sum_squares(7)
                floor_qk(6)
                invert_qk(6)
                floor_qk(7)
                norm_qk(6)
                invert_qk(7)
                take_qk(8)
                norm_qk(7)
            if back:
                slots()
            if front:
                sum_squares(8)
                floor_qk(8)
                invert_qk(8)
                norm_qk(8)
            want = V_BOTH if front and back else V_FRONT if front else V_BACK
            assert steps[0] == want, (front, back, steps[0])

        loop(dve, body)
        dve.wait_ge(slots_ready, B)
        dve.tensor_copy(taken[:], runs[:, 0:E, 0])

    @block.tensor
    def _(pe):
        pe_value, normed_value = pe.alloc_register("pe_value"), pe.alloc_register("pe_normed_value")
        def columns():
            pe.wait_ge(shapes_ready, 1)
            pe.wait_ge(small_in, 16 * N_SMALL)
            pe.matmul(ps[6][:, 0:1], value_of[:], read_in[:], start=True, stop=True)
            pe.transpose(ps[6][:, 8:8 + CBS], conv_b_in[:], ident[0:CBS, 0:CBS]).then_inc(setup_mm, 1)
            for f in range(FB):
                pe.matmul(ps[6][:, 16 + f:17 + f], head_of[:, f * P:(f + 1) * P], m_in[:], start=True, stop=True)
            pe.matmul(ps[6][:, 128:256], head_of[:, 0:P], head_of[:, 0:P], start=True, stop=True
                      ).then_inc(setup_mm, 1)
            for f in range(FB):
                ins = pe.transpose(ps[6][:, 32 + f * E:32 + (f + 1) * E], wg_in[:, f * P:(f + 1) * P],
                                   ident[0:E, 0:E])
            ins.then_inc(setup_mm, 1)

        def bias_column():
            pe.wait_ge(setup_v, 8)
            for cb in range(CBS):
                q = cb % 4
                ins = pe.matmul(ps[7][32 * q:32 * q + 32, cb // 4:cb // 4 + 1], feat_of[:], conv_b_col[:, cb:cb + 1],
                                start=True, stop=True, skip_group_check=True)
            ins.then_inc(setup_mm, 1)

        def body(b, front, back, it):
            W = NT + 1

            def turn_x(g):
                c = g // 8
                if g == 0 and not back:
                    pe.wait_ge(x_first, 16)
                elif g % 8 == 0 or (g == 4 and not back):
                    pe.wait_ge(x_loaded[c], 16 * b + 16)
                if g >= 2:
                    pe.wait_ge(xT_ready, 16 * b + g - 1)
                elif back:
                    pe.wait_ge(qk_taken, W * b + g - 2)
                for i in range(CT):
                    ins = pe.transpose(ps_x[g % 2][:, i * P:(i + 1) * P],
                                       x_in[:, CT * c + i, (g % 8) * P:(g % 8 + 1) * P], ident[:])
                ins.then_inc(x_turned, 1)

            def taps(c, f, between):
                pe.wait_ge(xT_ready, 16 * b + 8 * c + 4 * (f + 1))
                if (c, f) == (0, 0):
                    if back:
                        pe.wait_ge(counts_taken, b)
                elif (c, f) == (0, 1):
                    if back:
                        pe.wait_ge(qk_taken, W * b - 3)
                elif (c, f) == (1, 0):
                    pe.wait_ge(hT_ready, 4 * b + 1)
                    if back:
                        pe.wait_ge(M_ready, b)
                    pe.wait_ge(halo_ready, b + 1)
                else:
                    pe.wait_ge(hT_ready, 4 * b + 2)
                    if back:
                        pe.wait_ge(out_taken, UNITS * b - 1)
                for k in range(KC):
                    for q in range(4):
                        cb = 4 * f + q
                        ins = pe.matmul(ps_conv[c][f][32 * q:32 * q + 32, 0:CW], conv_mat[:, cb, k, :],
                                        xT[c][:, cb, k:k + CW], start=(k == 0), stop=(k == KC - 1),
                                        skip_group_check=True)
                    for g in between[k] if between else ():
                        turn_x(g)
                ins.then_inc(conv_done, 1)

            def turn_pair(src, dst, u, turned, feature_rows=False):
                bank = t_bank(dst, u)
                if u < UNITS - 1:
                    for f in range(FB):
                        for t in range(2):
                            ins = pe.transpose(bank[:, (2 * f + t) * P:(2 * f + t + 1) * P],
                                               src[:, 2 * u + t, f * P:(f + 1) * P], ident[:])
                else:
                    for f in range(FB):
                        ins = pe.transpose(bank[:, f * TX:(f + 1) * TX], src[0:TX, NT, f * P:(f + 1) * P],
                                           ident[0:TX, 0:TX])
                ins.then_inc(turned, 1)

            def turn_q(bb, u, free):
                for s, v in free:
                    pe.wait_ge(s, v)
                normed = W * bb + (2 * u + 2 if u < UNITS - 1 else W)
                if u == UNITS - 1:
                    normed = in_register(pe, pe_value, normed)
                    pe.wait_ge(const_ready, 1)
                pe.wait_ge(qk_normed, normed)
                turn_pair(q_n, qT, u, q_turned)

            def add_A(bb, tiles, first, last):
                for t in tiles:
                    r = P if t < NT else TX
                    for f in range(FB):
                        ins = pe.matmul(ps_a[:, f * D:(f + 1) * D], xln[0:r, t, f * P:(f + 1) * P], k_n[0:r, t, :],
                                        start=(first and t == 0 and f == 0), stop=bool(last) and t == NT,
                                        skip_group_check=True)
                if last is not None:
                    ins.then_inc(A_done, 1)

            def turn_h(u):
                pe.wait_ge(hT_ready, 4 * b + 2 * (u // 2) + 2)
                if back and u < 2:
                    pe.wait_ge(qT_ready, UNITS * (b - 1) + 4 + u)
                if u >= 2:
                    pe.wait_ge(xlnT_ready, UNITS * b + u - 1)
                c, bank = u // 2, h_bank(u)
                for t in range(2):
                    for f in range(FB):
                        col = (2 * (u % 2) + t) * P
                        ins = pe.transpose(bank[:, t * D + f * P:t * D + (f + 1) * P], hT[c][:, f, col:col + P], ident[:])
                ins.then_inc(h_turned, 1)

            def turn_xln(u):
                normed = UNITS * b + u + 1
                if u == UNITS - 1:
                    normed = in_register(pe, normed_value, normed)
                    copied = in_register(pe, pe_value, UNITS * b + 3)
                    pe.wait_ge(const_ready, 1)
                pe.wait_ge(xln_ready, normed)
                if u < 2:
                    if back:
                        pe.wait_ge(xfT_ready, UNITS * b - 1 + u)
                    else:
                        pe.wait_ge(h_ready, 4 * b + 2)
                elif u < 4:
                    pe.wait_ge(h_ready, 4 * b + u + 1)
                else:
                    pe.wait_ge(xlnT_ready, copied)
                turn_pair(xln, xlnT, u, xln_turned)

            def qk_tile(t):
                r = P if t < NT else TX
                if t == 0 and not back:
                    pe.wait_ge(params_in, 16 * N_PARAM)
                pe.wait_ge(xlnT_ready, UNITS * b + t // 2 + 1)
                if t == 0:
                    if back:
                        pe.wait_ge(out_taken, UNITS * b)
                elif t == 1:
                    pe.wait_ge(hT_ready, 4 * b + 4)
                elif t < 4:
                    pe.wait_ge(xT_ready, 16 * b + 13 + t)
                else:
                    pe.wait_ge(qk_taken, W * b + t - 3)
                for f in range(FB):
                    ins = pe.matmul(ps_qk[t % 4][0:r, :], xlnT[:, f, t * P:t * P + r], wqk[:, f, :],
                                    start=(f == 0), stop=(f == FB - 1))
                ins.then_inc(qk_done, 1)

            def kv():
                pe.wait_ge(A_ready, b)
                pe.wait_ge(k_summed, W * b)
                pe.wait_ge(qk_taken, W * b)
                for v in range(FB):
                    cols = slice(v * P, (v + 1) * P)
                    for f in range(FB):
                        pe.matmul(ps_w[0][:, cols], wv[:, f, cols], A[:, f, cols], start=(f == 0), stop=False)
                    ins = pe.matmul(ps_w[0][:, cols], bv_rows[:, cols], k_sum[:, cols], start=False, stop=True)
                ins.then_inc(kv_done, 1)

            def fold():
                pe.wait_ge(kv_ready, b)
                if front:
                    pe.wait_ge(hT_ready, 4 * b + 1)
                else:
                    pe.wait_ge(counts_taken, b)
                for f in range(FB):
                    ins = pe.matmul(ps_c[:, f * D:(f + 1) * D], kvT[:, f, :], wo[:, f, :], start=True, stop=True)
                ins.then_inc(M_done, 1)

            def attend(u):
                bb = b - 1
                if u == 0:
                    pe.wait_ge(M_ready, b)
                pe.wait_ge(qT_ready, UNITS * bb + u + 1)
                if u == 1:
                    if front:
                        pe.wait_ge(hT_ready, 4 * b + 2)
                elif u > 1:
                    pe.wait_ge(out_taken, UNITS * bb + u - 1)
                for t in ((2 * u, 2 * u + 1) if u < UNITS - 1 else (NT,)):
                    r = P if t < NT else TX
                    for f in range(FB):
                        ins = pe.matmul(ps_w[u % 2][0:r, (t % 2) * D:(t % 2 + 1) * D], qT[:, f, t * P:t * P + r],
                                        M[:, f, :], start=(f == 0), stop=(f == FB - 1))
                ins.then_inc(out_done, 1)

            def turn_xf(u):
                bb = b - 1
                normed, copied = UNITS * bb + u + 1, UNITS * bb + u - 1
                if u == UNITS - 1:
                    normed = in_register(pe, normed_value, normed)
                    copied = in_register(pe, pe_value, copied)
                    pe.wait_ge(const_ready, 1)
                pe.wait_ge(xf_ready, normed)
                if u < 2:
                    if front:
                        pe.wait_ge(h_ready, 4 * b + u + 1)
                    else:
                        pe.wait_ge(qT_ready, UNITS * bb + 4 + u)
                else:
                    pe.wait_ge(xfT_ready, copied)
                turn_pair(xf, xfT, u, xf_turned)

            def gates():
                bb = b - 1
                pe.wait_ge(xfT_ready, UNITS * bb + UNITS)
                if front:
                    pe.wait_ge(hT_ready, 4 * b + 3)
                for f in range(FB):
                    for u in range(UNITS - 1):
                        pe.matmul(ps_c[32 * u:32 * u + 32, 0:2 * P], wgT[:, f, :], xfT[:, f, 2 * u * P:(2 * u + 2) * P],
                                  start=(f == 0), stop=(f == FB - 1), skip_group_check=True)
                for f in range(FB):
                    ins = pe.matmul(ps_c[0:32, 2 * P:2 * P + TX], wgT[:, f, :], xfT[:, f, NT * P:NT * P + TX],
                                    start=(f == 0), stop=(f == FB - 1), skip_group_check=True)
                ins.then_inc(gates_done, 1)

            def turn_gates():
                pe.wait_ge(gates_copied, b)
                for q in range(2):
                    pe.transpose(ps_c[:, q * P:(q + 1) * P], lT[:, q * P:(q + 1) * P], ident[:])
                pe.transpose(ps_c[0:TX, 2 * P:2 * P + TX], lT[0:TX, 2 * P:], ident[0:TX, 0:TX]).then_inc(logits_done, 1)

            def counts():
                n = 2 * E * W
                pe.wait_ge(hot_ready, b)
                pe.matmul(ps_c[:, 0:n], before_bf[:], hot_bf[:], start=True, stop=True)
                pe.matmul(ps_c[:, n:2 * n], ones_bf[:], hot_bf[:], start=True, stop=True).then_inc(counts_done, 1)

            if front and not back:
                columns()
                turn_x(0)
                bias_column()
                turn_x(1)
                pe.wait_ge(const_ready, 1)
                pe.wait_ge(setup_v, 12)
                pe.wait_ge(setup_a, 2)
            if front:
                if back:
                    turn_x(0)
                    turn_x(1)
                turn_x(2)
            if back:
                turn_q(b - 1, 2, [(qT_ready, UNITS * (b - 1) + 2)])
            if front:
                turn_x(3)
            if back:
                add_A(b - 1, (4, 5), False, None)
            if front:
                taps(0, 0, ((4, 5), (6,), (7,), ()))
            if back:
                turn_q(b - 1, 3, [])
                add_A(b - 1, (6, 7), False, None)
                turn_q(b - 1, 4, [(qT_ready, UNITS * (b - 1) + 3)])
                add_A(b - 1, (NT,), False, True)
            if front:
                taps(0, 1, ((8, 9), (10,), (11,), ()))
            if back:
                kv()
            if front:
                turn_h(0)
                turn_h(1)
            if back:
                fold()
            if front:
                turn_x(12)
            if back:
                for u in range(UNITS):
                    attend(u)
            if front:
                taps(1, 0, ((13,), (14,), (15,), ()))
            if back:
                turn_xf(0)
                turn_xf(1)
            if front:
                taps(1, 1, ())
            if back:
                turn_xf(2)
                turn_xf(3)
                turn_xf(4)
            if front:
                turn_xln(0)
            if back:
                gates()
            if front:
                turn_xln(1)
                turn_h(2)
            if back:
                turn_gates()
            if front:
                turn_h(3)
                for t in range(CT):
                    qk_tile(t)
                turn_xln(2)
                turn_xln(3)
                qk_tile(4)
                turn_xln(4)
                qk_tile(5)
                qk_tile(6)
                qk_tile(7)
                turn_q(b, 0, [(xlnT_ready, UNITS * b + 4)])
                if back:
                    pe.wait_ge(A_ready, b)
                add_A(b, (0, 1), True, None)
                qk_tile(8)
                turn_q(b, 1, [(xlnT_ready, UNITS * b + UNITS)])
                add_A(b, (2, 3), False, False)
            if back:
                counts()

        loop(pe, body)


LOG_S = 6.962243464266207
V_FRONT, V_BOTH, V_BACK = 29, 70, 41


def stage_two(nc, ctx, dram, keep):
    W1, b1, W2, b2, sums = (dram[n] for n in ("W1", "b1", "W2", "b2", "sums"))
    rows, tab_first, tab_second = dram["rows"], dram["tab_first"], dram["tab_second"]
    ident, taken = keep["ident"], keep["taken"]

    def sb(name, shape, dt=F32):
        return ctx.enter_context(nc.sbuf_tensor(name, shape, dt))

    def sem(name):
        return ctx.enter_context(nc.semaphore(name))

    first = sb("first", [SR, E, ST, 2])
    second = sb("second", [SR, E, ST, 2])
    slot_no = sb("slot_no", [SR, ST])
    is_first = sb("is_first", [SR, E, ST], I32)
    near = sb("near", [SR, E * ST])
    spare = sb("spare", [SR, E * NCH, CC])
    plan = sb("plan", [SR, E * NCH, 3, CC], I32)
    take = sb("take", [SR, CC], I32)
    give = sb("give", [SR, 2, CC], I32)
    w1_in, w2_in = (keep["x_in"][:].rearrange("p i n -> p (i n)")[:, at:at + n * w].rearrange("p (b n) -> p b n", b=n)
                    for at, n, w in W_AT)
    w1_hi, w1_lo = (sb(f"w1_{n}", [P, FB, H], F32R) for n in ("hi", "lo"))
    w2_hi, w2_lo = (sb(f"w2_{n}", [P, MB, D], F32R) for n in ("hi", "lo"))
    b1_col, b1_next = sb("b1_col", [P, MB]), sb("b1_next", [P, MB])
    b2_col = sb("b2_col", [P, FB])
    xg = sb("xg", [SR, CC, D])
    x_hi, x_lo = (sb(f"x_{n}", [P, FB, N2], F32R) for n in ("hi", "lo"))
    g = sb("g", [P, 4, N2])
    g_hi, g_lo = (sb(f"g_{n}", [P, MB, N2], F32R) for n in ("hi", "lo"))
    yT = sb("yT", [P, FB, N2])
    y = sb("y", [SR, CC, D])
    y_last = sb("y_last", [SR, NCH, CC, D])

    ps = [ctx.enter_context(nc.psum_tensor(f"qs{i}", [P, 512], F32)) for i in range(8)]
    ps_h, ps_y, ps_x, ps_r = ps[0:3], ps[3:5], ps[5:7], ps[7]

    tables_in = sem("tables_in")
    t_step = sem("t_step")
    slots_no = sem("slots_no")
    plan_ready = sem("plan_ready")
    take_loaded = sem("take_loaded")
    give_loaded = sem("give_loaded")
    w1_loaded, w2_loaded = keep["w1_loaded"], keep["w2_loaded"]
    b1_loaded = sem("b1_loaded")
    b1_taken = sem("b1_taken")
    b2_loaded = sem("b2_loaded")
    w1_high = sem("w1_high")
    w2_high = sem("w2_high")
    w1_split = sem("w1_split")
    w2_split = sem("w2_split")
    gathered = sem("gathered")
    x_turned = sem("x_turned2")
    x_halves = sem("x_halves")
    x_split = sem("x_split")
    h_done = sem("h_done")
    gelu_done = sem("gelu_done")
    g_high = sem("g_high")
    g_split = sem("g_split")
    y_done = sem("y_done")
    yT_ready = sem("yT_ready")
    y_turned = sem("y_turned")
    y_ready = sem("y_ready")
    added = sem("added")
    based = [sem(f"based{j}") for j in range(NCH)]
    copied = sem("copied")
    placed = sem("placed")
    NG = E * NCH
    LAST = NG - NCH

    block = ctx.enter_context(nc.Block())

    @block.sync
    def _(sp):
        def load_w1(e):
            sp.wait_ge(w1_split, MB * e)
            sp.dma_start(w1_in, W1[bass.ds(e, 1), :, :].rearrange("a (b p) n -> p (a b) n", p=P)
                         ).then_inc(w1_loaded, 16)

        def load_w2(e):
            sp.wait_ge(w2_split, MB * e)
            sp.dma_start(w2_in, W2[bass.ds(e, 1), :, :].rearrange("a (b p) n -> p (a b) n", p=P)
                         ).then_inc(w2_loaded, 16)

        def load_b1(e):
            sp.dma_start(b1_next[:], b1[bass.ds(e, 1), :].rearrange("a (m p) -> p (a m)", p=P),
                         allow_slow_non_contiguous=True).then_inc(b1_loaded, 16)

        def load_b2(e):
            sp.dma_start(b2_col[:], b2[bass.ds(e, 1), :].rearrange("a (m p) -> p (a m)", p=P),
                         allow_slow_non_contiguous=True).then_inc(b2_loaded, 16)

        def load_take(c):
            sp.dma_start(take[:], plan[:, bass.ds(c, 1), 0, :].rearrange("p a i -> p (a i)")
                         ).then_inc(take_loaded, 16)

        def load_give(c, first):
            if not first:
                sp.wait_ge(added, 64 * c)
            sp.dma_start(give[:], plan[:, bass.ds(c, 1), 1:3, :].rearrange("p a k i -> p (a k) i")
                         ).then_inc(give_loaded, 16)

        def copy_sums(batches, done):
            for n, b in enumerate(batches):
                sp.wait_ge(h_done, done + 3 * n + 1)
                sp.dma_start(dram["out"][b, :, :], sums[b * S:(b + 1) * S, :]).then_inc(copied, 16)

        def expert(e, first=False, last=False):
            if not last:
                load_w1(e + 1)
                sp.wait_ge(b1_taken, e + 1)
                load_b1(e + 1)
            for j in range(NCH):
                c = NCH * e + j
                if not (last and j == NCH - 1):
                    sp.wait_ge(gathered, 64 * (c + 1))
                    load_take(c + 1)
                if j == 0:
                    if not first:
                        sp.wait_ge(yT_ready, c)
                    load_b2(e)
                if not last:
                    load_give(c, first and j == 0)
                elif j == 0:
                    sp.wait_ge(added, 64 * LAST)
                elif j == 2:
                    copy_sums((0, 1), MB * (LAST + 1))
                elif j == 3:
                    copy_sums((2, 3, 4), MB * (LAST + 2))
                    copy_sums((5, 6, 7), MB * (LAST + 3))
                if j == 1 and not last:
                    load_w2(e + 1)

        for tab, dst in ((tab_first, first), (tab_second, second)):
            sp.dma_start(dst[:].rearrange("p e i w -> p e (i w)"),
                         tab.rearrange("(e p i) w -> p e (i w)", e=E, p=SR)).then_inc(tables_in, 16)
        load_b1(0)
        sp.wait_ge(plan_ready, 1)
        load_take(0)
        expert(0, first=True)
        with sp.Fori(1, E - 1) as e:
            expert(e)
        expert(E - 1, last=True)
        sp.wait_ge(copied, 16 * B)

    @block.gpsimd
    def _(pool):
        loaded_value, weighed_value, before_value = (
            pool.alloc_register(f"{n}_value") for n in ("loaded", "weighed", "before"))
        pool.iota(slot_no[:], [[1, ST]], base=0, channel_multiplier=ST,
                  allow_small_or_imprecise_dtypes=True).then_inc(slots_no, 1)
        pool.iota(spare[:], [[0, E * NCH], [SR, CC]], base=TOK, channel_multiplier=1,
                  allow_small_or_imprecise_dtypes=True).then_inc(slots_no, 1)

        def gather(c):
            loaded = in_register(pool, loaded_value, 16 * (c + 1))
            pool.wait_ge(slots_no, 1)
            pool.wait_ge(take_loaded, loaded)
            for i in range(CC):
                pool.indirect_dma_start(xg[:, i, :], None, rows,
                                        bass.IndirectOffsetOnAxis(take[:, i:i + 1].bitcast(U32), 0)
                                        ).then_inc(gathered, 16)

        def add(c):
            loaded = in_register(pool, loaded_value, 16 * (c + 1))
            weighed = in_register(pool, weighed_value, 2 * (c + 1))
            before = in_register(pool, before_value, 64 * c)
            pool.wait_ge(slots_no, 1)
            pool.wait_ge(give_loaded, loaded)
            pool.wait_ge(y_ready, weighed)
            if not (isinstance(c, int) and c == 0):
                pool.wait_ge(added, before)
            for i in range(CC):
                pool.indirect_dma_start(sums, bass.IndirectOffsetOnAxis(give[:, 0, i:i + 1].bitcast(U32), 0),
                                        y[:, i, :], None, compute_op=ALU.add).then_inc(added, 16)

        def gather_sums(j):
            for i in range(CC):
                pool.indirect_dma_start(y_last[:, j, i, :], None, sums,
                                        bass.IndirectOffsetOnAxis(plan[:, LAST + j, 0, i:i + 1].bitcast(U32), 0)
                                        ).then_inc(based[j], 16)

        def place(j):
            pool.wait_ge(y_ready, 2 * (LAST + j + 1))
            for i in range(CC):
                pool.indirect_dma_start(dram["out_rows"],
                                        bass.IndirectOffsetOnAxis(plan[:, LAST + j, 1, i:i + 1].bitcast(U32), 0),
                                        y_last[:, j, i, :], None, bounds_check=TOK - 1, oob_is_err=False
                                        ).then_inc(placed, 16)

        def gather_next(c):
            pool.wait_ge(x_turned, 2 * (c + 1))
            gather(c + 1)

        gather(0)
        gather_next(0)
        gather_next(1)
        add(0)
        with pool.Fori(2, LAST + 1) as c:
            gather_next(c)
            add(c - 1)
        pool.wait_ge(added, 64 * LAST)
        gather_sums(0)
        for j in range(1, NCH):
            if j < NCH - 1:
                gather_next(LAST + j)
            gather_sums(j)
        pool.wait_ge(copied, 16 * B)
        for j in range(NCH):
            place(j)
        pool.wait_ge(placed, 64 * NCH)

    @block.scalar
    def _(act):
        def body(c, first):
            for m in range(MB):
                act.wait_ge(h_done, MB * c + m + 1)
                if not (first and m < 4):
                    act.wait_ge(g_split, MB * c + m - 3)
                act.activation(g[:, m % 4, :], ps_h[m % 3][:, 0:N2], ACT.Gelu, bias=b1_col[:, m:m + 1]
                               ).then_inc(gelu_done, 1)
            act.wait_ge(y_done, c + 1)
            if not first:
                act.wait_ge(y_turned, 2 * c)
            for f in range(FB):
                ins = act.activation(yT[:, f, :], ps_y[f][:, 0:N2], ACT.Identity, bias=b2_col[:, f:f + 1])
            ins.then_inc(yT_ready, 1)

        body(0, True)
        with act.Fori(1, NG) as c:
            body(c, False)

    @block.vector
    def _(dve):
        dve.wait_ge(slots_no, 2)
        dve.tensor_tensor(is_first[:],
                          slot_no[:].rearrange("p (a i) -> p a i", a=1).to_broadcast([SR, E, ST]),
                          taken[0:SR, :].rearrange("p (e a) -> p e a", a=1).to_broadcast([SR, E, ST]),
                          ALU.is_lt).then_inc(t_step, 1)
        dve.wait_ge(t_step, 1)
        dve.wait_ge(tables_in, 32)
        for w in range(2):
            dve.copy_predicated(second[:, :, :, w], is_first[:], first[:, :, :, w]).then_inc(t_step, 1)
        dve.wait_ge(t_step, 3)
        dve.tensor_scalar(near[:], second[:, :, :, 0].rearrange("p e i -> p (e i)"), float(TOK - 1), None, ALU.min
                          ).then_inc(t_step, 1)
        chunks = second[:].rearrange("p e (c q) w -> p (e c) q w", q=CC)
        dve.tensor_tensor(plan[:, :, 1, :], chunks[:, :, :, 0], spare[:], ALU.min).then_inc(t_step, 1)
        dve.tensor_copy(plan[:, :, 2, :].bitcast(F32), chunks[:, :, :, 1]).then_inc(t_step, 1)
        dve.wait_ge(t_step, 6)
        dve.tensor_copy(plan[:, :, 0, :], near[:].rearrange("p (c q) -> p c q", q=CC)).then_inc(plan_ready, 1)

        def split_w1(e, m):
            cols = slice(m * P, (m + 1) * P)
            if m == 0:
                dve.wait_ge(w1_loaded, 16 * (e + 1))
            dve.tensor_copy(w1_hi[:, :, cols], w1_in[:, :, cols]).then_inc(w1_high, 1)
            dve.wait_ge(w1_high, MB * e + m + 1)
            dve.tensor_tensor(w1_lo[:, :, cols], w1_in[:, :, cols], w1_hi[:, :, cols].bitcast(F32), ALU.subtract
                              ).then_inc(w1_split, 1)

        def split_w2(e, m):
            if m == 0:
                dve.wait_ge(w2_loaded, 16 * (e + 1))
            dve.tensor_copy(w2_hi[:, m, :], w2_in[:, m, :]).then_inc(w2_high, 1)
            dve.wait_ge(w2_high, MB * e + m + 1)
            dve.tensor_tensor(w2_lo[:, m, :], w2_in[:, m, :], w2_hi[:, m, :].bitcast(F32), ALU.subtract
                              ).then_inc(w2_split, 1)

        def take_b1(e):
            dve.wait_ge(b1_loaded, 16 * (e + 1))
            dve.tensor_copy(b1_col[:], b1_next[:]).then_inc(b1_taken, 1)

        def split_x(c):
            for f in range(FB):
                dve.wait_ge(x_turned, 2 * c + f + 1)
                dve.tensor_copy(x_hi[:, f, :], ps_x[f][:, 0:N2]).then_inc(x_halves, 1)
            dve.wait_ge(x_halves, 2 * c + 2)
            for f in range(FB):
                ins = dve.tensor_tensor(x_lo[:, f, :], ps_x[f][:, 0:N2], x_hi[:, f, :].bitcast(F32), ALU.subtract)
            ins.then_inc(x_split, 1)

        def weigh(c, half):
            last = isinstance(c, int) and c >= LAST
            dve.wait_ge(y_turned, 2 * c + half + 1)
            if last:
                dve.wait_ge(based[c - LAST], 64)
            elif half == 0:
                dve.wait_ge(give_loaded, 16 * (c + 1))
                if not (isinstance(c, int) and c == 0):
                    dve.wait_ge(added, 64 * c)
            for i in (0, 1):
                t = 2 * half + i
                rows_in = ps_r[0:SR, i * D:(i + 1) * D]
                if last:
                    dst = y_last[:, c - LAST, t, :]
                    ins = dve.scalar_tensor_tensor(out=dst, in0=rows_in, scalar=plan[:, c, 2, t:t + 1].bitcast(F32),
                                                   in1=dst, op0=ALU.mult, op1=ALU.add)
                else:
                    ins = dve.tensor_scalar(y[:, t, :], rows_in, give[:, 1, t:t + 1].bitcast(F32), None, ALU.mult)
            ins.then_inc(y_ready, 1)

        def chunk(c, e, start=False, end=False, first=False, last=False):
            if not first:
                dve.wait_ge(y_done, c)
            for m in range(MB):
                if start:
                    split_w2(e, m)
                dve.wait_ge(gelu_done, MB * c + m + 1)
                dve.tensor_copy(g_hi[:, m, :], g[:, m % 4, :]).then_inc(g_high, 1)
                dve.wait_ge(g_high, MB * c + m + 1)
                dve.tensor_tensor(g_lo[:, m, :], g[:, m % 4, :], g_hi[:, m, :].bitcast(F32), ALU.subtract
                                  ).then_inc(g_split, 1)
                if m in (2, 5) and not first:
                    weigh(c - 1, m // 3)
                if end and not last:
                    dve.wait_ge(h_done, MB * c + m + 1)
                    split_w1(e + 1, m)
                if m == 5 and start:
                    dve.wait_ge(b2_loaded, 16 * (e + 1))
            if last:
                return
            dve.wait_ge(h_done, MB * (c + 1))
            if end:
                take_b1(e + 1)
            split_x(c + 1)

        def expert(e, first=False, last=False):
            chunk(NCH * e, e, start=True, first=first)
            if first or last:
                for j in range(1, NCH - 1):
                    chunk(NCH * e + j, e)
            else:
                with dve.Fori(1, NCH - 1) as j:
                    chunk(NCH * e + j, e)
            chunk(NCH * e + NCH - 1, e, end=True, last=last)

        for m in range(MB):
            split_w1(0, m)
        take_b1(0)
        split_x(0)
        expert(0, first=True)
        with dve.Fori(1, E - 1) as e:
            expert(e)
        expert(E - 1, last=True)
        weigh(NG - 1, 0)
        weigh(NG - 1, 1)

    @block.tensor
    def _(pe):
        def turn_x(c):
            pe.wait_ge(gathered, 64 * (c + 1))
            for f in range(FB):
                for i in range(CC):
                    ins = pe.transpose(ps_x[f][:, i * SR:(i + 1) * SR], xg[:, i, f * P:(f + 1) * P],
                                       ident[0:SR, 0:SR])
                ins.then_inc(x_turned, 1)

        def turn_y(c, half, first):
            if half == 0:
                pe.wait_ge(yT_ready, c + 1)
            if not (first and half == 0):
                pe.wait_ge(y_ready, 2 * c + half)
            for i in (0, 1):
                t = 2 * half + i
                for f in range(FB):
                    ins = pe.transpose(ps_r[0:SR, i * D + f * P:i * D + (f + 1) * P],
                                       yT[:, f, t * SR:(t + 1) * SR], ident[:])
            ins.then_inc(y_turned, 1)

        def product(dst, w_hi, w_lo, v_hi, v_lo, start, stop):
            pe.matmul(dst, w_hi, v_hi, start=start, stop=False)
            pe.matmul(dst, w_hi, v_lo, start=False, stop=False)
            return pe.matmul(dst, w_lo, v_hi, start=False, stop=stop)

        def body(c, first, last):
            pe.wait_ge(x_split, c + 1)
            for m in range(MB):
                if m >= 3:
                    pe.wait_ge(gelu_done, MB * c + m - 2)
                elif not first and m < 2:
                    pe.wait_ge(gelu_done, MB * c - 1 + m)
                cols = slice(m * P, (m + 1) * P)
                for f in range(FB):
                    ins = product(ps_h[m % 3][:, 0:N2], w1_hi[:, f, cols], w1_lo[:, f, cols],
                                  x_hi[:, f, :], x_lo[:, f, :], f == 0, f == FB - 1)
                ins.then_inc(h_done, 1)
                if not first and m in (2, 5):
                    turn_y(c - 1, m // 3, False)
            for k in range(MB):
                pe.wait_ge(g_split, MB * c + k + 1)
                for f in range(FB):
                    cols = slice(f * P, (f + 1) * P)
                    ins = product(ps_y[f][:, 0:N2], w2_hi[:, k, cols], w2_lo[:, k, cols],
                                  g_hi[:, k, :], g_lo[:, k, :], k == 0, k == MB - 1)
                if k == MB // 2 - 1 and not last:
                    turn_x(c + 1)
            ins.then_inc(y_done, 1)

        turn_x(0)
        body(0, True, False)
        with pe.Fori(1, NG - 1) as c:
            body(c, False, False)
        body(NG - 1, False, True)
        for half in (0, 1):
            turn_y(NG - 1, half, False)


def tokens_attention_experts(nc, dram):
    with ExitStack() as ctx:
        rows = nc.dram_tensor("rows", [TOK, D], F32).ap()
        sums = nc.dram_tensor("sums", [TOK + N2, D], F32).ap()
        tab_first = nc.dram_tensor("tab_first", [E * SL, 2], F32).ap()
        tab_second = nc.dram_tensor("tab_second", [E * SL, 2], F32).ap()
        dram = dict(dram, rows=rows, sums=sums, tab_first=tab_first, tab_second=tab_second,
                    out_rows=dram["out"].rearrange("b s n -> (b s) n"))
        keep = {"ident": ctx.enter_context(nc.sbuf_tensor("ident", [P, P], F32)),
                "taken": ctx.enter_context(nc.sbuf_tensor("taken", [P, E], F32)),
                "x_in": ctx.enter_context(nc.sbuf_tensor("x_in", [P, NT, CH], F32)),
                "w1_loaded": ctx.enter_context(nc.semaphore("w1_loaded")),
                "w2_loaded": ctx.enter_context(nc.semaphore("w2_loaded"))}
        with ExitStack() as one:
            stage_one(nc, one, dram, keep)
        with ExitStack() as two:
            stage_two(nc, two, dram, keep)


_INS = {'x': 'x', 'txt': 'txt', 'L0_tok_conv_w': 'conv_w', 'L0_tok_conv_b': 'conv_b', 'L0_tok_read': 'read',
        'L0_attn_Wq': 'Wq', 'L0_attn_bq': 'bq', 'L0_attn_Wk': 'Wk', 'L0_attn_bk': 'bk', 'L0_attn_Wv': 'Wv',
        'L0_attn_bv': 'bv', 'L0_attn_Wo': 'Wo', 'L0_attn_bo': 'bo', 'L0_attn_m': 'm', 'L0_ffn_Wg': 'Wg',
        'L0_ffn_W1': 'W1', 'L0_ffn_b1': 'b1', 'L0_ffn_W2': 'W2', 'L0_ffn_b2': 'b2'}


def kernel(**inputs):
    import numpy as _np
    import concourse.bacc as _bacc
    from concourse import mybir as _mybir
    from concourse.bass_utils import run_bass_kernel_spmd as _run

    nc = _bacc.Bacc("TRN2", target_bir_lowering=False, num_devices=1)
    arrays, dram = {}, {}
    for name, short in _INS.items():
        a = _np.ascontiguousarray(inputs[name])
        arrays[f"in_{name}_dram"] = a
        dram[short] = nc.dram_tensor(f"in_{name}_dram", a.shape, _mybir.dt.from_np(a.dtype), kind="ExternalInput").ap()
    dram["out"] = nc.dram_tensor("out_0_dram", (B, S, D), F32, kind="ExternalOutput").ap()
    tokens_attention_experts(nc, dram)
    r = _run(nc, [arrays], core_ids=[0])
    return r.results[0]["out_0_dram"]
```
